# Optimizing a Trainium2 kernel written in Bass

```python
import numpy as np
import jax
import jax.numpy as jnp

def _softmax(x, axis=-1):
    return jax.nn.softmax(x, axis=axis)

def _gelu(x):
    return jax.nn.gelu(x, approximate=True)

def _silu(x):
    return jax.nn.silu(x)

def _sigmoid(x):
    return jax.nn.sigmoid(x)

def _layernorm(x, axis=-1, eps=1e-05):
    m = jnp.mean(x, axis=axis, keepdims=True)
    v = jnp.var(x, axis=axis, keepdims=True)
    return (x - m) / jnp.sqrt(v + eps)

def _scatter_add(tgt, idx, src, axis=0):
    return tgt.at[idx].add(src)

def _segment_sum(src, seg, n):
    return jax.ops.segment_sum(src, seg, n)
kernel_name = 'mk_hybrid_d1_jaxref_r8_34f014'

def setup_inputs(seed: int=0):
    np.random.seed(seed)
    _w = jnp.asarray

    def _L0_attn_a_setup():
        import jax, jax.numpy as jnp
        import numpy as np
        D_MODEL = 128
        N_HEADS = 16
        HEAD_DIM = D_MODEL // N_HEADS
        ROPE_BASE = 10000.0

        def _rope(q, k):
            S, Dh = (q.shape[1], q.shape[-1])
            inv_freq = 1.0 / ROPE_BASE ** (jnp.arange(0, Dh, 2, dtype=jnp.float32) / Dh)
            t = jnp.arange(S, dtype=jnp.float32)
            freqs = jnp.outer(t, inv_freq)
            emb = jnp.concatenate([freqs, freqs], axis=-1)
            cos = jnp.cos(emb)[None, :, None, :]
            sin = jnp.sin(emb)[None, :, None, :]

            def rotate_half(v):
                v1, v2 = (v[..., :Dh // 2], v[..., Dh // 2:])
                return jnp.concatenate([-v2, v1], axis=-1)
            return (q * cos + rotate_half(q) * sin, k * cos + rotate_half(k) * sin)
        key = jax.random.key(seed)
        ks = jax.random.split(key, 5)
        B, S = (1, 512)
        scale = 1.0 / np.sqrt(D_MODEL)
        x = jax.random.normal(ks[0], (B, S, D_MODEL), dtype=jnp.float32)
        Wq = jax.random.normal(ks[1], (D_MODEL, D_MODEL), dtype=jnp.float32) * scale
        Wk = jax.random.normal(ks[2], (D_MODEL, D_MODEL), dtype=jnp.float32) * scale
        Wv = jax.random.normal(ks[3], (D_MODEL, D_MODEL), dtype=jnp.float32) * scale
        Wo = jax.random.normal(ks[4], (D_MODEL, D_MODEL), dtype=jnp.float32) * scale
        return {'x': x, 'Wq': Wq, 'Wk': Wk, 'Wv': Wv, 'Wo': Wo}
    _L0_attn_a_in = _L0_attn_a_setup()

    def _L0_attn_b_setup():
        import jax, jax.numpy as jnp
        import numpy as np
        D_MODEL = 128
        D_QK = 128
        NUM_HEADS = 16
        HEAD_DIM = D_QK // NUM_HEADS
        V_DIM = D_MODEL // NUM_HEADS
        B, S = (2, 256)
        key = jax.random.key(seed)
        ks = jax.random.split(key, 9)
        sc = 0.02
        return {'x': jax.random.normal(ks[0], (B, S, D_MODEL), dtype=jnp.float32), 'Wqk': jax.random.normal(ks[1], (D_MODEL, 2 * D_QK), dtype=jnp.float32) * sc, 'bqk': jax.random.normal(ks[2], (2 * D_QK,), dtype=jnp.float32) * sc, 'Wv': jax.random.normal(ks[3], (D_MODEL, D_MODEL), dtype=jnp.float32) * sc, 'bv': jax.random.normal(ks[4], (D_MODEL,), dtype=jnp.float32) * sc, 'Wn': jax.random.normal(ks[5], (D_MODEL, NUM_HEADS), dtype=jnp.float32) * sc, 'bn': jax.random.normal(ks[6], (NUM_HEADS,), dtype=jnp.float32) * sc, 'Wo': jax.random.normal(ks[7], (D_MODEL, D_MODEL), dtype=jnp.float32) * sc, 'bo': jax.random.normal(ks[8], (D_MODEL,), dtype=jnp.float32) * sc}
    _L0_attn_b_in = _L0_attn_b_setup()

    def _L0_ffn_setup():
        import jax, jax.numpy as jnp
        import numpy as np
        D = 128
        H = 512
        E = 64
        K = 3
        B, S = (2, 256)
        C = 64
        key = jax.random.key(seed)
        ks = jax.random.split(key, 6)
        s = 0.02
        return {'x': jax.random.normal(ks[0], (B, S, D), jnp.float32), 'gate_w': jax.random.normal(ks[1], (D, E), jnp.float32) * s, 'gate_b': jnp.zeros((E,), jnp.float32), 'w1': jax.random.normal(ks[2], (E, D, H), jnp.float32) * s, 'b1': jnp.zeros((E, H), jnp.float32), 'w2': jax.random.normal(ks[3], (E, H, D), jnp.float32) * s, 'b2': jnp.zeros((E, D), jnp.float32)}
    _L0_ffn_in = _L0_ffn_setup()
    _d = {'L0_attn_a_x': _L0_attn_a_in['x'], 'L0_attn_a_Wq': _L0_attn_a_in['Wq'], 'L0_attn_a_Wk': _L0_attn_a_in['Wk'], 'L0_attn_a_Wv': _L0_attn_a_in['Wv'], 'L0_attn_a_Wo': _L0_attn_a_in['Wo'], 'L0_attn_b_Wqk': _L0_attn_b_in['Wqk'], 'L0_attn_b_bqk': _L0_attn_b_in['bqk'], 'L0_attn_b_Wv': _L0_attn_b_in['Wv'], 'L0_attn_b_bv': _L0_attn_b_in['bv'], 'L0_attn_b_Wn': _L0_attn_b_in['Wn'], 'L0_attn_b_bn': _L0_attn_b_in['bn'], 'L0_attn_b_Wo': _L0_attn_b_in['Wo'], 'L0_attn_b_bo': _L0_attn_b_in['bo'], 'L0_ffn_gate_w': _L0_ffn_in['gate_w'], 'L0_ffn_gate_b': _L0_ffn_in['gate_b'], 'L0_ffn_w1': _L0_ffn_in['w1'], 'L0_ffn_b1': _L0_ffn_in['b1'], 'L0_ffn_w2': _L0_ffn_in['w2'], 'L0_ffn_b2': _L0_ffn_in['b2']}
    _x0 = _d['L0_attn_a_x']
    _d['L0_attn_a_x'] = jax.random.normal(jax.random.fold_in(jax.random.key(seed), 1), (8, 512, 128), dtype=_x0.dtype)
    del _x0
    return _d

def reference(L0_attn_a_x, L0_attn_a_Wq, L0_attn_a_Wk, L0_attn_a_Wv, L0_attn_a_Wo, L0_attn_b_Wqk, L0_attn_b_bqk, L0_attn_b_Wv, L0_attn_b_bv, L0_attn_b_Wn, L0_attn_b_bn, L0_attn_b_Wo, L0_attn_b_bo, L0_ffn_gate_w, L0_ffn_gate_b, L0_ffn_w1, L0_ffn_b1, L0_ffn_w2, L0_ffn_b2):

    def _L0_attn_a_ref(x, Wq, Wk, Wv, Wo):
        import jax, jax.numpy as jnp
        import numpy as np
        D_MODEL = 128
        N_HEADS = 16
        HEAD_DIM = D_MODEL // N_HEADS
        ROPE_BASE = 10000.0

        def _rope(q, k):
            S, Dh = (q.shape[1], q.shape[-1])
            inv_freq = 1.0 / ROPE_BASE ** (jnp.arange(0, Dh, 2, dtype=jnp.float32) / Dh)
            t = jnp.arange(S, dtype=jnp.float32)
            freqs = jnp.outer(t, inv_freq)
            emb = jnp.concatenate([freqs, freqs], axis=-1)
            cos = jnp.cos(emb)[None, :, None, :]
            sin = jnp.sin(emb)[None, :, None, :]

            def rotate_half(v):
                v1, v2 = (v[..., :Dh // 2], v[..., Dh // 2:])
                return jnp.concatenate([-v2, v1], axis=-1)
            return (q * cos + rotate_half(q) * sin, k * cos + rotate_half(k) * sin)
        B, S, _ = x.shape
        H, Dh = (N_HEADS, HEAD_DIM)
        q = (x @ Wq.T).reshape(B, S, H, Dh)
        k = (x @ Wk.T).reshape(B, S, H, Dh)
        v = (x @ Wv.T).reshape(B, S, H, Dh)
        q, k = _rope(q, k)
        scale = 1.0 / np.sqrt(Dh)
        scores = jnp.einsum('bqhd,bkhd->bhqk', q, k) * scale
        causal = jnp.triu(jnp.ones((S, S), dtype=bool), k=1)
        scores = jnp.where(causal, -jnp.inf, scores)
        attn = jax.nn.softmax(scores, axis=-1)
        out = jnp.einsum('bhqk,bkhd->bqhd', attn, v).reshape(B, S, H * Dh)
        return out @ Wo.T

    def _L0_attn_b_ref(x, Wqk, bqk, Wv, bv, Wn, bn, Wo, bo):
        import jax, jax.numpy as jnp
        import numpy as np
        D_MODEL = 128
        D_QK = 128
        NUM_HEADS = 16
        HEAD_DIM = D_QK // NUM_HEADS
        V_DIM = D_MODEL // NUM_HEADS
        B, S = (2, 256)
        b, s, _ = x.shape
        qk = x @ Wqk + bqk
        v = x @ Wv + bv
        n = x @ Wn + bn
        qk = qk.reshape(b, s, 2, NUM_HEADS, HEAD_DIM)
        q, k = (qk[:, :, 0], qk[:, :, 1])
        v = v.reshape(b, s, NUM_HEADS, V_DIM)
        scores = jnp.einsum('bthd,bshd->bhts', q, k)
        mask = jnp.tril(jnp.ones((s, s), dtype=scores.dtype))
        n_exp = jnp.exp(jnp.transpose(n, (0, 2, 1)))
        attn = scores * mask / n_exp[:, :, :, None]
        ctx = jnp.einsum('bhts,bshd->bthd', attn, v)
        ctx = ctx.reshape(b, s, D_MODEL)
        return ctx @ Wo + bo

    def _L0_ffn_ref(x, gate_w, gate_b, w1, b1, w2, b2):
        import jax, jax.numpy as jnp
        import numpy as np
        D = 128
        H = 512
        E = 64
        K = 3
        B, S = (2, 256)
        C = 64
        xf = x.reshape(-1, D)
        T = xf.shape[0]
        logits = xf @ gate_w + gate_b
        top_l, top_i = jax.lax.top_k(logits, K)
        gates = jax.nn.softmax(top_l, axis=-1)
        fe = top_i.reshape(-1)
        fg = gates.reshape(-1)
        tok = jnp.repeat(jnp.arange(T), K)
        oh = jax.nn.one_hot(fe, E, dtype=jnp.int32)
        pos = (jnp.cumsum(oh, axis=0) * oh).sum(-1) - 1
        valid = pos < C
        buf = jnp.zeros((E, C, D), x.dtype).at[fe, pos].set(xf[tok], mode='drop')
        h = jax.nn.gelu(jnp.einsum('ecd,edh->ech', buf, w1) + b1[:, None, :], approximate=False)
        y = jnp.einsum('ech,ehd->ecd', h, w2) + b2[:, None, :]
        rows = y[fe, jnp.minimum(pos, C - 1)] * (fg * valid.astype(x.dtype))[:, None]
        out = jnp.zeros_like(xf).at[tok].add(rows)
        return out.reshape(x.shape)
    x = L0_attn_a_x
    x = x + _L0_attn_a_ref(_layernorm(x, axis=-1), L0_attn_a_Wq, L0_attn_a_Wk, L0_attn_a_Wv, L0_attn_a_Wo)
    x = x + _L0_ffn_ref(_layernorm(x, axis=-1), L0_ffn_gate_w, L0_ffn_gate_b, L0_ffn_w1, L0_ffn_b1, L0_ffn_w2, L0_ffn_b2)
    x = x + _L0_attn_b_ref(_layernorm(x, axis=-1), L0_attn_b_Wqk, L0_attn_b_bqk, L0_attn_b_Wv, L0_attn_b_bv, L0_attn_b_Wn, L0_attn_b_bn, L0_attn_b_Wo, L0_attn_b_bo)
    x = x + _L0_ffn_ref(_layernorm(x, axis=-1), L0_ffn_gate_w, L0_ffn_gate_b, L0_ffn_w1, L0_ffn_b1, L0_ffn_w2, L0_ffn_b2)
    return x

_drawn_inputs = setup_inputs


def setup_inputs(seed=0):
    import zlib

    import numpy as np

    out = dict(_drawn_inputs(seed))
    spreads = {'L0_ffn_gate_b': (0.0, 0.1), 'L0_ffn_b1': (0.0, 0.517), 'L0_ffn_b2': (0.0, 0.1)}
    factors = {'L0_attn_b_bn': 8.0}
    for name, (base, spread) in spreads.items():
        noise = np.random.default_rng([zlib.crc32(name.encode()), seed]).standard_normal(out[name].shape)
        drawn = base * np.exp(spread * noise) if base else spread * noise
        out[name] = jnp.asarray(drawn.astype(out[name].dtype))
    for name, factor in factors.items():
        out[name] = (out[name] * factor).astype(out[name].dtype)
    return out
```

```python
from contextlib import ExitStack

import concourse.bass as bass
from concourse import mybir

F32 = mybir.dt.float32
BF16 = mybir.dt.bfloat16
U32 = mybir.dt.uint32
ALU = mybir.AluOpType
ACT = mybir.ActivationFunctionType
AX = mybir.AxisListType

P = 128
B, S, D = 8, 512, 128
H, DH = 16, 8
TB = S // P
NT = B * TB
E, HID, CAP, K = 64, 512, 64, 3
HC = HID // P
PAIRS = E // 2
RING = 4
EPS = 1e-5
SCALE = 1.0 / DH ** 0.5
NEG = -1e30
NPARTS = 3
Q_ROWS = (0, 0, 1, 1, 0, 2)
K_ROWS = (0, 1, 0, 1, 2, 0)
KR = len(Q_ROWS) * DH
KM = KR + 2
UNITS = 20
BANKS = 40
HG = 8
OUT_OF_RANGE = 8192.0

KEY_BANKS = [[(0, 0, 0, 512)], [(0, 1, 0, 384), (0, 3, 384, 128)], [(1, 0, 0, 512)],
             [(1, 1, 0, 384), (1, 3, 384, 128)], [(0, 2, 0, 256), (1, 2, 256, 256)]]
QUERY_BANKS = [[(0, 3, 0, 512)], [(0, 0, 0, 128), (0, 2, 128, 384)], [(1, 3, 0, 512)],
               [(1, 0, 0, 128), (1, 2, 128, 384)], [(0, 1, 0, 256), (1, 1, 256, 256)]]

A_XT, A_Q, A_QR, A_K, A_KR, A_V, A_MAX, A_MT = 1, 2, 3, 4, 5, 6, 10, 16
A_WO, A_XT2, A_LG, A_POS = 7, 9, 11, 14
C_XT, C_N, C_Q, C_K, C_KV, C_ST = 1, 2, 3, 4, 5, 6
C_WO, C_XT2, C_LG, C_POS = 7, 9, 11, 13


class Chain:

    def __init__(self, eng, sem):
        self.eng, self.sem, self.base, self.k = eng, sem, 0, 0

    def __call__(self, ins):
        self.k += 1
        ins.then_inc(self.sem, 1)
        self.eng.wait_ge(self.sem, self.base + self.k)

    def mark(self, ins):
        self.k += 1
        ins.then_inc(self.sem, 1)

    def settle(self):
        self.eng.wait_ge(self.sem, self.base + self.k)

    def enter(self, i, per):
        self.start = self.base + self.k
        self.base, self.k, self.per = i * per + self.start, 0, per

    def leave(self, turns):
        assert self.k == self.per, (self.sem, self.k, self.per)
        self.base, self.k = self.start + turns * self.per, 0


def place_of(h):
    return 64 * (h // HG), h % HG


def wait(eng, sem, count):
    if not isinstance(count, int) or count > 0:
        eng.wait_ge(sem, count)


def over_batches(eng, body, chain=None, per=0):
    turns = (B - 4) // 2
    for it in range(3):
        body(it, it % 2, True, it >= 1, it >= 2)
    with eng.Fori(0, turns) as i:
        if chain:
            chain.enter(i, per)
        body(i * 2 + 3, 1, True, True, True)
        body(i * 2 + 4, 0, True, True, True)
        if chain:
            chain.leave(turns)
    for it in range(3 + 2 * turns, B + 2):
        body(it, it % 2, it < B, it <= B, True)


def over_pairs(eng, turn):
    for p in range(4):
        turn(p, p % RING, p % 2, True, p >= 1, p >= 2)
    turns = (PAIRS - 4) // RING
    with eng.Fori(0, turns) as i:
        for j in range(RING):
            turn(i * RING + (4 + j), (4 + j) % RING, j % 2, True, True, True)
    for p in range(4 + turns * RING, PAIRS + 2):
        turn(p, p % RING, p % 2, p < PAIRS, p <= PAIRS, True)


def flat(ap):
    return ap.rearrange("p a n -> p (a n)")


def build(nc, x, Wq, Wk, Wv, Wo, Wqk, bqk, bWv, bv, Wn, bn, bWo, bo, gate_w, gate_b, w1, b1, w2, b2,
          cosT, sinT, out):
    ctx = ExitStack()
    with ctx:
        def sb(name, shape, dt=F32):
            return ctx.enter_context(nc.sbuf_tensor(name, shape, dt))

        def sem(name):
            return ctx.enter_context(nc.semaphore(name))

        parts_d = [nc.dram_tensor(f"parts_{n}", (NPARTS, P, S), BF16, kind="Internal").ap() for n in "qk"]
        bucket_d = nc.dram_tensor("bucket", (E * CAP, D), F32, kind="Internal").ap()
        y_d = [nc.dram_tensor(f"expert_out_{n}", (E * CAP, D), F32, kind="Internal").ap() for n in range(2)]

        ident = sb("ident", [P, P])
        ident_b = sb("ident_b", [P, P], BF16)
        mask_q = sb("mask_q", [P, 2, P], BF16)
        mask_k = sb("mask_k", [P, 2, P], BF16)
        keep_k = sb("keep_k", [P, P])
        same_head = sb("same_head", [P, P])
        before = sb("before", [P, P], BF16)
        ones_b = sb("ones_b", [P, P], BF16)
        expert_no = sb("expert_no", [P, E])
        minus_half = sb("minus_half", [P, NT])
        zero1 = sb("zero1", [P, 1])
        pool_scratch, dve_scratch = sb("pool_scratch", [P, 96], BF16), sb("dve_scratch", [P, 96], BF16)
        pool_columns, dve_columns = iter(range(96)), iter(range(96))
        cossin = sb("cossin", [P, 2, S])
        wT = sb("wT", [P, 6, P])
        wq2_s = sb("wq2_s", [P, P])
        wkv_s = sb("wkv_s", [P, 2 * P])
        wn_s = sb("wn_s", [P, P])
        wo2_s = sb("wo2_s", [P, P])
        wn_in = sb("wn_in", [P, H])
        bq_s = sb("bq_s", [P, 2])
        bn_s = sb("bn_s", [P, 2])
        bkv_s = sb("bkv_s", [P, 2 * P])
        bo_s = sb("bo_s", [P, P])
        gate_ws = sb("gate_ws", [P, E])
        gate_bs = sb("gate_bs", [P, E])
        b1_s = sb("b1_s", [P, E, HC])

        xres = sb("xres", [P, NT, D])
        stat1 = sb("stat1", [P, NT, 2])
        rstd1 = sb("rstd1", [P, NT])
        bn6 = sb("bn6", [P, NT, 6])
        var1 = sb("var1", [P, NT])
        nwt1 = sb("nwt1", [P, NT])
        count = sb("count", [P, E], BF16)
        gate_tab = [sb(f"gate_tab{n}", [P, NT, K]) for n in range(2)]
        row_tab = [sb(f"row_tab{n}", [P, NT + TB, K], U32) for n in range(2)]

        vpad_f = sb("vpad", [P, (TB * H + 1) * P])
        vpad = vpad_f[:, 0:TB * H * P].rearrange("p (t h c) -> p t h c", t=TB, h=H)
        qstk = [sb(f"qstk{n}", [P, H // 2, S], BF16) for n in range(2)]
        kstk = [sb(f"kstk{n}", [P, H // 2, S], BF16) for n in range(2)]
        probs = sb("probs", [P, 4, 2 * 512])
        xn = sb("xn", [P, TB, D])
        w_in = xn
        xnT = sb("xnT", [P, S])
        rope = [sb(f"rope_{n}", [P, 2, S]) for n in "qk"]
        parts = [sb(f"parts_{n}s", [P, NPARTS, S], BF16) for n in "qk"]
        v_s = sb("v_s", [P, TB, P])
        bmax = sb("bmax", [P, BANKS * 4])
        negm = sb("negm", [P, 2, TB, HG])
        mbuf = sb("mbuf", [P, S])
        mparts = mbuf[0:HG, :].bitcast(BF16).rearrange("p (a s) -> p a s", a=2)
        o_s = sb("o_s", [P, S])
        rden = sb("rden", [P, S])
        attnT = sb("attnT", [P, S])
        qs = [rope[0][:, 0, :], sb("qs1", [P, S])[:, :]]
        kvn = cossin[:, :, :].rearrange("p a (t n) -> p (a t) n", n=2 * P)
        stm = [v_s[:, 0:TB - 1, :], mbuf[:, :].rearrange("p (t n) -> p t n", n=P)[:, 0:TB - 1, :]]
        nexp = rden

        xn2 = sb("xn2", [P, TB, D])
        xn2T = sb("xn2T", [P, S])
        rst6 = sb("rst6", [P, TB, 6])
        rst2 = sb("rst2", [P, TB, 2])
        rvar = sb("rvar", [P, TB])
        rpow = sb("rpow", [P, TB])
        rnwt = sb("rnwt", [P, TB])
        logit = sb("logit", [P, TB, E])
        top8 = sb("top8", [P, TB, 8])
        idx8 = sb("idx8", [P, TB, 8], U32)
        topi = sb("topi", [P, TB, K])
        topd = sb("topd", [P, TB, K])
        tope = sb("tope", [P, TB, K])
        esum = sb("esum", [P, TB])
        onehot = sb("onehot", [P, K, TB, E], BF16)
        chosen = sb("chosen", [P, TB, E], BF16)
        csum = sb("csum", [P, E])
        ptmp = sb("ptmp", [P, K, TB, E])
        pos = sb("pos", [P, TB, K])
        room = sb("room", [P, TB, K])
        slot = sb("slot", [P, TB, K])
        slot_u = sb("slot_u", [P, TB * K], U32)
        row_u = [sb(f"row_u{n}", [P, TB * K], U32) for n in range(2)]
        yrows = [sb(f"yrows{n}", [P, TB * K, D]) for n in range(2)]

        w1_s = sb("w1_s", [P, RING, 2, HID])
        w2_s = sb("w2_s", [P, RING, 2, HC, D])
        xb_s = sb("xb_s", [P, RING, D])
        xbT = sb("xbT", [P, 2, P])
        b2_s = sb("b2_s", [P, RING, D])
        hpre = probs[:, 0:1, :].rearrange("p b (q a c n) -> p (b q) a c n", q=2, a=2, c=HC)
        hact = probs[:, 1:2, :].rearrange("p b (q a c n) -> p (b q) a c n", q=2, a=2, c=HC)
        y_s = probs[:, 2, 0:2 * D].rearrange("p (q d) -> p q d", q=2)

        bank = ctx.enter_context(nc.psum_tensor("bank", [P, 8, 512], F32))
        SC = bank[:, 0:4, :]
        MX = bank[:, 4:6, :]
        O = bank[:, 6, :]
        X = bank[:, 7, :]
        Xt = X.rearrange("p (t n) -> p t n", t=TB)

        consts_dma, x_dma, w_dma, bias_dma, zero_dma = map(sem, ("consts_dma", "x_dma", "w_dma", "bias_dma", "zero_dma"))
        consts_ready, zeros_ready = sem("consts_ready"), sem("zeros_ready")
        wT_full, wT_copied, weights_ready = sem("wT_full"), sem("wT_copied"), sem("weights_ready")
        var1_ready, pow1_ready, ln1_ready = sem("var1_ready"), sem("pow1_ready"), sem("ln1_ready")
        dve_chain, pool_chain = sem("dve_chain"), sem("pool_chain")

        def sems(n, *names):
            return {s: sem(f"{s}_{n}") for s in names}

        both = ("xn_ready", "xt_full", "xnT_ready", "proj_full", "split_ready", "parts_written", "stack_loaded",
                "vpad_ready", "score_full", "probs_ready", "pv_done", "o_copied", "wo_full", "residual_ready")
        sa = sems("a", *both, "rope_ready", "v_ready", "max_full", "max_done", "negm_ready", "mt_full",
                  "mparts_ready", "mrows_loaded", "attn_ready")
        sc_ = sems("c", *both, "nexp_ready", "q_ready", "k_ready", "kv_full", "kvn_ready", "state_full",
                   "state_ready", "row_u_ready", "vpad_cleared", "var_ready", "pow_ready")

        def routing_sems(n):
            return {s: sem(f"{s}_{n}") for s in (
                "rvar_ready", "rpow_ready", "xn2_ready", "xt2_full", "xn2T_ready", "logit_full",
                "topd_ready", "tope_ready", "chosen_ready", "pos_full", "pos_read", "slot_ready",
                "scattered")}

        def expert_sems(n):
            return {s: sem(f"{s}_{n}") for s in (
                "xbt_full", "xbt_ready", "h_full", "hpre_ready", "h_ready", "y_full", "y_ready")} | {
                "y_stored": [sem(f"y_stored_{n}_{j}") for j in range(2)],
                "landed": [sem(f"landed_{n}_{r}") for r in range(RING)]}

        ra, rc, eb, ed = routing_sems("a"), routing_sems("c"), expert_sems("b"), expert_sems("d")
        final_rows, final_ready, out_stored = map(sem, ("final_rows", "final_ready", "out_stored"))
        rows_gathered, final_gathered = ([sem(f"{s}_{j}") for j in range(2)] for s in ("rows_gathered", "final_gathered"))
        GATHER = TB * K * 16

        x_v = x.rearrange("b (t p) d -> p (b t) d", p=P)
        out_v = out.rearrange("b (t p) d -> p (b t) d", p=P)
        w1_v = w1.rearrange("e d h -> d e h")
        w2_v = w2.rearrange("e (p c) d -> p e c d", c=HC)
        PAIR_DMAS = 5
        MROW_DMAS = 2 * HG
        STACK_DMAS = 2 * 2 * len(Q_ROWS)
        BIAS_DMAS = 2 + DH + 4 + 1

        block = ctx.enter_context(nc.Block())

        @block.sync
        def _(sp):
            for dst, src in ((w_in[:, 0, :], Wq), (w_in[:, 1, :], Wk), (w_in[:, 2, :], Wv), (w_in[:, 3, :], Wo)):
                sp.dma_start(dst, src).then_inc(w_dma, 16)
            sp.dma_start(xres[:, :, :], x_v).then_inc(x_dma, 16)
            for dst, src in ((cossin[:, 0, :], cosT), (cossin[:, 1, :], sinT), (wq2_s[:, :], Wqk[:, 0:P]),
                             (wkv_s[:, 0:P], Wqk[:, P:2 * P]), (wkv_s[:, P:2 * P], bWv), (wo2_s[:, :], bWo),
                             (wn_in[:, :], Wn), (gate_ws[:, :], gate_w)):
                sp.dma_start(dst, src).then_inc(consts_dma, 16)
            for t in range(2):
                sp.dma_start(bq_s[:, t:t + 1], bqk[t * P:(t + 1) * P].rearrange("(p o) -> p o", o=1)).then_inc(bias_dma, 16)
            for j in range(DH):
                sp.dma_start(bn_s[j:P:DH, 0:1], bn.rearrange("(h o) -> h o", o=1)).then_inc(bias_dma, 16)
            for dst, src in ((bkv_s[:, 0:P], bqk[P:2 * P]), (bkv_s[:, P:2 * P], bv), (bo_s[:, :], bo),
                             (gate_bs[:, :], gate_b)):
                sp.dma_start(dst, src.unsqueeze(0).to_broadcast([P, src.shape[0]])).then_inc(bias_dma, 16)
            sp.dma_start(b1_s[:, :, :], b1.rearrange("e (p c) -> p e c", c=HC)).then_inc(bias_dma, 16)
            sp.wait_ge(zeros_ready, 1)
            sp.dma_start(bucket_d.rearrange("(p r) d -> p (r d)", p=P), vpad_f[:, 0:E * CAP * D // P]).then_inc(zero_dma, 16)

            def load_weights(e, q, r):
                sp.dma_start(w1_s[:, r, :, :], w1_v[:, bass.ds(q * 2, 2), :]).then_inc(e["landed"][r], 16)
                sp.dma_start(w2_s[:, r, :, :, :], w2_v[:, bass.ds(q * 2, 2), :, :]).then_inc(e["landed"][r], 16)
                for t in range(2):
                    sp.dma_start(b2_s[CAP * t:CAP * (t + 1), r, :], b2[bass.ds(q * 2 + t, 1), :]
                                 .to_broadcast([CAP, D])).then_inc(e["landed"][r], 16)

            def load_bucket(e, q, r):
                sp.dma_start(xb_s[:, r, :], bucket_d[bass.ds(q * P, P), :]).then_inc(e["landed"][r], 16)

            def store_y(e, q, r, yd):
                sp.wait_ge(e["y_ready"], q + 1)
                sp.dma_start(yd[bass.ds(q * P, P), :], y_s[:, r % 2, :]).then_inc(e["y_stored"][r % 2], 16)

            def restack(s, b, par, n):
                sp.wait_ge(s["split_ready"], b * 2 + n + 1)
                sp.dma_start(parts_d[n].rearrange("g p s -> p g s"), parts[n][:, :, :]).then_inc(s["parts_written"], 16)
                sp.wait_ge(s["parts_written"], (b * 2 + n + 1) * 16)
                src = parts_d[n].rearrange("g (t a d) s -> g t d a s", t=2, d=DH)
                dst = (qstk, kstk)[n][par]
                for g, part in enumerate((Q_ROWS, K_ROWS)[n]):
                    for t in range(2):
                        at = 64 * t + DH * g
                        sp.dma_start(dst[at:at + DH, :, :], src[part, t]).then_inc(s["stack_loaded"], 16)

            def stacks(s, b, par, units):
                wait(sp, s["score_full"], (b - 1) * units)
                wait(sp, s["stack_loaded"], b * STACK_DMAS * 16)
                restack(s, b, par, 0)
                restack(s, b, par, 1)

            def a_body(it, par, s1, s2, s3):
                if not s1:
                    return
                stacks(sa, it, par, UNITS)
                for half in range(2):
                    sp.wait_ge(sa["mparts_ready"], it * 2 + half + 1)
                    for j in range(HG):
                        for part in range(2):
                            p0, col = place_of(HG * half + j)
                            sp.dma_start(qstk[par][p0 + KR + part:p0 + KR + part + 1, col, :],
                                         mparts[j:j + 1, part, :]).then_inc(sa["mrows_loaded"], 16)

            def c_body(it, par, s1, s2, s3):
                if s1:
                    stacks(sc_, it, par, H)

            def expert_phase(e, ring_ready, yd):
                for q in range(RING):
                    load_weights(e, q, q)
                ring_ready()
                for q in range(RING):
                    load_bucket(e, q, q)

                def turn(q, r):
                    store_y(e, q, r, yd)
                    load_weights(e, q + RING, r)
                    load_bucket(e, q + RING, r)

                n = (PAIRS - RING) // RING
                with sp.Fori(0, n) as i:
                    for r in range(RING):
                        turn(i * RING + r, r)
                for q in range(n * RING, PAIRS):
                    if q + RING < PAIRS:
                        turn(q, q % RING)
                    else:
                        store_y(e, q, q % RING, yd)
                for j in range(2):
                    sp.wait_ge(e["y_stored"][j], PAIRS // 2 * 16)

            def phase_a():
                over_batches(sp, a_body)
                sp.wait_ge(ra["scattered"], B * TB * K * 16)
            expert_phase(eb, phase_a, y_d[0])

            def phase_c():
                over_batches(sp, c_body)
                sp.wait_ge(rc["scattered"], B * TB * K * 16)
            expert_phase(ed, phase_c, y_d[1])
            with sp.Fori(0, B) as b:
                sp.wait_ge(final_ready, b + 1)
                sp.dma_start(out_v[:, bass.ds(b * TB, TB), :], xres[:, bass.ds(b * TB, TB), :]).then_inc(out_stored, 16)
            sp.wait_ge(out_stored, B * 16)

        @block.gpsimd
        def _(pool):
            link = Chain(pool, pool_chain)

            def select(t, pattern, op, fill, base=0, cm=1):
                link(nc.gpsimd.affine_select(out=t, in_=t, pattern=pattern, compare_op=op, fill=fill, base=base,
                                             channel_multiplier=cm))

            nc.gpsimd.memset(vpad_f[:, :], 0.0).then_inc(zeros_ready, 1)
            nc.gpsimd.memset(minus_half[:, :], -0.5)
            nc.gpsimd.memset(zero1[:, :], 0.0)
            nc.gpsimd.memset(row_tab[0][:, NT:NT + TB, :], 0)
            nc.gpsimd.memset(ident[:, :], 0.0)
            nc.gpsimd.memset(ident_b[:, :], 0.0)
            nc.gpsimd.memset(mask_q[:, :, :], 0.0)
            nc.gpsimd.memset(mask_k[:, :, :], 0.0)
            nc.gpsimd.memset(keep_k[:, :], 1.0)
            nc.gpsimd.memset(same_head[:, :], 1.0)
            nc.gpsimd.memset(before[:, :], 1.0)
            nc.gpsimd.memset(count[:, :], 0.0)
            nc.gpsimd.memset(kstk[0][:, :, :], 1.0)
            nc.gpsimd.memset(kstk[1][:, :, :], 1.0)
            nc.gpsimd.iota(expert_no[:, :], pattern=[[1, E]], base=0, channel_multiplier=0,
                           allow_small_or_imprecise_dtypes=True)
            link(nc.gpsimd.memset(ones_b[:, :], 1.0))
            select(ident[:, :], [[-1, P]], ALU.not_equal, 1.0)
            select(ident_b[:, :], [[-1, P]], ALU.not_equal, 1.0)
            select(mask_q[:, :, :], [[0, 2], [-1, P]], ALU.is_ge, NEG)
            select(mask_k[:, :, :], [[0, 2], [1, P]], ALU.is_ge, NEG, cm=-1)
            select(keep_k[:, :], [[1, P]], ALU.is_ge, 0.0, cm=-1)
            select(same_head[:, :].rearrange("p (h d) -> p h d", d=DH), [[-DH, H], [0, DH]], ALU.is_ge, 0.0)
            select(same_head[:, :].rearrange("p (h d) -> p h d", d=DH), [[DH, H], [0, DH]], ALU.is_ge, 0.0,
                   base=DH - 1, cm=-1)
            select(before[:, :], [[1, P]], ALU.is_gt, 0.0, cm=-1)
            pool.wait_ge(zero_dma, 16)
            for t in range(TB):
                for g in range(2):
                    v = vpad[:, t, HG * g:HG * g + HG, 64:P].rearrange("p h (j d) -> p h j d", d=DH)
                    select(v, [[1, HG], [-1, HG], [0, DH]], ALU.not_equal, 1.0, cm=0)
            nc.gpsimd.memset(rnwt[:, :], 0.0).then_inc(consts_ready, 1)
            pool.wait_ge(var1_ready, 1)
            nc.gpsimd.tensor_tensor(rstd1[:, :], var1[:, :], minus_half[:, :], ALU.pow).then_inc(pow1_ready, 1)

            def split(n, s, b):
                high, src = parts[n][:, 0, :], rope[n][:, 0, :]
                wait(pool, s["parts_written"], (b * 2 + n - 1) * 16)
                pool.wait_ge(s["rope_ready"], b * 4 + 2 * n + 2)
                nc.gpsimd.tensor_tensor(high, rope[n][:, 0, :], rope[n][:, 1, :], ALU.add)
                link(nc.gpsimd.tensor_tensor(src, rope[n][:, 0, :], rope[n][:, 1, :], ALU.add))
                split_rest(n, s, src)

            def split_parts(n, s, src):
                link(nc.gpsimd.tensor_tensor(parts[n][:, 0, :], src, zero1[:, :].to_broadcast([P, S]), ALU.add))
                split_rest(n, s, src)

            def split_rest(n, s, src):
                high, mid, low = (parts[n][:, j, :] for j in range(NPARTS))
                rest = rope[n][:, 1, :]
                nc.gpsimd.tensor_tensor(mid, src, high, ALU.subtract)
                link(nc.gpsimd.tensor_tensor(rest, src, high, ALU.subtract))
                nc.gpsimd.tensor_tensor(low, rest, mid, ALU.subtract).then_inc(s["split_ready"], 1)

            def fence():
                n = next(pool_columns)
                return nc.gpsimd.tensor_tensor(pool_scratch[:, n:n + 1], minus_half[:, 0:1], minus_half[:, 0:1], ALU.mult)

            def fill_vpad(s, g, src, first):
                wide = P + DH
                fence()
                for t in range(TB):
                    at = (t * H + HG * g) * P + first
                    last = nc.gpsimd.tensor_copy(
                        vpad_f[:, at:at + HG * wide].rearrange("p (j c) -> p j c", c=wide)[:, :, 0:DH],
                        src[:, t, HG * g * DH:HG * (g + 1) * DH].rearrange("p (j d) -> p j d", d=DH))
                last.then_inc(s["vpad_ready"], 1)

            def power(ready, done, b):
                pool.wait_ge(ready, b + 1)
                nc.gpsimd.tensor_tensor(rpow[:, :], rvar[:, :], minus_half[:, 0:TB], ALU.pow).then_inc(done, 1)

            def scatter(r, d):
                pool.wait_ge(r["slot_ready"], d + 1)
                fence()
                for t in range(TB):
                    for k in range(K):
                        j = t * K + k
                        nc.gpsimd.indirect_dma_start(
                            bucket_d[:, :], bass.IndirectOffsetOnAxis(ap=slot_u[:, j:j + 1], axis=0),
                            xn2[:, t, :], None, bounds_check=E * CAP - 1, oob_is_err=False).then_inc(r["scattered"], 16)

            def gather(src_d, ready, gathered, b, par):
                link.settle()
                pool.wait_ge(ready, b + 1)
                link.mark(fence())
                for j in range(TB * K):
                    nc.gpsimd.indirect_dma_start(
                        yrows[par][:, j, :], None, src_d[:, :],
                        bass.IndirectOffsetOnAxis(ap=row_u[par][:, j:j + 1], axis=0),
                        bounds_check=E * CAP - 1, oob_is_err=False).then_inc(gathered[par], 16)

            def a_body(it, par, s1, s2, s3):
                if s2:
                    wait(pool, sa["pv_done"], (it - 1) * UNITS)
                    fill_vpad(sa, 1, v_s, 0)
                if s1:
                    split(0, sa, it)
                    split(1, sa, it)
                if s3:
                    power(ra["rvar_ready"], ra["rpow_ready"], it - 2)
                if s1:
                    pool.wait_ge(sa["v_ready"], it + 1)
                    wait(pool, sa["pv_done"], (it - 1) * UNITS + UNITS // 2)
                    fill_vpad(sa, 0, v_s, 0)
                if s3:
                    scatter(ra, it - 2)

            over_batches(pool, a_body, link, 8)

            pool.wait_ge(sa["pv_done"], B * UNITS)
            nc.gpsimd.memset(count[:, :], 0.0)
            nc.gpsimd.memset(vpad_f[:, :], 0.0).then_inc(sc_["vpad_cleared"], 1)
            pool.wait_ge(sc_["vpad_cleared"], 1)
            for j in range(2):
                pool.wait_ge(eb["y_stored"][j], PAIRS // 2 * 16)
            gather(y_d[0], sc_["row_u_ready"], rows_gathered, 0, 0)

            def c_body(it, par, s1, s2, s3):
                kv_v = kvn[:, :, P:2 * P]
                if s2:
                    wait(pool, sc_["pv_done"], (it - 1) * H)
                    fill_vpad(sc_, 1, kv_v, HG * DH)
                if s1:
                    power(sc_["var_ready"], sc_["pow_ready"], it)
                    gather(y_d[0], sc_["row_u_ready"], rows_gathered, it + 1, 1 - par)
                    pool.wait_ge(sc_["q_ready"], it + 1)
                    wait(pool, sc_["parts_written"], (it * 2 - 1) * 16)
                    split_parts(0, sc_, qs[par])
                    pool.wait_ge(sc_["k_ready"], it + 1)
                    wait(pool, sc_["parts_written"], it * 2 * 16)
                    split_parts(1, sc_, rope[1][:, 0, :])
                if s3:
                    power(rc["rvar_ready"], rc["rpow_ready"], it - 2)
                if s1:
                    pool.wait_ge(sc_["kvn_ready"], it + 1)
                    wait(pool, sc_["pv_done"], (it - 1) * H + HG)
                    fill_vpad(sc_, 0, kv_v, 0)
                if s3:
                    scatter(rc, it - 2)

            over_batches(pool, c_body, link, 10)
            pool.wait_ge(rows_gathered[0], (B // 2 + 1) * GATHER)
            for j in range(2):
                pool.wait_ge(ed["y_stored"][j], PAIRS // 2 * 16)
            with pool.Fori(0, B // 2) as i:
                link.enter(i, 2)
                for par in range(2):
                    gather(y_d[1], final_rows, final_gathered, i * 2 + par, par)
                link.leave(B // 2)

        @block.scalar
        def _(act):
            act.wait_ge(wT_full, 1)
            nc.scalar.activation(wT[:, 0, :], Xt[:, 0, :], ACT.Copy)
            nc.scalar.activation(wT[:, 2, :], Xt[:, 1, :], ACT.Copy)
            nc.scalar.activation(wT[:, 4:6, :], Xt[:, 2:4, :], ACT.Copy).then_inc(wT_copied, 1)

            def evacuate(dst, src, full, count_, done):
                act.wait_ge(full, count_)
                nc.scalar.activation(dst, src, ACT.Copy).then_inc(done, 1)

            def take_out(s, n, after):
                act.wait_ge(s["pv_done"], after)
                wait(act, s["attn_ready"], n)
                nc.scalar.activation(o_s[:, :], O, ACT.Copy).then_inc(s["o_copied"], 1)

            def transposed_again(r, d):
                evacuate(xn2T[:, :], X, r["xt2_full"], d + 1, r["xn2T_ready"])

            def gate_exp(r, d):
                act.wait_ge(r["topd_ready"], d + 1)
                nc.scalar.activation(tope[:, :, :], topd[:, :, :], ACT.Exp).then_inc(r["tope_ready"], 1)

            def a_body(it, par, s1, s2, s3):
                b, c, d = it, it - 1, it - 2
                for u in range(UNITS):
                    if s2:
                        act.wait_ge(sa["score_full"], c * UNITS + u + 1)
                        wait(act, sa["pv_done"], c * UNITS + u - 3)
                        nc.scalar.activation(probs[:, u % 4, :].rearrange("p (a n) -> p a n", a=2),
                                             SC[:, 2 * (u % 2):2 * (u % 2) + 2, :], ACT.Exp, scale=SCALE) \
                            .then_inc(sa["probs_ready"], 1)
                        if u == UNITS // 2:
                            take_out(sa, c * 2, c * UNITS + UNITS // 2)
                    if s1 and u == A_XT:
                        evacuate(xnT[:, :], X, sa["xt_full"], b + 1, sa["xnT_ready"])
                    if s1 and u == A_V:
                        wait(act, sa["vpad_ready"], b * 2)
                        evacuate(v_s[:, :, :], Xt, sa["proj_full"], b * 5 + 5, sa["v_ready"])
                    if s3 and u == A_XT2:
                        transposed_again(ra, d)
                    if s3 and u == A_POS - 1:
                        gate_exp(ra, d)
                if s2:
                    take_out(sa, c * 2 + 1, c * UNITS + UNITS)

            over_batches(act, a_body)

            def expert_phase(e):
                def turn(p, r, par, t, h, y):
                    if t:
                        act.wait_ge(e["xbt_full"], p + 1)
                        nc.scalar.activation(xbT[:, par, :], bank[:, par, 0:P], ACT.Copy).then_inc(e["xbt_ready"], 1)
                    if h:
                        act.wait_ge(e["hpre_ready"], p)
                        wait(act, e["y_full"], p - 2)
                        nc.scalar.activation(hact[:, 1 - par, :, :, :], hpre[:, 1 - par, :, :, :], ACT.Gelu) \
                            .then_inc(e["h_ready"], 1)
                over_pairs(act, turn)

            expert_phase(eb)

            def c_body(it, par, s1, s2, s3):
                b, c, d = it, it - 1, it - 2
                for u in range(H):
                    if s1 and u == C_XT:
                        evacuate(xnT[:, :], X, sc_["xt_full"], b + 1, sc_["xnT_ready"])
                    if s1 and u == C_N:
                        act.wait_ge(sc_["proj_full"], b * 3 + 1)
                        wait(act, sc_["q_ready"], b)
                        nc.scalar.activation(nexp[:, :], X, ACT.Exp, scale=-1.0, bias=bn_s[:, 1:2]) \
                            .then_inc(sc_["nexp_ready"], 1)
                    if s1 and u == C_K:
                        act.wait_ge(sc_["proj_full"], b * 3 + 3)
                        wait(act, sc_["split_ready"], b * 2)
                        nc.scalar.activation(rope[1][:, 0, :], X, ACT.Identity, bias=bq_s[:, 1:2]) \
                            .then_inc(sc_["k_ready"], 1)
                    if s3 and u == C_XT2:
                        transposed_again(rc, d)
                    if s3 and u == C_POS - 1:
                        gate_exp(rc, d)
                if s2:
                    act.wait_ge(sc_["pv_done"], c * H + H)
                    wait(act, sc_["wo_full"], c)
                    nc.scalar.activation(attnT[:, :], O, ACT.Copy).then_inc(sc_["o_copied"], 1)

            over_batches(act, c_body)
            expert_phase(ed)

        @block.vector
        def _(dve):
            link = Chain(dve, dve_chain)
            tt, ts, stt = nc.vector.tensor_tensor, nc.vector.tensor_scalar, nc.vector.scalar_tensor_tensor

            def refine(y, v, t):
                link(tt(t, y, y, ALU.mult))
                link(tt(t, t, v, ALU.mult))
                link(ts(t, t, -0.5, 1.5, ALU.mult, ALU.add))
                return tt(y, y, t, ALU.mult)

            nc.vector.memset(rvar[:, :], 0.0)
            dve.wait_ge(x_dma, 16)
            for t in range(NT):
                last = nc.vector.bn_stats(bn6[:, t, :], xres[:, t, :])
            link(last)
            for t in range(NT):
                last = nc.vector.bn_aggr(stat1[:, t, :], bn6[:, t, :])
            link(last)
            ts(var1[:, :], stat1[:, :, 1], EPS, None, ALU.add).then_inc(var1_ready, 1)
            dve.wait_ge(wT_copied, 1)
            for n in (0, 2):
                for t in range(2):
                    last = nc.vector.tensor_copy(
                        wT[:, n + 1, :].rearrange("p (h t d) -> p h t d", t=2, d=DH // 2)[:, :, t, :],
                        wT[:, n, :].rearrange("p (h t d) -> p h t d", t=2, d=DH // 2)[:, :, 1 - t, :])
            dve.wait_ge(consts_dma, 8 * 16)
            dve.wait_ge(bias_dma, BIAS_DMAS * 16)
            ts(bn_s[:, 1:2], bn_s[:, 0:1], -1.0, None, ALU.mult)
            nc.vector.tensor_copy(wn_s[:, :].rearrange("p (h d) -> p h d", d=DH),
                                  wn_in[:, :].unsqueeze(2).to_broadcast([P, H, DH])).then_inc(weights_ready, 1)
            dve.wait_ge(pow1_ready, 1)
            dve.wait_ge(consts_ready, 1)
            link(refine(rstd1[:, :], var1[:, :], nwt1[:, :]))

            def fence():
                n = next(dve_columns)
                nc.vector.tensor_copy(dve_scratch[:, n:n + 1], ident[:, 0:1])

            def statistics(tile0):
                fence()
                for t in range(TB):
                    last = nc.vector.bn_stats(rst6[:, t, :], xres[:, bass.ds(tile0 + t, 1), :].rearrange("p a d -> p (a d)"))
                link(last)
                fence()
                for t in range(TB):
                    last = nc.vector.bn_aggr(rst2[:, t, :], rst6[:, t, :])
                link(last)
                return ts(rvar[:, :], rst2[:, :, 1], EPS, None, ALU.add)

            def normalise(dst, tile0, mean, rstd):
                for t in range(TB):
                    last = ts(dst[:, t, :], xres[:, bass.ds(tile0 + t, 1), :].rearrange("p a d -> p (a d)"),
                              mean(t), rstd(t), ALU.subtract, ALU.mult)
                return last

            def norm_2(r, d):
                statistics(d * TB).then_inc(r["rvar_ready"], 1)
                dve.wait_ge(r["rpow_ready"], d + 1)
                link(refine(rpow[:, :], rvar[:, :], rnwt[:, :]))
                wait(dve, r["scattered"], d * TB * K * 16)
                normalise(xn2, d * TB, lambda t: rst2[:, t, 0:1], lambda t: rpow[:, t:t + 1]).then_inc(r["xn2_ready"], 1)

            def choose(r, n, d):
                dve.wait_ge(r["logit_full"], d + 1)
                link(tt(logit[:, :, :], X[:, 0:TB * E].rearrange("p (t e) -> p t e", e=E),
                        gate_bs[:, :].unsqueeze(1).to_broadcast([P, TB, E]), ALU.add))
                fence()
                for t in range(TB):
                    last = nc.vector.max(top8[:, t, :], logit[:, t, :])
                link(last)
                tt(topd[:, :, :], top8[:, :, 0:K], top8[:, :, 0:1].to_broadcast([P, TB, K]), ALU.subtract) \
                    .then_inc(r["topd_ready"], 1)
                for t in range(TB):
                    last = nc.vector.max_index(idx8[:, t, :], top8[:, t, :], logit[:, t, :])
                link(last)
                link(nc.vector.tensor_copy(topi[:, :, :], idx8[:, :, 0:K]))
                for k in range(K):
                    last = tt(onehot[:, k, :, :], expert_no[:, :].unsqueeze(1).to_broadcast([P, TB, E]),
                              topi[:, :, k:k + 1].to_broadcast([P, TB, E]), ALU.is_equal)
                link(last)
                link(tt(ptmp[:, 0, :, :], onehot[:, 0, :, :], onehot[:, 1, :, :], ALU.add))
                tt(chosen[:, :, :], ptmp[:, 0, :, :], onehot[:, 2, :, :], ALU.add).then_inc(r["chosen_ready"], 1)

            def place(r, n, d):
                dve.wait_ge(r["pos_full"], d + 1)
                pos_ps = X[:, 0:TB * E].rearrange("p (t e) -> p t e", e=E)
                for k in range(K):
                    last = tt(ptmp[:, k, :, :], onehot[:, k, :, :], pos_ps, ALU.mult)
                last.then_inc(r["pos_read"], 1)
                dve.wait_ge(r["pos_read"], d + 1)
                for k in range(K):
                    last = nc.vector.reduce_sum(pos[:, :, k], ptmp[:, k, :, :], AX.X)
                link(last)
                dve.wait_ge(r["tope_ready"], d + 1)
                link(nc.vector.reduce_sum(esum[:, :], tope[:, :, :], AX.X))
                link(nc.vector.reciprocal(esum[:, :], esum[:, :]))
                link(tt(tope[:, :, :], tope[:, :, :], esum[:, :].unsqueeze(2).to_broadcast([P, TB, K]), ALU.mult))
                link(nc.vector.reduce_sum(csum[:, :], chosen[:, :, :].rearrange("p t e -> p e t"), AX.X))
                link(tt(count[:, :], count[:, :], csum[:, :], ALU.add))
                ts(room[:, :, :], pos[:, :, :], float(CAP), None, ALU.is_lt)
                link(stt(slot[:, :, :], topi[:, :, :], float(CAP), pos[:, :, :], ALU.mult, ALU.add))
                link(tt(gate_tab[n][:, bass.ds(d * TB, TB), :], tope[:, :, :], room[:, :, :], ALU.mult))
                link(ts(room[:, :, :], room[:, :, :], -OUT_OF_RANGE, OUT_OF_RANGE, ALU.mult, ALU.add))
                tt(slot_u[:, :].rearrange("p (t k) -> p t k", k=K), slot[:, :, :], room[:, :, :], ALU.add) \
                    .then_inc(r["slot_ready"], 1)
                link(ts(pos[:, :, :], pos[:, :, :], float(CAP - 1), None, ALU.min))
                link(stt(slot[:, :, :], topi[:, :, :], float(CAP), pos[:, :, :], ALU.mult, ALU.add))
                link(nc.vector.tensor_copy(row_tab[n][:, bass.ds(d * TB, TB), :], slot[:, :, :]))

            def normalise_group(s, n, g):
                dve.wait_ge(s["o_copied"], n + 1)
                link(nc.vector.reciprocal(rden[0:64, :], o_s[64:P, :]))
                tt(attnT[64 * g:64 * g + 64, :], o_s[0:64, :], rden[0:64, :], ALU.mult).then_inc(s["attn_ready"], 1)

            def maxima(it, u):
                for k in range(4 * (u - A_MAX), 4 * (u - A_MAX) + 4):
                    dve.wait_ge(sa["max_full"], it * BANKS + k + 1)
                    last = nc.vector.tensor_reduce(bmax[:, 4 * k:4 * k + 4],
                                                   MX[:, k % 2, :].rearrange("p (j n) -> p j n", n=P), AX.X, ALU.max)
                    last.then_inc(sa["max_done"], 1)

            def join_maxima(it, half):
                dve.wait_ge(sa["max_done"], it * BANKS + 20 * (half + 1))
                wait(dve, sa["mt_full"], it * 2 + half)
                v = bmax[:, 80 * half:80 * half + 80].rearrange("p (r c) -> p r c", c=20)
                wide = v[:, :, 0:16].rearrange("p r (h c) -> p r h c", c=8)
                tail = v[:, :, 16:20].rearrange("p r (h c) -> p r h c", c=2)
                dst = negm[:, half, :, :].rearrange("p q (r h) -> p q r h", h=2)
                for q, src in ((3, wide[:, :, :, 0:4]), (0, wide[:, :, :, 4:5]), (2, wide[:, :, :, 5:8]), (1, tail)):
                    last = nc.vector.tensor_reduce(dst[:, q, :, :], src, AX.X, ALU.max, negate=True)
                last.then_inc(sa["negm_ready"], 1)

            def split_maxima(it, half):
                dve.wait_ge(sa["mt_full"], it * 2 + half + 1)
                wait(dve, sa["mrows_loaded"], (it * 2 + half) * MROW_DMAS * 16)
                link(nc.vector.tensor_copy(mparts[:, 0, :], X[0:HG, :]))
                tt(mparts[:, 1, :], X[0:HG, :], mparts[:, 0, :], ALU.subtract).then_inc(sa["mparts_ready"], 1)

            def a_body(it, par, s1, s2, s3):
                b, c, d = it, it - 1, it - 2
                if s1:
                    wait(dve, sa["xt_full"], b)
                    t0 = b * TB
                    for t in range(TB):
                        last = ts(xn[:, t, :], xres[:, bass.ds(t0 + t, 1), :].rearrange("p a d -> p (a d)"),
                                  stat1[:, bass.ds(t0 + t, 1), 0:1].rearrange("p a d -> p (a d)"),
                                  rstd1[:, bass.ds(t0 + t, 1)], ALU.subtract, ALU.mult)
                    last.then_inc(sa["xn_ready"], 1)
                if s3:
                    normalise_group(sa, d * 2 + 1, 1)
                for u in range(UNITS):
                    if s1 and A_Q <= u <= A_KR:
                        n, j = divmod(u - A_Q, 2)
                        dve.wait_ge(sa["proj_full"], b * 5 + (u - A_Q) + 1)
                        if j == 0:
                            wait(dve, sa["split_ready"], b * 2 + n - 1)
                        tt(rope[n][:, j, :], X, cossin[:, j, :], ALU.mult).then_inc(sa["rope_ready"], 1)
                    if s3 and u == A_WO:
                        dve.wait_ge(sa["wo_full"], d + 1)
                        xt = xres[:, bass.ds(d * TB, TB), :]
                        ins = tt(xt, Xt, xt, ALU.add)
                        ins.then_inc(sa["residual_ready"], 1)
                        dve.wait_ge(sa["residual_ready"], d + 1)
                        norm_2(ra, d)
                    if s3 and u == A_LG:
                        choose(ra, 0, d)
                    if s1 and u >= A_MAX:
                        maxima(b, u)
                    if s2 and u == 12:
                        wait(dve, sa["wo_full"], c)
                        normalise_group(sa, c * 2, 0)
                    if s3 and u == A_POS:
                        place(ra, 0, d)
                    if s1 and u == A_MAX + 4:
                        join_maxima(b, 0)
                    if s1 and u == A_MT:
                        split_maxima(b, 0)
                if s1:
                    join_maxima(b, 1)
                    split_maxima(b, 1)

            over_batches(dve, a_body, link, 2 * 28)

            def expert_phase(e):
                def turn(p, r, par, t, h, y):
                    if h:
                        dve.wait_ge(e["h_full"], p)
                        wait(dve, e["h_ready"], p - 2)
                        q = p - 1
                        tt(hpre[:, 1 - par, :, :, :].rearrange("p a c n -> p (a c) n"),
                           bank[:, 2 + (1 - par), :].rearrange("p (a n) -> p a n", n=CAP),
                           b1_s[:, bass.ds(q * 2, 2), :].rearrange("p a c -> p (a c)").unsqueeze(2)
                           .to_broadcast([P, 2 * HC, CAP]), ALU.add).then_inc(e["hpre_ready"], 1)
                    if y:
                        dve.wait_ge(e["y_full"], p - 1)
                        wait(dve, e["y_stored"][par], (p - par - 2) * 8)
                        q = p - 2
                        tt(y_s[:, par, :], bank[:, 4 + par, 0:D],
                           b2_s[:, (r - 2) % RING, :], ALU.add).then_inc(e["y_ready"], 1)
                over_pairs(dve, turn)

            expert_phase(eb)

            def rows(n, ready, b, par):
                nc.vector.tensor_copy(row_u[par][:, :].rearrange("p (t k) -> p t k", k=K),
                                      row_tab[n][:, bass.ds(b * TB, TB), :]).then_inc(ready, 1)

            def add_rows(n, b, par):
                for k in range(K):
                    for t in range(TB):
                        xt = xres[:, bass.ds(b * TB + t, 1), :].rearrange("p a d -> p (a d)")
                        last = stt(xt, yrows[par][:, t * K + k, :],
                                   gate_tab[n][:, bass.ds(b * TB + t, 1), k:k + 1].rearrange("p a k -> p (a k)"),
                                   xt, ALU.mult, ALU.add)
                    if k < K - 1:
                        link(last)
                return last

            dve.wait_ge(sc_["vpad_cleared"], 1)
            rows(0, sc_["row_u_ready"], 0, 0)

            def mask_scores(c, u):
                dve.wait_ge(sc_["score_full"], c * H + u + 1)
                wait(dve, sc_["pv_done"], c * H + u - 3)
                tt(probs[:, u % 4, 0:S].rearrange("p (t n) -> p t n", n=P),
                   SC[:, u % 2, :].rearrange("p (t n) -> p t n", n=P),
                   keep_k[:, :].unsqueeze(1).to_broadcast([P, TB, P]), ALU.mult).then_inc(sc_["probs_ready"], 1)

            def c_body(it, par, s1, s2, s3):
                b, c, d = it, it - 1, it - 2
                if s1:
                    wait(dve, rows_gathered[1 - par], (b + par) * (GATHER // 2))
                    rows(0, sc_["row_u_ready"], b + 1, 1 - par)
                    dve.wait_ge(rows_gathered[par], (b - par + 2) * (GATHER // 2))
                    link(add_rows(0, b, par))
                    statistics(b * TB).then_inc(sc_["var_ready"], 1)
                    dve.wait_ge(sc_["pow_ready"], b + 1)
                    link(refine(rpow[:, :], rvar[:, :], rnwt[:, :]))
                    wait(dve, sc_["xt_full"], b)
                    normalise(xn, b * TB, lambda t: rst2[:, t, 0:1], lambda t: rpow[:, t:t + 1]) \
                        .then_inc(sc_["xn_ready"], 1)
                for u in range(H):
                    if s2:
                        mask_scores(c, u)
                    if s1 and u == C_Q:
                        dve.wait_ge(sc_["proj_full"], b * 3 + 2)
                        dve.wait_ge(sc_["nexp_ready"], b + 1)
                        wait(dve, sc_["pv_done"], (b - 1) * H)
                        stt(qs[par], X, bq_s[:, 0:1], nexp[:, :], ALU.add, ALU.mult).then_inc(sc_["q_ready"], 1)
                    if s1 and u == C_KV:
                        dve.wait_ge(sc_["kv_full"], b + 1)
                        wait(dve, sc_["vpad_ready"], b * 2)
                        wait(dve, sc_["state_full"], b * 3)
                        for j in range(2):
                            last = tt(kvn[:, 2 * j:2 * j + 2, :], SC[:, 2 + j, :].rearrange("p (t n) -> p t n", t=2),
                                      bkv_s[:, :].unsqueeze(1).to_broadcast([P, 2, 2 * P]), ALU.add)
                        last.then_inc(sc_["kvn_ready"], 1)
                    if s1 and C_ST <= u < C_ST + TB - 1:
                        j = u - C_ST
                        dve.wait_ge(sc_["state_full"], b * 3 + j + 1)
                        tt(stm[par][:, j, :], MX[:, 0, 0:P], same_head[:, :], ALU.mult).then_inc(sc_["state_ready"], 1)
                    if s3 and u == C_WO:
                        dve.wait_ge(sc_["wo_full"], d + 1)
                        xt = xres[:, bass.ds(d * TB, TB), :]
                        ins = tt(xt, Xt, xt, ALU.add)
                        ins.then_inc(sc_["residual_ready"], 1)
                        dve.wait_ge(sc_["residual_ready"], d + 1)
                        link(tt(xt, xt, bo_s[:, :].unsqueeze(1).to_broadcast([P, TB, D]), ALU.add))
                        norm_2(rc, d)
                    if s3 and u == C_LG:
                        choose(rc, 1, d)
                    if s3 and u == C_POS:
                        place(rc, 1, d)

            over_batches(dve, c_body, link, 2 * 34)
            expert_phase(ed)

            rows(1, final_rows, 0, 0)

            def final(b, par, more):
                if more:
                    wait(dve, final_gathered[1 - par], (b + par) * (GATHER // 2))
                    rows(1, final_rows, b + 1, 1 - par)
                dve.wait_ge(final_gathered[par], (b - par + 2) * (GATHER // 2))
                add_rows(1, b, par).then_inc(final_ready, 1)

            final(0, 0, True)
            with dve.Fori(0, B // 2 - 1) as i:
                link.enter(i, 2 * (K - 1))
                final(i * 2 + 1, 1, True)
                final(i * 2 + 2, 0, True)
                link.leave(B // 2 - 1)
            final(B - 1, 1, False)

        @block.tensor
        def _(pe):
            mm = nc.tensor.matmul

            pe.wait_ge(consts_ready, 1)
            pe.wait_ge(w_dma, 4 * 16)
            for n in range(4):
                last = nc.tensor.transpose(Xt[:, n, :], w_in[:, n, :], ident[:, :])
            last.then_inc(wT_full, 1)
            pe.wait_ge(wT_copied, 1)
            pe.wait_ge(weights_ready, 1)

            def turn_tiles(src, ready, full, b):
                pe.wait_ge(ready, b + 1)
                for t in range(TB):
                    last = nc.tensor.transpose(Xt[:, t, :], src[:, t, :], ident[:, :])
                last.then_inc(full, 1)

            def project(s, w, b, n, j):
                mm(X, w, xnT[:, :], start=True, stop=True).then_inc(s["proj_full"], 1)

            def tile_products(w, srcT, width):
                for t in range(TB):
                    last = mm(X[:, t * width:(t + 1) * width], srcT[:, t * P:(t + 1) * P], w, start=True, stop=True)
                return last

            def out_projection(s, w, d):
                tile_products(w, attnT, D).then_inc(s["wo_full"], 1)

            def positions(r, d):
                pe.wait_ge(r["chosen_ready"], d + 1)
                for t in range(TB):
                    o = X[:, t * E:(t + 1) * E]
                    mm(o, ones_b[:, :], count[:, :], start=True, stop=False)
                    for j in range(t):
                        mm(o, ones_b[:, :], chosen[:, j, :], start=False, stop=False)
                    last = mm(o, before[:, :], chosen[:, t, :], start=False, stop=True)
                last.then_inc(r["pos_full"], 1)

            def scores(dst, left, right, par, pair, segments, rows_, mask, query_major):
                for n, (h, i, at, cols) in enumerate(segments):
                    p0, col = place_of(2 * pair + h)
                    lhs = left[p0:p0 + rows_, col, P * i:P * (i + 1)]
                    rhs = right[p0:p0 + rows_, col, 0:cols] if query_major else right[p0:p0 + rows_, col, P * i:S]
                    mm(dst[:, at:at + cols], lhs, rhs, start=(n == 0), stop=False, skip_group_check=True)
                diag = [at + cols - P if query_major else at for _, _, at, cols in segments]
                if len(diag) == 1:
                    return mm(dst[:, diag[0]:diag[0] + P], ident_b[:, :], mask[:, 0, :], start=False, stop=True,
                              skip_group_check=True)
                step = diag[1] - diag[0]
                for n, a in enumerate(diag):
                    last = mm(dst[:, a:a + P], ident_b[:, :], mask[:, 0, :], start=False, stop=(n == 1),
                              skip_group_check=True)
                return last

            def a_body(it, par, s1, s2, s3):
                b, c, d = it, it - 1, it - 2

                def products(u):
                    g = u // (UNITS // 2)
                    pe.wait_ge(sa["probs_ready"], c * UNITS + u + 1)
                    if u % (UNITS // 2) == 0:
                        pe.wait_ge(sa["vpad_ready"], c * 2 + g + 1)
                        wait(pe, sa["o_copied"], c * 2 + g)
                    for a in range(2):
                        k = 2 * u + a
                        for n, (h, i, at, cols) in enumerate(KEY_BANKS[k % 5]):
                            last = mm(O[:, P * i:S], vpad[:, i, 2 * (k // 5) + h, :],
                                      probs[:, u % 4, 512 * a + at:512 * a + at + cols],
                                      start=(k % 20 == 0), stop=(k % 20 == 19 and n == 1))
                    last.then_inc(sa["pv_done"], 1)

                for u in range(UNITS):
                    if s2:
                        wait(pe, sa["probs_ready"], c * UNITS + u - 1)
                        if u == 0 or u == UNITS // 2:
                            pe.wait_ge(sa["mrows_loaded"], (c * 2 + (u > 0) + 1) * MROW_DMAS * 16)
                        for a in range(2):
                            k = 2 * u + a
                            last = scores(SC[:, 2 * (u % 2) + a, :], kstk[1 - par], qstk[1 - par], par, k // 5,
                                          KEY_BANKS[k % 5], KM, mask_k, False)
                        last.then_inc(sa["score_full"], 1)
                    if s1 and u == A_XT:
                        wait(pe, sa["mparts_ready"], b * 2)
                        turn_tiles(xn, sa["xn_ready"], sa["xt_full"], b)
                    if s1 and A_Q <= u <= A_KR:
                        if u == A_Q:
                            pe.wait_ge(sa["xnT_ready"], b + 1)
                        else:
                            pe.wait_ge(sa["rope_ready"], b * 4 + u - A_Q)
                        project(sa, wT[:, u - A_Q, :], b, 4, u - A_Q)
                    if s1 and u == A_V:
                        pe.wait_ge(sa["rope_ready"], b * 4 + 4)
                        tile_products(wT[:, 4, :], xnT, P).then_inc(sa["proj_full"], 1)
                    if s3 and u == A_WO:
                        if s1:
                            pe.wait_ge(sa["v_ready"], b + 1)
                        else:
                            pe.wait_ge(sa["mparts_ready"], B * 2)
                            pe.wait_ge(ra["pos_read"], d)
                        pe.wait_ge(sa["attn_ready"], d * 2 + 2)
                        out_projection(sa, wT[:, 5, :], d)
                    if s3 and u == A_XT2:
                        pe.wait_ge(sa["residual_ready"], d + 1)
                        turn_tiles(xn2, ra["xn2_ready"], ra["xt2_full"], d)
                    if s3 and u == A_LG:
                        pe.wait_ge(ra["xn2T_ready"], d + 1)
                        tile_products(gate_ws[:, :], xn2T, E).then_inc(ra["logit_full"], 1)
                    if s3 and u == A_POS:
                        positions(ra, d)
                    if s1 and u >= A_MAX:
                        if u == A_MAX:
                            pe.wait_ge(sa["stack_loaded"], (b + 1) * STACK_DMAS * 16)
                        for k in range(4 * (u - A_MAX), 4 * (u - A_MAX) + 4):
                            wait(pe, sa["max_done"], b * BANKS + k - 1)
                            scores(MX[:, k % 2, :], qstk[par], kstk[par], par, k // 5, QUERY_BANKS[k % 5], KR,
                                   mask_q, True).then_inc(sa["max_full"], 1)
                    if s1 and u == A_MT:
                        if s3:
                            pe.wait_ge(ra["pos_read"], d + 1)
                        else:
                            pe.wait_ge(sa["v_ready"], b + 1)
                        turn_maxima(b, 0)
                    if s2 and u:
                        products(u - 1)
                if s2:
                    products(UNITS - 1)
                if s1:
                    pe.wait_ge(sa["mparts_ready"], b * 2 + 1)
                    turn_maxima(b, 1)

            def turn_maxima(b, half):
                pe.wait_ge(sa["negm_ready"], b * 2 + half + 1)
                for q in range(TB):
                    last = nc.tensor.transpose(X[0:HG, q * P:(q + 1) * P], negm[:, half, q, :], ident[:, :])
                last.then_inc(sa["mt_full"], 1)

            over_batches(pe, a_body)

            def expert_phase(e):
                def turn(p, r, par, t, h, y):
                    if t:
                        pe.wait_ge(e["landed"][r], (p - r) * (PAIR_DMAS * 16 // RING) + PAIR_DMAS * 16)
                        wait(pe, e["xbt_ready"], p - 1)
                        nc.tensor.transpose(bank[:, par, 0:P], xb_s[:, r, :], ident[:, :]).then_inc(e["xbt_full"], 1)
                    if h:
                        q, rq, bq_ = p - 1, (r - 1) % RING, 1 - par
                        pe.wait_ge(e["xbt_ready"], p)
                        wait(pe, e["hpre_ready"], p - 2)
                        for t_ in range(2):
                            for c in range(HC):
                                at = (t_ * HC + c) * CAP
                                last = mm(bank[:, 2 + bq_, at:at + CAP], w1_s[:, rq, t_, c:HID:HC],
                                          xbT[:, bq_, CAP * t_:CAP * (t_ + 1)], start=True, stop=True)
                        last.then_inc(e["h_full"], 1)
                    if y:
                        rq = (r - 2) % RING
                        pe.wait_ge(e["h_ready"], p - 1)
                        wait(pe, e["y_ready"], p - 3)
                        for t_ in range(2):
                            for c in range(HC):
                                last = mm(bank[CAP * t_:CAP * (t_ + 1), 4 + par, 0:D], hact[:, par, t_, c, :],
                                          w2_s[:, rq, t_, c, :], start=(c == 0), stop=(c == HC - 1))
                        last.then_inc(e["y_full"], 1)
                over_pairs(pe, turn)

            expert_phase(eb)

            def c_body(it, par, s1, s2, s3):
                b, c, d = it, it - 1, it - 2

                def products(u):
                    pe.wait_ge(sc_["probs_ready"], c * H + u + 1)
                    if u == 0:
                        wait(pe, sc_["o_copied"], c)
                    if u % HG == 0:
                        pe.wait_ge(sc_["vpad_ready"], c * 2 + u // HG + 1)
                    for t in range(TB):
                        last = mm(O[:, t * P:(t + 1) * P], vpad[:, t, u, :], probs[:, u % 4, t * P:(t + 1) * P],
                                  start=(u == 0 and t == 0), stop=False, skip_group_check=True)
                    if u == H - 1:
                        pe.wait_ge(sc_["state_ready"], (c + 1) * (TB - 1))
                        for t in range(1, TB):
                            last = mm(O[:, t * P:(t + 1) * P], stm[1 - par][:, t - 1, :],
                                      qs[1 - par][:, t * P:(t + 1) * P], start=False, stop=(t == TB - 1),
                                      skip_group_check=True)
                    last.then_inc(sc_["pv_done"], 1)

                def x_read():
                    wait(pe, sc_["k_ready"], b if s1 else B)
                    if not isinstance(d, int) or d > 0:
                        wait(pe, rc["pos_read"], d)

                for u in range(H):
                    if s2:
                        if u == 0:
                            pe.wait_ge(sc_["stack_loaded"], (c + 1) * STACK_DMAS * 16)
                        wait(pe, sc_["probs_ready"], c * H + u - 1)
                        p0, col = place_of(u)
                        for t in range(TB):
                            last = mm(SC[:, u % 2, t * P:(t + 1) * P],
                                      kstk[1 - par][p0:p0 + KR, col, t * P:(t + 1) * P],
                                      qstk[1 - par][p0:p0 + KR, col, t * P:(t + 1) * P], start=True, stop=True)
                        last.then_inc(sc_["score_full"], 1)
                    if s1 and u == C_XT:
                        x_read()
                        turn_tiles(xn, sc_["xn_ready"], sc_["xt_full"], b)
                    if s1 and u == C_N:
                        pe.wait_ge(sc_["xnT_ready"], b + 1)
                        project(sc_, wn_s[:, :], b, 3, 0)
                    if s1 and u == C_Q:
                        pe.wait_ge(sc_["nexp_ready"], b + 1)
                        project(sc_, wq2_s[:, :], b, 3, 1)
                    if s1 and u == C_K:
                        pe.wait_ge(sc_["q_ready"], b + 1)
                        project(sc_, wkv_s[:, 0:P], b, 3, 2)
                    if s1 and u == C_KV:
                        wait(pe, sc_["kvn_ready"], b)
                        for t in range(TB):
                            last = mm(SC[:, 2 + t // 2, (t % 2) * 256:(t % 2) * 256 + 256], xnT[:, t * P:(t + 1) * P],
                                      wkv_s[:, :], start=True, stop=True)
                        last.then_inc(sc_["kv_full"], 1)
                    if s1 and C_ST <= u < C_ST + TB - 1:
                        j = u - C_ST
                        pe.wait_ge(sc_["kvn_ready"], b + 1)
                        wait(pe, sc_["state_ready"], b * 3 + j)
                        mm(MX[:, 0, 0:P], kvn[:, j, 0:P], kvn[:, j, P:2 * P], start=(j == 0), stop=True,
                           skip_group_check=True).then_inc(sc_["state_full"], 1)
                    if s3 and u == C_WO:
                        if s1:
                            pe.wait_ge(sc_["k_ready"], b + 1)
                        else:
                            x_read()
                        pe.wait_ge(sc_["o_copied"], d + 1)
                        out_projection(sc_, wo2_s[:, :], d)
                    if s3 and u == C_XT2:
                        pe.wait_ge(sc_["residual_ready"], d + 1)
                        turn_tiles(xn2, rc["xn2_ready"], rc["xt2_full"], d)
                    if s3 and u == C_LG:
                        pe.wait_ge(rc["xn2T_ready"], d + 1)
                        tile_products(gate_ws[:, :], xn2T, E).then_inc(rc["logit_full"], 1)
                    if s3 and u == C_POS:
                        positions(rc, d)
                    if s2 and u:
                        products(u - 1)
                if s2:
                    products(H - 1)

            over_batches(pe, c_body)
            expert_phase(ed)


_INS = ["L0_attn_a_x", "L0_attn_a_Wq", "L0_attn_a_Wk", "L0_attn_a_Wv", "L0_attn_a_Wo", "L0_attn_b_Wqk",
        "L0_attn_b_bqk", "L0_attn_b_Wv", "L0_attn_b_bv", "L0_attn_b_Wn", "L0_attn_b_bn", "L0_attn_b_Wo",
        "L0_attn_b_bo", "L0_ffn_gate_w", "L0_ffn_gate_b", "L0_ffn_w1", "L0_ffn_b1", "L0_ffn_w2", "L0_ffn_b2"]


def rotary_tables():
    import numpy as np
    inv = (1.0 / np.float32(10000.0) ** (np.arange(0, DH, 2, dtype=np.float32) / np.float32(DH))).astype(np.float32)
    f = np.outer(np.arange(S, dtype=np.float32), inv).astype(np.float32)
    cos, sin = np.cos(f).T, np.sin(f).T
    return (np.ascontiguousarray(np.tile(np.concatenate([cos, cos]), (H, 1)), dtype=np.float32),
            np.ascontiguousarray(np.tile(np.concatenate([-sin, sin]), (H, 1)), dtype=np.float32))


def kernel(**inputs):
    import numpy as np
    import concourse.bacc as bacc
    from concourse.bass_utils import run_bass_kernel_spmd

    nc = bacc.Bacc("TRN2", target_bir_lowering=False, num_devices=1)
    arrays = {name: np.ascontiguousarray(inputs[name]) for name in _INS}
    arrays["cosT"], arrays["sinT"] = rotary_tables()
    args = [nc.dram_tensor(name, a.shape, mybir.dt.from_np(a.dtype), kind="ExternalInput").ap()
            for name, a in arrays.items()]
    args.append(nc.dram_tensor("out", (B, S, D), F32, kind="ExternalOutput").ap())
    build(nc, *args)
    return run_bass_kernel_spmd(nc, [arrays], core_ids=[0]).results[0]["out"]
```

```python
from contextlib import ExitStack

import concourse.bass as bass
from concourse import mybir

F32 = mybir.dt.float32
BF16 = mybir.dt.bfloat16
U32 = mybir.dt.uint32
ALU = mybir.AluOpType
ACT = mybir.ActivationFunctionType
AX = mybir.AxisListType

P = 128
B, S, D = 8, 512, 128
H, DH = 16, 8
TB = S // P
NT = B * TB
E, HID, CAP, K = 64, 512, 64, 3
HC = HID // P
PAIRS = E // 2
RING = 8
BLOCK = 4
EPS = 1e-5
SCALE = 1.0 / DH ** 0.5
NEG = -1e30
NPARTS = 3
Q_ROWS = (0, 0, 1, 1, 0, 2)
K_ROWS = (0, 1, 0, 1, 2, 0)
KR = len(Q_ROWS) * DH
KM = KR + 2
UNITS = 20
BANKS = 40
HG = 8
QG = 4
GROUPS = H // QG
OUT_OF_RANGE = 8192.0

KEY_BANKS = ([[(h, 0, 0, 512)] for h in range(QG)] + [[(h, 1, 0, 384), (h, 3, 384, 128)] for h in range(QG)]
             + [[(h, 2, 0, 256), (h + 1, 2, 256, 256)] for h in (0, 2)])
QUERY_BANKS = [[(0, 3, 0, 512)], [(0, 0, 0, 128), (0, 2, 128, 384)], [(1, 3, 0, 512)],
               [(1, 0, 0, 128), (1, 2, 128, 384)], [(0, 1, 0, 256), (1, 1, 256, 256)]]
GROUP_UNITS = UNITS // GROUPS
PV_STEPS = ((1, (0,)), (3, (1, 3)), (4, (2,)))
PV_OF_UNIT = (1, 1, 2, 2, 3)


def key_place(h, i):
    for k, bank_ in enumerate(KEY_BANKS):
        for hh, ii, at, cols in bank_:
            if (hh, ii) == (h, i):
                return k // 2, k % 2, at


A_ORDER = (("den", 0, 3), ("mt1", 1, 2), ("xt", 2, 0), ("q", 3, 0), ("qr", 4, 0), ("out", 5, 3), ("wo", 6, 3),
           ("k", 7, 0), ("kr", 8, 0), ("v", 9, 0), ("xt2", 10, 3), ("mt0", 12, 1), ("lg", 13, 3), ("pos", 16, 3))
C_ORDER = (("ctx", 0, 2), ("xt", 1, 0), ("wo", 2, 2), ("n", 3, 0), ("q", 4, 0), ("k", 5, 0), ("xt2", 7, 2),
           ("lg", 9, 2), ("pos", 12, 2))
C_KV, C_ST = 6, 7


class Chain:

    def __init__(self, eng, sem):
        self.eng, self.sem, self.base, self.k = eng, sem, 0, 0

    def __call__(self, ins):
        self.k += 1
        ins.then_inc(self.sem, 1)
        self.eng.wait_ge(self.sem, self.base + self.k)

    def mark(self, ins):
        self.k += 1
        ins.then_inc(self.sem, 1)

    def settle(self):
        self.eng.wait_ge(self.sem, self.base + self.k)

    def enter(self, i, per):
        self.start = self.base + self.k
        self.base, self.k, self.per = i * per + self.start, 0, per

    def leave(self, turns):
        assert self.k == self.per, (self.sem, self.k, self.per)
        self.base, self.k = self.start + turns * self.per, 0


def place_of(h):
    return 64 * (h // HG), h % HG


def wait(eng, sem, count):
    if not isinstance(count, int) or count > 0:
        eng.wait_ge(sem, count)


def over_batches(eng, stages, body, chain=None, per=0):
    first = stages + stages % 2
    turns = (B - first) // 2

    def plain(it):
        body(it, it % 2, [0 <= it - s < B for s in range(stages)])

    for it in range(first):
        plain(it)
    with eng.Fori(0, turns) as i:
        if chain:
            chain.enter(i, per)
        body(i * 2 + first, 0, [True] * stages)
        body(i * 2 + (first + 1), 1, [True] * stages)
        if chain:
            chain.leave(turns)
    for it in range(first + 2 * turns, B + stages - 1):
        plain(it)


def step_before(order, it, on, name):
    n = [o[0] for o in order].index(name)
    for m in range(n - 1, -1, -1):
        if on[order[m][2]]:
            return order[m], it
    for o in reversed(order):
        if not isinstance(it, int) or 0 <= it - 1 - o[2] < B:
            return o, it - 1
    return None


def over_pairs(eng, turn):
    for p in range(4):
        turn(p, p % RING, p % 2, True, p >= 1, p >= 2)
    turns = (PAIRS - 4) // RING
    with eng.Fori(0, turns) as i:
        for j in range(RING):
            turn(i * RING + (4 + j), (4 + j) % RING, j % 2, True, True, True)
    for p in range(4 + turns * RING, PAIRS + 2):
        turn(p, p % RING, p % 2, p < PAIRS, p <= PAIRS, True)


def flat(ap):
    return ap.rearrange("p a n -> p (a n)")


def build(nc, x, Wq, Wk, Wv, Wo, Wqk, bqk, bWv, bv, Wn, bn, bWo, bo, gate_w, gate_b, w1, b1, w2, b2,
          cosT, sinT, out):
    ctx = ExitStack()
    with ctx:
        def sb(name, shape, dt=F32):
            return ctx.enter_context(nc.sbuf_tensor(name, shape, dt))

        def sem(name):
            return ctx.enter_context(nc.semaphore(name))

        parts_d = [[nc.dram_tensor(f"parts_{n}{par}", (NPARTS, P, S), BF16, kind="Internal").ap() for n in "qk"]
                   for par in range(2)]
        bucket_d = nc.dram_tensor("bucket", (E * CAP, D), F32, kind="Internal").ap()
        y_d = [nc.dram_tensor(f"expert_out_{n}", (E * CAP, D), F32, kind="Internal").ap() for n in range(2)]

        ident = sb("ident", [P, P])
        ident_b = sb("ident_b", [P, P], BF16)
        mask_q = sb("mask_q", [P, P], BF16)
        mask_k = sb("mask_k", [P, P], BF16)
        keep_k = sb("keep_k", [P, P])
        same_head = sb("same_head", [P, P])
        before = sb("before", [P, P], BF16)
        ones_b = sb("ones_b", [P, P], BF16)
        expert_no = sb("expert_no", [P, E])
        minus_half = sb("minus_half", [P, NT])
        zero1 = sb("zero1", [P, 1])
        pool_scratch, dve_scratch = sb("pool_scratch", [P, 96], BF16), sb("dve_scratch", [P, 96], BF16)
        pool_columns, dve_columns = iter(range(96)), iter(range(96))
        cossin = sb("cossin", [P, 2, S])
        wT = sb("wT", [P, 6, P])
        wq2_s = sb("wq2_s", [P, P])
        wkv_s = sb("wkv_s", [P, 2 * P])
        wn_s = sb("wn_s", [P, P])
        wo2_s = sb("wo2_s", [P, P])
        wn_in = sb("wn_in", [P, H])
        bq_s = sb("bq_s", [P, 2])
        bn_s = sb("bn_s", [P, 2])
        bkv_s = sb("bkv_s", [P, 2 * P])
        bo_s = sb("bo_s", [P, P])
        gate_ws = sb("gate_ws", [P, E])
        gate_bs = sb("gate_bs", [P, E])
        b1_s = sb("b1_s", [P, E, HC])

        xres = sb("xres", [P, NT, D])
        stat1 = sb("stat1", [P, NT, 2])
        rstd1 = sb("rstd1", [P, NT])
        bn6 = sb("bn6", [P, NT, 6])
        var1 = sb("var1", [P, NT])
        nwt1 = sb("nwt1", [P, NT])
        count = sb("count", [P, E], BF16)
        gate_tab = [sb(f"gate_tab{n}", [P, NT, K]) for n in range(2)]
        row_tab = [sb(f"row_tab{n}", [P, NT + TB, K], U32) for n in range(2)]

        vext = [sb(f"vext{n}", [P, TB, H, 32]) for n in range(2)]
        qstk = [sb(f"qstk{n}", [P, H // 2, S], BF16) for n in range(2)]
        kstk = [sb(f"kstk{n}", [P, H // 2, S], BF16) for n in range(2)]
        probs = sb("probs", [P, GROUP_UNITS, 2 * 512])
        xn = sb("xn", [P, TB, D])
        w_in = xn
        xnT = sb("xnT", [P, S])
        rope = [sb(f"rope_{n}", [P, 2, S]) for n in "qk"]
        parts = [sb(f"parts_{n}s", [P, NPARTS, S], BF16) for n in "qk"]
        v_s = sb("v_s", [P, TB, P])
        sel_o = sb("sel_o", [P, 32])
        sel_d = sb("sel_d", [P, 32])
        bmax = sb("bmax", [P, BANKS * 4])
        negm = sb("negm", [P, 2, TB, HG])
        mbuf = sb("mbuf", [P, S])
        mparts = mbuf[0:HG, :].bitcast(BF16).rearrange("p (a s) -> p a s", a=2)
        o_s = sb("o_s", [P, GROUPS, S])
        den_s = sb("den_s", [P, S])
        rden = sb("rden", [P, S])
        attnT = sb("attnT", [P, S])
        qs = [rope[0][:, 0, :], sb("qs1", [P, S])[:, :]]
        kn = cossin[:, 0, :].rearrange("p (t n) -> p t n", n=P)
        stm = [v_s[:, 0:TB - 1, :], mbuf[:, :].rearrange("p (t n) -> p t n", n=P)[:, 0:TB - 1, :]]
        nexp = rden

        xn2 = sb("xn2", [P, TB, D])
        xn2T = sb("xn2T", [P, S])
        rst6 = sb("rst6", [P, TB, 6])
        rst2 = sb("rst2", [P, TB, 2])
        rvar = sb("rvar", [P, TB])
        rpow = sb("rpow", [P, TB])
        rnwt = sb("rnwt", [P, TB])
        logit = sb("logit", [P, TB, E])
        top8 = sb("top8", [P, TB, 8])
        idx8 = sb("idx8", [P, TB, 8], U32)
        topi = sb("topi", [P, TB, K])
        topd = sb("topd", [P, TB, K])
        tope = sb("tope", [P, TB, K])
        esum = sb("esum", [P, TB])
        onehot = sb("onehot", [P, K, TB, E], BF16)
        chosen = sb("chosen", [P, TB, E], BF16)
        csum = sb("csum", [P, E])
        ptmp = sb("ptmp", [P, K, TB, E])
        pos = sb("pos", [P, TB, K])
        room = sb("room", [P, TB, K])
        slot = sb("slot", [P, TB, K])
        slot_u = sb("slot_u", [P, TB * K], U32)
        row_u = [sb(f"row_u{n}", [P, TB * K], U32) for n in range(2)]
        yrows = [sb(f"yrows{n}", [P, TB * K, D]) for n in range(2)]

        w1_own = sb("w1_own", [P, RING // 2, 2, HID])
        w2_own = sb("w2_own", [P, RING // 2, 2, HC, D])
        lent = [t[:, :, :].rearrange("p a s -> p (a s)").bitcast(F32) for t in (*qstk, *kstk)]
        w1_s = [w1_own[:, r, :, :] for r in range(RING // 2)] + [
            t[:, 0:2 * HID].rearrange("p (a n) -> p a n", a=2) for t in lent]
        w2_s = [w2_own[:, r, :, :, :] for r in range(RING // 2)] + [
            t[:, 2 * HID:4 * HID].rearrange("p (a c n) -> p a c n", a=2, c=HC) for t in lent]
        xb_s = sb("xb_s", [P, RING, D])
        xbT = sb("xbT", [P, 2, P])
        b2_s = sb("b2_s", [P, RING, D])
        hpre = probs[:, 0:1, :].rearrange("p b (q a c n) -> p (b q) a c n", q=2, a=2, c=HC)
        hact = probs[:, 1:2, :].rearrange("p b (q a c n) -> p (b q) a c n", q=2, a=2, c=HC)
        y_s = probs[:, 2, 0:2 * D].rearrange("p (q d) -> p q d", q=2)

        bank = ctx.enter_context(nc.psum_tensor("bank", [P, 8, 512], F32))
        SC = bank[:, 0:4, :]
        MX = bank[:, 4:6, :]
        O = bank[:, 6, :]
        X = bank[:, 7, :]
        Xt = X.rearrange("p (t n) -> p t n", t=TB)

        consts_dma, x_dma, w_dma, bias_dma, zero_dma = map(sem, ("consts_dma", "x_dma", "w_dma", "bias_dma", "zero_dma"))
        consts_ready, zeros_ready = sem("consts_ready"), sem("zeros_ready")
        wT_full, wT_copied, weights_ready = sem("wT_full"), sem("wT_copied"), sem("weights_ready")
        var1_ready, pow1_ready, ln1_ready = sem("var1_ready"), sem("pow1_ready"), sem("ln1_ready")
        dve_chain, pool_chain = sem("dve_chain"), sem("pool_chain")

        def sems(n, *names):
            return {s: sem(f"{s}_{n}") for s in names}

        both = ("xn_ready", "xt_full", "xnT_ready", "proj_full", "split_ready", "parts_written",
                "vpad_ready", "score_full", "probs_ready", "pv_done", "o_copied", "wo_full", "residual_ready")
        sa = sems("a", *both, "rope_ready", "v_ready", "max_full", "max_done", "negm_ready", "mt_full", "high_ready",
                  "mparts_ready", "mrows_loaded", "den_full", "den_read", "recip_ready", "out_full", "attn_ready")
        sc_ = sems("c", *both, "nexp_ready", "q_ready", "k_ready", "high_ready", "kv_full", "kvn_ready", "state_full",
                   "state_ready", "row_u_ready", "vext_cleared", "var_ready", "pow_ready", "ctx_full", "ctx_ready")
        for s_, n in ((sa, "a"), (sc_, "c")):
            s_["stack_loaded"] = [sem(f"stack_loaded_{n}_{t}") for t in range(2)]
        sc_["stack_loaded"][1] = sc_["stack_loaded"][0]
        def routing_sems(n):
            return {s: sem(f"{s}_{n}") for s in (
                "rvar_ready", "rpow_ready", "xn2_ready", "xt2_full", "xn2T_ready", "logit_full",
                "topd_ready", "tope_ready", "chosen_ready", "pos_full", "pos_read", "slot_ready",
                "scattered")}

        def expert_sems(n):
            return {s: sem(f"{s}_{n}") for s in (
                "xbt_full", "xbt_ready", "h_full", "hpre_ready", "h_ready", "y_full", "y_ready")} | {
                "y_stored": [sem(f"y_stored_{n}_{j}") for j in range(2)],
                "landed": [sem(f"landed_{n}_{r}") for r in range(RING)],
                "block_landed": [sem(f"block_landed_{n}_{z}") for z in range(RING // BLOCK)]}

        ra, rc, eb, ed = routing_sems("a"), routing_sems("c"), expert_sems("b"), expert_sems("d")
        final_rows, final_ready, out_stored = map(sem, ("final_rows", "final_ready", "out_stored"))
        rows_gathered, final_gathered = ([sem(f"{s}_{j}") for j in range(2)] for s in ("rows_gathered", "final_gathered"))
        GATHER = TB * K * 16

        x_v = x.rearrange("b (t p) d -> p (b t) d", p=P)
        out_v = out.rearrange("b (t p) d -> p (b t) d", p=P)
        w1_v = w1.rearrange("e d h -> d e h")
        w2_v = w2.rearrange("e (p c) d -> p e c d", c=HC)
        b2_v = b2.rearrange("(q t) d -> t q d", t=2)
        bucket_v = bucket_d.rearrange("(q p) d -> p q d", p=P)

        A_READERS = {"den": (sa["den_read"], 1, 1), "mt1": (sa["mparts_ready"], 2, 2), "xt": (sa["xnT_ready"], 1, 1),
                     "q": (sa["rope_ready"], 4, 1), "qr": (sa["rope_ready"], 4, 2), "out": (sa["attn_ready"], 1, 1),
                     "wo": (sa["residual_ready"], 1, 1), "k": (sa["rope_ready"], 4, 3), "kr": (sa["rope_ready"], 4, 4),
                     "v": (sa["v_ready"], 1, 1), "xt2": (ra["xn2T_ready"], 1, 1), "mt0": (sa["mparts_ready"], 2, 1),
                     "lg": (ra["chosen_ready"], 1, 1), "pos": (ra["pos_read"], 1, 1)}
        C_READERS = {"ctx": (sc_["ctx_ready"], 1, 1), "xt": (sc_["xnT_ready"], 1, 1), "wo": (sc_["residual_ready"], 1, 1),
                     "n": (sc_["nexp_ready"], 1, 1), "q": (sc_["q_ready"], 1, 1), "k": (sc_["k_ready"], 1, 1),
                     "xt2": (rc["xn2T_ready"], 1, 1), "lg": (rc["chosen_ready"], 1, 1), "pos": (rc["pos_read"], 1, 1)}
        PAIR_DMAS = 2
        BLOCK_DMAS = 3
        MROW_DMAS = 2 * HG
        STACK_DMAS = 2 * len(Q_ROWS)
        BIAS_DMAS = 2 + DH + 4 + 1
        ZERO_DMAS = E * CAP * D // P // 1024

        def masked(u):
            n = u % (2 * QG)
            return probs[:, n // 2, 512 * (n % 2):512 * (n % 2) + 512]

        block = ctx.enter_context(nc.Block())

        @block.sync
        def _(sp):
            for dst, src in ((w_in[:, 0, :], Wq), (w_in[:, 1, :], Wk), (w_in[:, 2, :], Wv), (w_in[:, 3, :], Wo)):
                sp.dma_start(dst, src).then_inc(w_dma, 16)
            sp.dma_start(xres[:, :, :], x_v).then_inc(x_dma, 16)
            for dst, src in ((cossin[:, 0, :], cosT), (cossin[:, 1, :], sinT), (wq2_s[:, :], Wqk[:, 0:P]),
                             (wkv_s[:, 0:P], Wqk[:, P:2 * P]), (wkv_s[:, P:2 * P], bWv), (wo2_s[:, :], bWo),
                             (wn_in[:, :], Wn), (gate_ws[:, :], gate_w)):
                sp.dma_start(dst, src).then_inc(consts_dma, 16)
            for t in range(2):
                sp.dma_start(bq_s[:, t:t + 1], bqk[t * P:(t + 1) * P].rearrange("(p o) -> p o", o=1)).then_inc(bias_dma, 16)
            for j in range(DH):
                sp.dma_start(bn_s[j:P:DH, 0:1], bn.rearrange("(h o) -> h o", o=1)).then_inc(bias_dma, 16)
            for dst, src in ((bkv_s[:, 0:P], bqk[P:2 * P]), (bkv_s[:, P:2 * P], bv), (bo_s[:, :], bo),
                             (gate_bs[:, :], gate_b)):
                sp.dma_start(dst, src.unsqueeze(0).to_broadcast([P, src.shape[0]])).then_inc(bias_dma, 16)
            sp.dma_start(b1_s[:, :, :], b1.rearrange("e (p c) -> p e c", c=HC)).then_inc(bias_dma, 16)
            sp.wait_ge(zeros_ready, 1)
            zero_rows = E * CAP // ZERO_DMAS
            for n in range(ZERO_DMAS):
                sp.dma_start(bucket_d[n * zero_rows:(n + 1) * zero_rows, :].rearrange("(p r) d -> p (r d)", p=P),
                             probs[:, 0, :]).then_inc(zero_dma, 16)

            def load_weights(e, q, r):
                sp.dma_start(w1_s[r], w1_v[:, bass.ds(q * 2, 2), :]).then_inc(e["landed"][r], 16)
                sp.dma_start(w2_s[r], w2_v[:, bass.ds(q * 2, 2), :, :]).then_inc(e["landed"][r], 16)

            def load_block(e, q, z):
                at = slice(z * BLOCK, (z + 1) * BLOCK)
                sp.dma_start(xb_s[:, at, :], bucket_v[:, bass.ds(q, BLOCK), :]).then_inc(e["block_landed"][z], 16)
                for t in range(2):
                    sp.dma_start(b2_s[CAP * t:CAP * (t + 1), at, :], b2_v[t][bass.ds(q, BLOCK), :].unsqueeze(0)
                                 .to_broadcast([CAP, BLOCK, D])).then_inc(e["block_landed"][z], 16)

            def store_y(e, q, r, yd):
                sp.wait_ge(e["y_ready"], q + 1)
                sp.dma_start(yd[bass.ds(q * P, P), :], y_s[:, r % 2, :]).then_inc(e["y_stored"][r % 2], 16)

            def write_parts(s, b, par, n):
                sp.wait_ge(s["split_ready"], b * 2 + n + 1)
                sp.dma_start(parts_d[par][n].rearrange("g p s -> p g s"), parts[n][:, :, :]).then_inc(s["parts_written"], 16)

            def load_stacks(s, par, t):
                for n, rows_ in enumerate((Q_ROWS, K_ROWS)):
                    src = parts_d[par][n].rearrange("g (t a d) s -> g t d a s", t=2, d=DH)
                    for g, part in enumerate(rows_):
                        at = 64 * t + DH * g
                        sp.dma_start((qstk, kstk)[n][par][at:at + DH, :, :], src[part, t]) \
                            .then_inc(s["stack_loaded"][t], 16)

            def maxima_rows(b, par, half, parts_of=None):
                sp.wait_ge(sa["mparts_ready"], b * 2 + half + 1)
                for j in range(HG):
                    for part in range(2):
                        if (j, part) == (HG - 1, 1) and parts_of is not None:
                            sp.wait_ge(sa["parts_written"], (parts_of + 1) * 32)
                        p0, col = place_of(HG * half + j)
                        sp.dma_start(qstk[par][p0 + KR + part:p0 + KR + part + 1, col, :],
                                     mparts[j:j + 1, part, :]).then_inc(sa["mrows_loaded"], 16)

            def a_body(it, par, on):
                a, b, c = it, it - 1, it - 2
                if on[1]:
                    wait(sp, sa["score_full"], (b - 1) * UNITS)
                    load_stacks(sa, 1 - par, 1)
                if on[2]:
                    maxima_rows(c, par, 1)
                if on[0]:
                    write_parts(sa, a, par, 0)
                    write_parts(sa, a, par, 1)
                if on[1]:
                    maxima_rows(b, 1 - par, 0, a if on[0] else None)
                elif on[0]:
                    sp.wait_ge(sa["parts_written"], (a + 1) * 32)
                if on[0]:
                    wait(sp, sa["score_full"], (a - 2) * UNITS + UNITS // 2)
                    load_stacks(sa, par, 0)

            def c_body(it, par, on):
                if not on[0]:
                    return
                write_parts(sc_, it, par, 0)
                write_parts(sc_, it, par, 1)
                sp.wait_ge(sc_["parts_written"], (it + 1) * 32)
                for t in range(2):
                    load_stacks(sc_, par, t)

            def expert_phase(e, attention, stacks_free, buckets_ready, yd):
                for q in range(RING // 2):
                    load_weights(e, q, q)
                attention()
                sp.wait_ge(*stacks_free)
                for q in range(RING // 2, RING):
                    load_weights(e, q, q)
                sp.wait_ge(*buckets_ready)
                for z in range(RING // BLOCK):
                    load_block(e, z * BLOCK, z)
                with sp.Fori(0, PAIRS // RING - 1) as i:
                    for r in range(RING):
                        q = i * RING + r
                        store_y(e, q, r, yd)
                        load_weights(e, q + RING, r)
                        if r % BLOCK == BLOCK - 1:
                            load_block(e, q + (RING - BLOCK + 1), r // BLOCK)
                for q in range(PAIRS - RING, PAIRS):
                    store_y(e, q, q % RING, yd)
                for j in range(2):
                    sp.wait_ge(e["y_stored"][j], PAIRS // 2 * 16)

            expert_phase(eb, lambda: over_batches(sp, 4, a_body), (sa["score_full"], B * UNITS),
                         (ra["scattered"], B * TB * K * 16), y_d[0])
            expert_phase(ed, lambda: over_batches(sp, 3, c_body), (sc_["score_full"], B * H),
                         (rc["scattered"], B * TB * K * 16), y_d[1])
            with sp.Fori(0, B) as b:
                sp.wait_ge(final_ready, b + 1)
                sp.dma_start(out_v[:, bass.ds(b * TB, TB), :], xres[:, bass.ds(b * TB, TB), :]).then_inc(out_stored, 16)
            sp.wait_ge(out_stored, B * 16)

        @block.gpsimd
        def _(pool):
            link = Chain(pool, pool_chain)

            def select(t, pattern, op, fill, base=0, cm=1):
                link(nc.gpsimd.affine_select(out=t, in_=t, pattern=pattern, compare_op=op, fill=fill, base=base,
                                             channel_multiplier=cm))

            nc.gpsimd.memset(probs[:, 0, :], 0.0).then_inc(zeros_ready, 1)
            for t in vext:
                nc.gpsimd.memset(t[:, :, :, :], 1.0)
            nc.gpsimd.memset(sel_o[:, :], 0.0)
            nc.gpsimd.memset(sel_d[:, :], 0.0)
            nc.gpsimd.memset(minus_half[:, :], -0.5)
            nc.gpsimd.memset(zero1[:, :], 0.0)
            nc.gpsimd.memset(row_tab[0][:, NT:NT + TB, :], 0)
            nc.gpsimd.memset(ident[:, :], 0.0)
            nc.gpsimd.memset(ident_b[:, :], 0.0)
            nc.gpsimd.memset(mask_q[:, :], 0.0)
            nc.gpsimd.memset(mask_k[:, :], 0.0)
            nc.gpsimd.memset(keep_k[:, :], 1.0)
            nc.gpsimd.memset(same_head[:, :], 1.0)
            nc.gpsimd.memset(before[:, :], 1.0)
            nc.gpsimd.memset(count[:, :], 0.0)
            nc.gpsimd.memset(kstk[0][:, :, :], 1.0)
            nc.gpsimd.memset(kstk[1][:, :, :], 1.0)
            nc.gpsimd.iota(expert_no[:, :], pattern=[[1, E]], base=0, channel_multiplier=0,
                           allow_small_or_imprecise_dtypes=True)
            link(nc.gpsimd.memset(ones_b[:, :], 1.0))
            select(ident[:, :], [[-1, P]], ALU.not_equal, 1.0)
            select(ident_b[:, :], [[-1, P]], ALU.not_equal, 1.0)
            select(mask_q[:, :], [[-1, P]], ALU.is_ge, NEG)
            select(mask_k[:, :], [[1, P]], ALU.is_ge, NEG, cm=-1)
            select(keep_k[:, :], [[1, P]], ALU.is_ge, 0.0, cm=-1)
            select(same_head[:, :].rearrange("p (h d) -> p h d", d=DH), [[-DH, H], [0, DH]], ALU.is_ge, 0.0)
            select(same_head[:, :].rearrange("p (h d) -> p h d", d=DH), [[DH, H], [0, DH]], ALU.is_ge, 0.0,
                   base=DH - 1, cm=-1)
            select(before[:, :], [[1, P]], ALU.is_gt, 0.0, cm=-1)
            for t, base in ((sel_o, 0), (sel_d, -DH)):
                select(t[:, :].rearrange("p (j d) -> p j d", d=DH), [[-32, QG], [-1, DH]], ALU.not_equal, 1.0, base=base)
            pool.wait_ge(zero_dma, ZERO_DMAS * 16)
            nc.gpsimd.memset(rnwt[:, :], 0.0).then_inc(consts_ready, 1)
            pool.wait_ge(var1_ready, 1)
            nc.gpsimd.tensor_tensor(rstd1[:, :], var1[:, :], minus_half[:, :], ALU.pow).then_inc(pow1_ready, 1)

            def split(n, s, b):
                high, src = parts[n][:, 0, :], rope[n][:, 0, :]
                wait(pool, s["parts_written"], b * 32)
                pool.wait_ge(s["rope_ready"], b * 4 + 2 * n + 2)
                nc.gpsimd.tensor_tensor(high, rope[n][:, 0, :], rope[n][:, 1, :], ALU.add)
                link(nc.gpsimd.tensor_tensor(src, rope[n][:, 0, :], rope[n][:, 1, :], ALU.add))
                split_rest(n, s, src)

            def split_rest(n, s, src):
                high, mid, low = (parts[n][:, j, :] for j in range(NPARTS))
                rest = rope[n][:, 1, :]
                nc.gpsimd.tensor_tensor(mid, src, high, ALU.subtract)
                link(nc.gpsimd.tensor_tensor(rest, src, high, ALU.subtract))
                nc.gpsimd.tensor_tensor(low, rest, mid, ALU.subtract).then_inc(s["split_ready"], 1)

            def fence():
                n = next(pool_columns)
                return nc.gpsimd.tensor_tensor(pool_scratch[:, n:n + 1], minus_half[:, 0:1], minus_half[:, 0:1], ALU.mult)

            def power(ready, done, b):
                pool.wait_ge(ready, b + 1)
                nc.gpsimd.tensor_tensor(rpow[:, :], rvar[:, :], minus_half[:, 0:TB], ALU.pow).then_inc(done, 1)

            def scatter(r, d):
                pool.wait_ge(r["slot_ready"], d + 1)
                fence()
                for t in range(TB):
                    for k in range(K):
                        j = t * K + k
                        nc.gpsimd.indirect_dma_start(
                            bucket_d[:, :], bass.IndirectOffsetOnAxis(ap=slot_u[:, j:j + 1], axis=0),
                            xn2[:, t, :], None, bounds_check=E * CAP - 1, oob_is_err=False).then_inc(r["scattered"], 16)

            def gather(src_d, ready, gathered, b, par):
                link.settle()
                pool.wait_ge(ready, b + 1)
                link.mark(fence())
                for j in range(TB * K):
                    nc.gpsimd.indirect_dma_start(
                        yrows[par][:, j, :], None, src_d[:, :],
                        bass.IndirectOffsetOnAxis(ap=row_u[par][:, j:j + 1], axis=0),
                        bounds_check=E * CAP - 1, oob_is_err=False).then_inc(gathered[par], 16)

            def a_body(it, par, on):
                a, b, d = it, it - 1, it - 3
                if on[1]:
                    pool.wait_ge(sa["v_ready"], b + 1)
                    wait(pool, sa["pv_done"], (b - 1) * len(PV_STEPS) * GROUPS)
                    fence()
                    nc.gpsimd.tensor_copy(vext[1 - par][:, :, :, 0:DH], v_s[:, :, :].rearrange("p t (h d) -> p t h d", d=DH)) \
                        .then_inc(sa["vpad_ready"], 1)
                if on[0]:
                    split(0, sa, a)
                if on[3]:
                    power(ra["rvar_ready"], ra["rpow_ready"], d)
                if on[0]:
                    split(1, sa, a)
                if on[3]:
                    scatter(ra, d)

            over_batches(pool, 4, a_body, link, 8)

            pool.wait_ge(sa["pv_done"], B * len(PV_STEPS) * GROUPS)
            nc.gpsimd.memset(count[:, :], 0.0)
            nc.gpsimd.memset(vext[0][:, :, :, :], 0.0)
            nc.gpsimd.memset(vext[1][:, :, :, :], 0.0).then_inc(sc_["vext_cleared"], 1)
            for j in range(2):
                pool.wait_ge(eb["y_stored"][j], PAIRS // 2 * 16)
            gather(y_d[0], sc_["row_u_ready"], rows_gathered, 0, 0)

            def c_body(it, par, on):
                b, d = it, it - 2
                if on[0]:
                    power(sc_["var_ready"], sc_["pow_ready"], b)
                if on[2]:
                    power(rc["rvar_ready"], rc["rpow_ready"], d)
                if on[0]:
                    gather(y_d[0], sc_["row_u_ready"], rows_gathered, b + 1, 1 - par)
                    for n, src in ((0, qs[par]), (1, rope[1][:, 0, :])):
                        pool.wait_ge(sc_["high_ready"], b * 2 + n + 1)
                        split_rest(n, sc_, src)
                if on[2]:
                    scatter(rc, d)

            over_batches(pool, 3, c_body, link, 6)
            pool.wait_ge(rows_gathered[0], (B // 2 + 1) * GATHER)
            for j in range(2):
                pool.wait_ge(ed["y_stored"][j], PAIRS // 2 * 16)
            with pool.Fori(0, B // 2) as i:
                link.enter(i, 2)
                for par in range(2):
                    gather(y_d[1], final_rows, final_gathered, i * 2 + par, par)
                link.leave(B // 2)

        @block.scalar
        def _(act):
            act.wait_ge(wT_full, 1)
            nc.scalar.activation(wT[:, 0, :], Xt[:, 0, :], ACT.Copy)
            nc.scalar.activation(wT[:, 2, :], Xt[:, 1, :], ACT.Copy)
            nc.scalar.activation(wT[:, 4:6, :], Xt[:, 2:4, :], ACT.Copy).then_inc(wT_copied, 1)

            def evacuate(dst, src, full, count_, done):
                act.wait_ge(full, count_)
                nc.scalar.activation(dst, src, ACT.Copy).then_inc(done, 1)

            def take_out(s, n, steps, g, reads):
                act.wait_ge(s["pv_done"], steps)
                wait(act, *reads)
                nc.scalar.activation(o_s[:, g, :], O, ACT.Copy).then_inc(s["o_copied"], 1)

            def transposed_again(r, d):
                evacuate(xn2T[:, :], X, r["xt2_full"], d + 1, r["xn2T_ready"])

            def gate_exp(r, d):
                act.wait_ge(r["topd_ready"], d + 1)
                nc.scalar.activation(tope[:, :, :], topd[:, :, :], ACT.Exp).then_inc(r["tope_ready"], 1)

            def a_body(it, par, on):
                a, b, c, d = it, it - 1, it - 2, it - 3
                steps = {u: (name, stage) for name, u, stage in A_ORDER}
                for u in range(UNITS):
                    g, j = divmod(u, GROUP_UNITS)
                    if on[2]:
                        act.wait_ge(sa["score_full"], c * UNITS + u + 1)
                        wait(act, sa["pv_done"], (c * GROUPS + g - 1) * len(PV_STEPS) + PV_OF_UNIT[j])
                        nc.scalar.activation(probs[:, j, :].rearrange("p (a n) -> p a n", a=2),
                                             SC[:, 2 * (u % 2):2 * (u % 2) + 2, :], ACT.Exp, scale=SCALE) \
                            .then_inc(sa["probs_ready"], 1)
                        if g and j == 1:
                            take_out(sa, c * GROUPS + g - 1, (c * GROUPS + g) * len(PV_STEPS), g - 1,
                                     (sa["out_full"], c))
                    name, stage = steps.get(u, (None, 0))
                    if not on[stage]:
                        continue
                    if name == "den":
                        wait(act, sa["recip_ready"], d * 4)
                        evacuate(den_s[:, :], X, sa["den_full"], d + 1, sa["den_read"])
                    if name in ("mt1", "mt0"):
                        n = c * 2 + 1 if name == "mt1" else b * 2
                        act.wait_ge(sa["mt_full"], n + 1)
                        wait(act, sa["mrows_loaded"], n * MROW_DMAS * 16)
                        nc.scalar.activation(mparts[:, 0, :], X[0:HG, :], ACT.Copy).then_inc(sa["high_ready"], 1)
                    if name == "xt":
                        evacuate(xnT[:, :], X, sa["xt_full"], a + 1, sa["xnT_ready"])
                    if name == "v":
                        wait(act, sa["vpad_ready"], a)
                        evacuate(v_s[:, :, :], Xt, sa["proj_full"], a * 5 + 5, sa["v_ready"])
                    if name == "xt2":
                        transposed_again(ra, d)
                    if name == "lg":
                        gate_exp(ra, d)
                if on[2]:
                    take_out(sa, c * GROUPS + GROUPS - 1, (c + 1) * GROUPS * len(PV_STEPS), GROUPS - 1, (sa["out_full"], c))

            over_batches(act, 4, a_body)

            def expert_phase(e):
                def turn(p, r, par, t, h, y):
                    if t:
                        act.wait_ge(e["xbt_full"], p + 1)
                        nc.scalar.activation(xbT[:, par, :], bank[:, par, 0:P], ACT.Copy).then_inc(e["xbt_ready"], 1)
                    if h:
                        act.wait_ge(e["hpre_ready"], p)
                        wait(act, e["y_full"], p - 2)
                        nc.scalar.activation(hact[:, 1 - par, :, :, :], hpre[:, 1 - par, :, :, :], ACT.Gelu) \
                            .then_inc(e["h_ready"], 1)
                over_pairs(act, turn)

            expert_phase(eb)

            def c_body(it, par, on):
                b, c, d = it, it - 1, it - 2
                steps = {u: (name, stage) for name, u, stage in C_ORDER}
                for u in range(H):
                    g, j = divmod(u, QG)
                    if on[1] and g and j == 1:
                        take_out(sc_, c * GROUPS + g - 1, c * GROUPS + g, g - 1, (sc_["ctx_full"], c))
                    name, stage = steps.get(u, (None, 0))
                    if not on[stage]:
                        continue
                    if name == "ctx":
                        wait(act, sc_["wo_full"], d)
                        evacuate(attnT[:, :], X, sc_["ctx_full"], d + 1, sc_["ctx_ready"])
                    if name == "xt":
                        evacuate(xnT[:, :], X, sc_["xt_full"], b + 1, sc_["xnT_ready"])
                    if name == "n":
                        act.wait_ge(sc_["proj_full"], b * 3 + 1)
                        wait(act, sc_["q_ready"], b)
                        nc.scalar.activation(nexp[:, :], X, ACT.Exp, scale=-1.0, bias=bn_s[:, 1:2]) \
                            .then_inc(sc_["nexp_ready"], 1)
                    if name == "k":
                        wait(act, sc_["parts_written"], b * 32)
                        act.wait_ge(sc_["q_ready"], b + 1)
                        nc.scalar.activation(parts[0][:, 0, :], qs[par], ACT.Copy).then_inc(sc_["high_ready"], 1)
                        act.wait_ge(sc_["proj_full"], b * 3 + 3)
                        nc.scalar.activation(rope[1][:, 0, :], X, ACT.Identity, bias=bq_s[:, 1:2]) \
                            .then_inc(sc_["k_ready"], 1)
                        act.wait_ge(sc_["k_ready"], b + 1)
                        nc.scalar.activation(parts[1][:, 0, :], rope[1][:, 0, :], ACT.Copy).then_inc(sc_["high_ready"], 1)
                    if name == "xt2":
                        transposed_again(rc, d)
                    if name == "lg":
                        gate_exp(rc, d)
                if on[1]:
                    take_out(sc_, c * GROUPS + GROUPS - 1, (c + 1) * GROUPS, GROUPS - 1, (sc_["ctx_full"], c))

            over_batches(act, 3, c_body)
            expert_phase(ed)

        @block.vector
        def _(dve):
            link = Chain(dve, dve_chain)
            tt, ts, stt = nc.vector.tensor_tensor, nc.vector.tensor_scalar, nc.vector.scalar_tensor_tensor

            def refine(y, v, t):
                link(tt(t, y, y, ALU.mult))
                link(tt(t, t, v, ALU.mult))
                link(ts(t, t, -0.5, 1.5, ALU.mult, ALU.add))
                return tt(y, y, t, ALU.mult)

            nc.vector.memset(rvar[:, :], 0.0)
            dve.wait_ge(x_dma, 16)
            for t in range(NT):
                last = nc.vector.bn_stats(bn6[:, t, :], xres[:, t, :])
            link(last)
            for t in range(NT):
                last = nc.vector.bn_aggr(stat1[:, t, :], bn6[:, t, :])
            link(last)
            ts(var1[:, :], stat1[:, :, 1], EPS, None, ALU.add).then_inc(var1_ready, 1)
            dve.wait_ge(wT_copied, 1)
            for n in (0, 2):
                for t in range(2):
                    last = nc.vector.tensor_copy(
                        wT[:, n + 1, :].rearrange("p (h t d) -> p h t d", t=2, d=DH // 2)[:, :, t, :],
                        wT[:, n, :].rearrange("p (h t d) -> p h t d", t=2, d=DH // 2)[:, :, 1 - t, :])
            dve.wait_ge(consts_dma, 8 * 16)
            dve.wait_ge(bias_dma, BIAS_DMAS * 16)
            ts(bn_s[:, 1:2], bn_s[:, 0:1], -1.0, None, ALU.mult)
            nc.vector.tensor_copy(wn_s[:, :].rearrange("p (h d) -> p h d", d=DH),
                                  wn_in[:, :].unsqueeze(2).to_broadcast([P, H, DH])).then_inc(weights_ready, 1)
            dve.wait_ge(pow1_ready, 1)
            dve.wait_ge(consts_ready, 1)
            link(refine(rstd1[:, :], var1[:, :], nwt1[:, :]))

            def fence():
                n = next(dve_columns)
                nc.vector.tensor_copy(dve_scratch[:, n:n + 1], ident[:, 0:1])

            def statistics(tile0):
                fence()
                for t in range(TB):
                    last = nc.vector.bn_stats(rst6[:, t, :], xres[:, bass.ds(tile0 + t, 1), :].rearrange("p a d -> p (a d)"))
                link(last)
                fence()
                for t in range(TB):
                    last = nc.vector.bn_aggr(rst2[:, t, :], rst6[:, t, :])
                link(last)
                return ts(rvar[:, :], rst2[:, :, 1], EPS, None, ALU.add)

            def normalise(dst, tile0, mean, rstd):
                for t in range(TB):
                    last = ts(dst[:, t, :], xres[:, bass.ds(tile0 + t, 1), :].rearrange("p a d -> p (a d)"),
                              mean(t), rstd(t), ALU.subtract, ALU.mult)
                return last

            def norm_2(r, d):
                dve.wait_ge(r["rpow_ready"], d + 1)
                link(refine(rpow[:, :], rvar[:, :], rnwt[:, :]))
                wait(dve, r["scattered"], d * TB * K * 16)
                normalise(xn2, d * TB, lambda t: rst2[:, t, 0:1], lambda t: rpow[:, t:t + 1]).then_inc(r["xn2_ready"], 1)

            def choose(r, n, d):
                dve.wait_ge(r["logit_full"], d + 1)
                link(tt(logit[:, :, :], X[:, 0:TB * E].rearrange("p (t e) -> p t e", e=E),
                        gate_bs[:, :].unsqueeze(1).to_broadcast([P, TB, E]), ALU.add))
                fence()
                for t in range(TB):
                    last = nc.vector.max(top8[:, t, :], logit[:, t, :])
                link(last)
                tt(topd[:, :, :], top8[:, :, 0:K], top8[:, :, 0:1].to_broadcast([P, TB, K]), ALU.subtract) \
                    .then_inc(r["topd_ready"], 1)
                for t in range(TB):
                    last = nc.vector.max_index(idx8[:, t, :], top8[:, t, :], logit[:, t, :])
                link(last)
                link(nc.vector.tensor_copy(topi[:, :, :], idx8[:, :, 0:K]))
                for k in range(K):
                    last = tt(onehot[:, k, :, :], expert_no[:, :].unsqueeze(1).to_broadcast([P, TB, E]),
                              topi[:, :, k:k + 1].to_broadcast([P, TB, E]), ALU.is_equal)
                link(last)
                link(tt(ptmp[:, 0, :, :], onehot[:, 0, :, :], onehot[:, 1, :, :], ALU.add))
                tt(chosen[:, :, :], ptmp[:, 0, :, :], onehot[:, 2, :, :], ALU.add).then_inc(r["chosen_ready"], 1)

            def place(r, n, d):
                dve.wait_ge(r["pos_full"], d + 1)
                pos_ps = X[:, 0:TB * E].rearrange("p (t e) -> p t e", e=E)
                for k in range(K):
                    last = tt(ptmp[:, k, :, :], onehot[:, k, :, :], pos_ps, ALU.mult)
                last.then_inc(r["pos_read"], 1)
                dve.wait_ge(r["pos_read"], d + 1)
                for k in range(K):
                    last = nc.vector.reduce_sum(pos[:, :, k], ptmp[:, k, :, :], AX.X)
                link(last)
                dve.wait_ge(r["tope_ready"], d + 1)
                link(nc.vector.reduce_sum(esum[:, :], tope[:, :, :], AX.X))
                link(nc.vector.reciprocal(esum[:, :], esum[:, :]))
                link(tt(tope[:, :, :], tope[:, :, :], esum[:, :].unsqueeze(2).to_broadcast([P, TB, K]), ALU.mult))
                link(nc.vector.reduce_sum(csum[:, :], chosen[:, :, :].rearrange("p t e -> p e t"), AX.X))
                link(tt(count[:, :], count[:, :], csum[:, :], ALU.add))
                ts(room[:, :, :], pos[:, :, :], float(CAP), None, ALU.is_lt)
                link(stt(slot[:, :, :], topi[:, :, :], float(CAP), pos[:, :, :], ALU.mult, ALU.add))
                link(tt(gate_tab[n][:, bass.ds(d * TB, TB), :], tope[:, :, :], room[:, :, :], ALU.mult))
                link(ts(room[:, :, :], room[:, :, :], -OUT_OF_RANGE, OUT_OF_RANGE, ALU.mult, ALU.add))
                tt(slot_u[:, :].rearrange("p (t k) -> p t k", k=K), slot[:, :, :], room[:, :, :], ALU.add) \
                    .then_inc(r["slot_ready"], 1)
                link(ts(pos[:, :, :], pos[:, :, :], float(CAP - 1), None, ALU.min))
                link(stt(slot[:, :, :], topi[:, :, :], float(CAP), pos[:, :, :], ALU.mult, ALU.add))
                link(nc.vector.tensor_copy(row_tab[n][:, bass.ds(d * TB, TB), :], slot[:, :, :]))

            def reciprocals(d, n):
                if n == 0:
                    dve.wait_ge(sa["den_read"], d + 1)
                at = slice(n * P, (n + 1) * P)
                nc.vector.reciprocal(rden[:, at], den_s[:, at]).then_inc(sa["recip_ready"], 1)

            def maxima(it, u):
                for k in (2 * u, 2 * u + 1):
                    dve.wait_ge(sa["max_full"], it * BANKS + k + 1)
                    nc.vector.tensor_reduce(bmax[:, 4 * k:4 * k + 4], MX[:, k % 2, :].rearrange("p (j n) -> p j n", n=P),
                                            AX.X, ALU.max).then_inc(sa["max_done"], 1)

            def join_maxima(it, half):
                dve.wait_ge(sa["max_done"], it * BANKS + 20 * (half + 1))
                wait(dve, sa["mt_full"], it * 2 + half)
                v = bmax[:, 80 * half:80 * half + 80].rearrange("p (r c) -> p r c", c=20)
                wide = v[:, :, 0:16].rearrange("p r (h c) -> p r h c", c=8)
                tail = v[:, :, 16:20].rearrange("p r (h c) -> p r h c", c=2)
                dst = negm[:, half, :, :].rearrange("p q (r h) -> p q r h", h=2)
                for q, src in ((3, wide[:, :, :, 0:4]), (0, wide[:, :, :, 4:5]), (2, wide[:, :, :, 5:8]), (1, tail)):
                    last = nc.vector.tensor_reduce(dst[:, q, :, :], src, AX.X, ALU.max, negate=True)
                last.then_inc(sa["negm_ready"], 1)

            def split_maxima(it, half):
                dve.wait_ge(sa["mt_full"], it * 2 + half + 1)
                dve.wait_ge(sa["high_ready"], it * 2 + half + 1)
                tt(mparts[:, 1, :], X[0:HG, :], mparts[:, 0, :], ALU.subtract).then_inc(sa["mparts_ready"], 1)

            def a_body(it, par, on):
                a, b, c, d = it, it - 1, it - 2, it - 3
                for u in range(UNITS):
                    if u == 0 and on[2]:
                        join_maxima(c, 1)
                    if u == UNITS // 2 and on[1]:
                        join_maxima(b, 0)
                    if on[1]:
                        maxima(b, u)
                    if u == 0 and on[0]:
                        wait(dve, sa["xt_full"], a)
                        t0 = a * TB
                        for t in range(TB):
                            last = ts(xn[:, t, :], flat(xres[:, bass.ds(t0 + t, 1), :]),
                                      flat(stat1[:, bass.ds(t0 + t, 1), 0:1]), rstd1[:, bass.ds(t0 + t, 1)],
                                      ALU.subtract, ALU.mult)
                        last.then_inc(sa["xn_ready"], 1)
                    if 1 <= u <= 4 and on[3]:
                        reciprocals(d, u - 1)
                    if u == 1 and on[2]:
                        split_maxima(c, 1)
                    if u in (3, 4, 7, 8) and on[0]:
                        j = (3, 4, 7, 8).index(u)
                        dve.wait_ge(sa["proj_full"], a * 5 + j + 1)
                        if j % 2 == 0:
                            wait(dve, sa["split_ready"], a * 2 + j // 2 - 1)
                        tt(rope[j // 2][:, j % 2, :], X, cossin[:, j % 2, :], ALU.mult).then_inc(sa["rope_ready"], 1)
                    if u == 5 and on[3]:
                        dve.wait_ge(sa["out_full"], d + 1)
                        dve.wait_ge(sa["recip_ready"], (d + 1) * 4)
                        wait(dve, sa["wo_full"], d)
                        tt(attnT[:, :], X, rden[:, :], ALU.mult).then_inc(sa["attn_ready"], 1)
                    if u == 6 and on[3]:
                        dve.wait_ge(sa["wo_full"], d + 1)
                        xt = xres[:, bass.ds(d * TB, TB), :]
                        tt(xt, Xt, xt, ALU.add).then_inc(sa["residual_ready"], 1)
                        dve.wait_ge(sa["residual_ready"], d + 1)
                        statistics(d * TB).then_inc(ra["rvar_ready"], 1)
                    if u == 9 and on[3]:
                        norm_2(ra, d)
                    if u == 12 and on[1]:
                        split_maxima(b, 0)
                    if u == 13 and on[3]:
                        choose(ra, 0, d)
                    if u == 16 and on[3]:
                        place(ra, 0, d)

            over_batches(dve, 4, a_body, link, 2 * 24)

            def expert_phase(e):
                def turn(p, r, par, t, h, y):
                    if h:
                        dve.wait_ge(e["h_full"], p)
                        wait(dve, e["h_ready"], p - 2)
                        q = p - 1
                        tt(hpre[:, 1 - par, :, :, :].rearrange("p a c n -> p (a c) n"),
                           bank[:, 2 + (1 - par), :].rearrange("p (a n) -> p a n", n=CAP),
                           b1_s[:, bass.ds(q * 2, 2), :].rearrange("p a c -> p (a c)").unsqueeze(2)
                           .to_broadcast([P, 2 * HC, CAP]), ALU.add).then_inc(e["hpre_ready"], 1)
                    if y:
                        dve.wait_ge(e["y_full"], p - 1)
                        wait(dve, e["y_stored"][par], (p - par - 2) * 8)
                        q = p - 2
                        tt(y_s[:, par, :], bank[:, 4 + par, 0:D],
                           b2_s[:, (r - 2) % RING, :], ALU.add).then_inc(e["y_ready"], 1)
                over_pairs(dve, turn)

            expert_phase(eb)

            def rows(n, ready, b, par):
                nc.vector.tensor_copy(row_u[par][:, :].rearrange("p (t k) -> p t k", k=K),
                                      row_tab[n][:, bass.ds(b * TB, TB), :]).then_inc(ready, 1)

            def add_rows(n, b, par):
                for k in range(K):
                    for t in range(TB):
                        xt = xres[:, bass.ds(b * TB + t, 1), :].rearrange("p a d -> p (a d)")
                        last = stt(xt, yrows[par][:, t * K + k, :],
                                   gate_tab[n][:, bass.ds(b * TB + t, 1), k:k + 1].rearrange("p a k -> p (a k)"),
                                   xt, ALU.mult, ALU.add)
                    if k < K - 1:
                        link(last)
                return last

            dve.wait_ge(sc_["vext_cleared"], 1)
            rows(0, sc_["row_u_ready"], 0, 0)

            def mask_scores(c, u):
                dve.wait_ge(sc_["score_full"], c * H + u + 1)
                wait(dve, sc_["pv_done"], c * GROUPS + u // QG - 1)
                tt(masked(u).rearrange("p (t n) -> p t n", n=P), SC[:, u % 2, :].rearrange("p (t n) -> p t n", n=P),
                   keep_k[:, :].unsqueeze(1).to_broadcast([P, TB, P]), ALU.mult).then_inc(sc_["probs_ready"], 1)

            def c_body(it, par, on):
                b, c, d = it, it - 1, it - 2
                if on[0]:
                    wait(dve, rows_gathered[1 - par], (b + par) * (GATHER // 2))
                    rows(0, sc_["row_u_ready"], b + 1, 1 - par)
                    dve.wait_ge(rows_gathered[par], (b - par + 2) * (GATHER // 2))
                    link(add_rows(0, b, par))
                    statistics(b * TB).then_inc(sc_["var_ready"], 1)
                for u in range(H):
                    if on[1]:
                        mask_scores(c, u)
                    if on[0] and u == 0:
                        dve.wait_ge(sc_["pow_ready"], b + 1)
                        link(refine(rpow[:, :], rvar[:, :], rnwt[:, :]))
                        wait(dve, sc_["xt_full"], b)
                        normalise(xn, b * TB, lambda t: rst2[:, t, 0:1], lambda t: rpow[:, t:t + 1]) \
                            .then_inc(sc_["xn_ready"], 1)
                    if on[2] and u == 2:
                        dve.wait_ge(sc_["wo_full"], d + 1)
                        xt = xres[:, bass.ds(d * TB, TB), :]
                        tt(xt, Xt, xt, ALU.add).then_inc(sc_["residual_ready"], 1)
                        dve.wait_ge(sc_["residual_ready"], d + 1)
                        link(tt(xt, xt, bo_s[:, :].unsqueeze(1).to_broadcast([P, TB, D]), ALU.add))
                        statistics(d * TB).then_inc(rc["rvar_ready"], 1)
                    if on[0] and u == 4:
                        dve.wait_ge(sc_["proj_full"], b * 3 + 2)
                        dve.wait_ge(sc_["nexp_ready"], b + 1)
                        wait(dve, sc_["ctx_full"], b - 1)
                        stt(qs[par], X, bq_s[:, 0:1], nexp[:, :], ALU.add, ALU.mult).then_inc(sc_["q_ready"], 1)
                    if on[2] and u == 5:
                        norm_2(rc, d)
                    if on[0] and u == C_KV:
                        dve.wait_ge(sc_["kv_full"], b + 1)
                        wait(dve, sc_["state_full"], b * 3)
                        wait(dve, sc_["pv_done"], (b - 1) * GROUPS)
                        for j in range(2):
                            kv = SC[:, 2 + j, :].rearrange("p (t n) -> p t n", t=2)
                            tt(kn[:, 2 * j:2 * j + 2, :], kv[:, :, 0:P],
                               bkv_s[:, 0:P].unsqueeze(1).to_broadcast([P, 2, P]), ALU.add)
                            for t in range(2):
                                last = tt(vext[par][:, 2 * j + t, :, 0:DH], kv[:, t, P:2 * P].rearrange("p (h d) -> p h d", d=DH),
                                          bkv_s[:, P:2 * P].rearrange("p (h d) -> p h d", d=DH), ALU.add)
                        last.then_inc(sc_["kvn_ready"], 1)
                    if on[0] and C_ST <= u < C_ST + TB - 1:
                        j = u - C_ST
                        dve.wait_ge(sc_["state_full"], b * 3 + j + 1)
                        tt(stm[par][:, j, :], MX[:, 0, 0:P], same_head[:, :], ALU.mult).then_inc(sc_["state_ready"], 1)
                    if on[2] and u == 9:
                        choose(rc, 1, d)
                    if on[2] and u == 12:
                        place(rc, 1, d)

            over_batches(dve, 3, c_body, link, 2 * 34)
            expert_phase(ed)

            rows(1, final_rows, 0, 0)

            def final(b, par, more):
                if more:
                    wait(dve, final_gathered[1 - par], (b + par) * (GATHER // 2))
                    rows(1, final_rows, b + 1, 1 - par)
                dve.wait_ge(final_gathered[par], (b - par + 2) * (GATHER // 2))
                add_rows(1, b, par).then_inc(final_ready, 1)

            final(0, 0, True)
            with dve.Fori(0, B // 2 - 1) as i:
                link.enter(i, 2 * (K - 1))
                final(i * 2 + 1, 1, True)
                final(i * 2 + 2, 0, True)
                link.leave(B // 2 - 1)
            final(B - 1, 1, False)

        @block.tensor
        def _(pe):
            mm = nc.tensor.matmul

            pe.wait_ge(consts_ready, 1)
            pe.wait_ge(w_dma, 4 * 16)
            for n in range(4):
                last = nc.tensor.transpose(Xt[:, n, :], w_in[:, n, :], ident[:, :])
            last.then_inc(wT_full, 1)
            pe.wait_ge(wT_copied, 1)
            pe.wait_ge(weights_ready, 1)

            def turn_tiles(src, ready, full, b):
                pe.wait_ge(ready, b + 1)
                for t in range(TB):
                    last = nc.tensor.transpose(Xt[:, t, :], src[:, t, :], ident[:, :])
                last.then_inc(full, 1)

            def project(s, w):
                mm(X, w, xnT[:, :], start=True, stop=True).then_inc(s["proj_full"], 1)

            def tile_products(w, srcT, width):
                for t in range(TB):
                    last = mm(X[:, t * width:(t + 1) * width], srcT[:, t * P:(t + 1) * P], w, start=True, stop=True)
                return last

            def positions(r, d):
                pe.wait_ge(r["chosen_ready"], d + 1)
                for t in range(TB):
                    o = X[:, t * E:(t + 1) * E]
                    mm(o, ones_b[:, :], count[:, :], start=True, stop=False)
                    for j in range(t):
                        mm(o, ones_b[:, :], chosen[:, j, :], start=False, stop=False)
                    last = mm(o, before[:, :], chosen[:, t, :], start=False, stop=True)
                last.then_inc(r["pos_full"], 1)

            def scores(dst, left, right, head0, segments, rows_, mask, query_major):
                for n, (h, i, at, cols) in enumerate(segments):
                    p0, col = place_of(head0 + h)
                    lhs = left[p0:p0 + rows_, col, P * i:P * (i + 1)]
                    rhs = right[p0:p0 + rows_, col, 0:cols] if query_major else right[p0:p0 + rows_, col, P * i:S]
                    mm(dst[:, at:at + cols], lhs, rhs, start=(n == 0), stop=False, skip_group_check=True)
                diag = [at + cols - P if query_major else at for _, _, at, cols in segments]
                for a in diag:
                    last = mm(dst[:, a:a + P], ident_b[:, :], mask[:, :], start=False, stop=(a == diag[-1]),
                              skip_group_check=True)
                return last

            def claim(order, readers, it, on, name):
                found = step_before(order, it, on, name)
                if found:
                    (before_, _, stage), at = found
                    s, per, which = readers[before_]
                    pe.wait_ge(s, (at - stage) * per + which)

            def select_heads(sel, full, d):
                for g in range(GROUPS):
                    last = mm(X[32 * g:32 * g + 32, :], sel[:, :], o_s[:, g, :], start=True, stop=True)
                if full:
                    last.then_inc(full, 1)

            def turn_maxima(b, half):
                pe.wait_ge(sa["negm_ready"], b * 2 + half + 1)
                for q in range(TB):
                    last = nc.tensor.transpose(X[0:HG, q * P:(q + 1) * P], negm[:, half, q, :], ident[:, :])
                last.then_inc(sa["mt_full"], 1)

            def a_body(it, par, on):
                a, b, c, d = it, it - 1, it - 2, it - 3
                steps = {u: (name, stage) for name, u, stage in A_ORDER}

                def products(g, n):
                    unit, blocks = PV_STEPS[n]
                    pe.wait_ge(sa["probs_ready"], c * UNITS + g * GROUP_UNITS + unit + 1)
                    if n == 0:
                        if g == 0:
                            pe.wait_ge(sa["vpad_ready"], c + 1)
                        wait(pe, sa["o_copied"], c * GROUPS + g)
                    for i in blocks:
                        for j in range(QG):
                            k, half, at = key_place(j, i)
                            at += 512 * half
                            last = mm(O[32 * j:32 * j + 32, P * i:S], vext[par][:, i, QG * g + j, :],
                                      probs[:, k, at:at + S - P * i], start=(i == 0), stop=(i == 2),
                                      skip_group_check=True)
                    last.then_inc(sa["pv_done"], 1)

                for u in range(UNITS):
                    g, j = divmod(u, GROUP_UNITS)
                    if on[2]:
                        wait(pe, sa["probs_ready"], c * UNITS + u - 1)
                        if u in (0, UNITS // 2):
                            pe.wait_ge(sa["mrows_loaded"], (c * 2 + (u > 0) + 1) * MROW_DMAS * 16)
                        for n in range(2):
                            last = scores(SC[:, 2 * (u % 2) + n, :], kstk[par], qstk[par], QG * g, KEY_BANKS[2 * j + n],
                                          KM, mask_k, False)
                        last.then_inc(sa["score_full"], 1)
                    name, stage = steps.get(u, (None, 0))
                    if name and on[stage]:
                        if name == "den":
                            pe.wait_ge(sa["o_copied"], (d + 1) * GROUPS)
                        claim(A_ORDER, A_READERS, it, on, name)
                        if name == "den":
                            select_heads(sel_d, sa["den_full"], d)
                        if name == "out":
                            select_heads(sel_o, sa["out_full"], d)
                        if name == "mt1":
                            turn_maxima(c, 1)
                        if name == "mt0":
                            turn_maxima(b, 0)
                        if name == "xt":
                            turn_tiles(xn, sa["xn_ready"], sa["xt_full"], a)
                        if name in ("q", "qr", "k", "kr"):
                            if name == "q":
                                pe.wait_ge(sa["xnT_ready"], a + 1)
                            project(sa, wT[:, ("q", "qr", "k", "kr").index(name), :])
                        if name == "v":
                            tile_products(wT[:, 4, :], xnT, P).then_inc(sa["proj_full"], 1)
                        if name == "wo":
                            pe.wait_ge(sa["attn_ready"], d + 1)
                            tile_products(wT[:, 5, :], attnT, D).then_inc(sa["wo_full"], 1)
                        if name == "xt2":
                            turn_tiles(xn2, ra["xn2_ready"], ra["xt2_full"], d)
                        if name == "lg":
                            pe.wait_ge(ra["xn2T_ready"], d + 1)
                            tile_products(gate_ws[:, :], xn2T, E).then_inc(ra["logit_full"], 1)
                        if name == "pos":
                            positions(ra, d)
                    if on[1]:
                        if u in (0, UNITS // 2):
                            pe.wait_ge(sa["stack_loaded"][u > 0], (b + 1) * STACK_DMAS * 16)
                        for k in (2 * u, 2 * u + 1):
                            wait(pe, sa["max_done"], b * BANKS + k - 1)
                            scores(MX[:, k % 2, :], qstk[1 - par], kstk[1 - par], 2 * (k // 5), QUERY_BANKS[k % 5], KR,
                                   mask_q, True).then_inc(sa["max_full"], 1)
                    if on[2]:
                        if j == 0 and g:
                            products(g - 1, 2)
                        if j == 2:
                            products(g, 0)
                        if j == 4:
                            products(g, 1)
                if on[2]:
                    products(GROUPS - 1, 2)

            over_batches(pe, 4, a_body)

            def expert_phase(e):
                def turn(p, r, par, t, h, y):
                    if t:
                        pe.wait_ge(e["landed"][r], (p - r) * (PAIR_DMAS * 16 // RING) + PAIR_DMAS * 16)
                        if r % BLOCK == 0:
                            pe.wait_ge(e["block_landed"][r // BLOCK], (p - r) * (BLOCK_DMAS * 16 // RING) + BLOCK_DMAS * 16)
                        wait(pe, e["xbt_ready"], p - 1)
                        nc.tensor.transpose(bank[:, par, 0:P], xb_s[:, r, :], ident[:, :]).then_inc(e["xbt_full"], 1)
                    if h:
                        q, rq, bq_ = p - 1, (r - 1) % RING, 1 - par
                        pe.wait_ge(e["xbt_ready"], p)
                        wait(pe, e["hpre_ready"], p - 2)
                        for t_ in range(2):
                            for c in range(HC):
                                at = (t_ * HC + c) * CAP
                                last = mm(bank[:, 2 + bq_, at:at + CAP], w1_s[rq][:, t_, c:HID:HC],
                                          xbT[:, bq_, CAP * t_:CAP * (t_ + 1)], start=True, stop=True)
                        last.then_inc(e["h_full"], 1)
                    if y:
                        rq = (r - 2) % RING
                        pe.wait_ge(e["h_ready"], p - 1)
                        wait(pe, e["y_ready"], p - 3)
                        for t_ in range(2):
                            for c in range(HC):
                                last = mm(bank[CAP * t_:CAP * (t_ + 1), 4 + par, 0:D], hact[:, par, t_, c, :],
                                          w2_s[rq][:, t_, c, :], start=(c == 0), stop=(c == HC - 1))
                        last.then_inc(e["y_full"], 1)
                over_pairs(pe, turn)

            expert_phase(eb)

            def c_body(it, par, on):
                b, c, d = it, it - 1, it - 2
                steps = {u: (name, stage) for name, u, stage in C_ORDER}

                def products(g):
                    pe.wait_ge(sc_["probs_ready"], c * H + QG * g + QG)
                    wait(pe, sc_["o_copied"], c * GROUPS + g)
                    for t in range(TB):
                        for j in range(QG):
                            last = mm(O[32 * j:32 * j + 32, t * P:(t + 1) * P], vext[1 - par][:, t, QG * g + j, :],
                                      masked(QG * g + j)[:, t * P:(t + 1) * P], start=(t == 0), stop=(t == TB - 1),
                                      skip_group_check=True)
                    last.then_inc(sc_["pv_done"], 1)

                for u in range(H):
                    if on[1]:
                        if u == 0:
                            pe.wait_ge(sc_["stack_loaded"][0], (c + 1) * 2 * STACK_DMAS * 16)
                        wait(pe, sc_["probs_ready"], c * H + u - 1)
                        p0, col = place_of(u)
                        for t in range(TB):
                            last = mm(SC[:, u % 2, t * P:(t + 1) * P],
                                      kstk[1 - par][p0:p0 + KR, col, t * P:(t + 1) * P],
                                      qstk[1 - par][p0:p0 + KR, col, t * P:(t + 1) * P], start=True, stop=True)
                        last.then_inc(sc_["score_full"], 1)
                    name, stage = steps.get(u, (None, 0))
                    if name and on[stage]:
                        if name == "ctx":
                            pe.wait_ge(sc_["o_copied"], (d + 1) * GROUPS)
                        claim(C_ORDER, C_READERS, it, on, name)
                        if name == "ctx":
                            select_heads(sel_o, None, d)
                            pe.wait_ge(sc_["state_ready"], (d + 1) * (TB - 1))
                            for t in range(1, TB):
                                last = mm(X[:, t * P:(t + 1) * P], stm[par][:, t - 1, :], qs[par][:, t * P:(t + 1) * P],
                                          start=False, stop=(t == TB - 1), skip_group_check=True)
                            last.then_inc(sc_["ctx_full"], 1)
                        if name == "xt":
                            turn_tiles(xn, sc_["xn_ready"], sc_["xt_full"], b)
                        if name == "n":
                            pe.wait_ge(sc_["xnT_ready"], b + 1)
                            project(sc_, wn_s[:, :])
                        if name == "q":
                            project(sc_, wq2_s[:, :])
                        if name == "k":
                            project(sc_, wkv_s[:, 0:P])
                        if name == "wo":
                            pe.wait_ge(sc_["ctx_ready"], d + 1)
                            tile_products(wo2_s[:, :], attnT, D).then_inc(sc_["wo_full"], 1)
                        if name == "xt2":
                            turn_tiles(xn2, rc["xn2_ready"], rc["xt2_full"], d)
                        if name == "lg":
                            pe.wait_ge(rc["xn2T_ready"], d + 1)
                            tile_products(gate_ws[:, :], xn2T, E).then_inc(rc["logit_full"], 1)
                        if name == "pos":
                            positions(rc, d)
                    if on[0] and u == C_KV:
                        wait(pe, sc_["kvn_ready"], b)
                        for t in range(TB):
                            last = mm(SC[:, 2 + t // 2, (t % 2) * 256:(t % 2) * 256 + 256], xnT[:, t * P:(t + 1) * P],
                                      wkv_s[:, :], start=True, stop=True)
                        last.then_inc(sc_["kv_full"], 1)
                    if on[0] and C_ST <= u < C_ST + TB - 1:
                        j = u - C_ST
                        pe.wait_ge(sc_["kvn_ready"], b + 1)
                        wait(pe, sc_["state_ready"], b * 3 + j)
                        mm(MX[:, 0, 0:P].rearrange("p (h d) -> p h d", d=DH), kn[:, j, :], vext[par][:, j, :, 0:DH],
                           start=(j == 0), stop=True, skip_group_check=True).then_inc(sc_["state_full"], 1)
                    if on[1] and u % QG == 0 and u:
                        products(u // QG - 1)
                if on[1]:
                    products(GROUPS - 1)

            over_batches(pe, 3, c_body)
            expert_phase(ed)


_INS = ["L0_attn_a_x", "L0_attn_a_Wq", "L0_attn_a_Wk", "L0_attn_a_Wv", "L0_attn_a_Wo", "L0_attn_b_Wqk",
        "L0_attn_b_bqk", "L0_attn_b_Wv", "L0_attn_b_bv", "L0_attn_b_Wn", "L0_attn_b_bn", "L0_attn_b_Wo",
        "L0_attn_b_bo", "L0_ffn_gate_w", "L0_ffn_gate_b", "L0_ffn_w1", "L0_ffn_b1", "L0_ffn_w2", "L0_ffn_b2"]


def rotary_tables():
    import numpy as np
    inv = (1.0 / np.float32(10000.0) ** (np.arange(0, DH, 2, dtype=np.float32) / np.float32(DH))).astype(np.float32)
    f = np.outer(np.arange(S, dtype=np.float32), inv).astype(np.float32)
    cos, sin = np.cos(f).T, np.sin(f).T
    return (np.ascontiguousarray(np.tile(np.concatenate([cos, cos]), (H, 1)), dtype=np.float32),
            np.ascontiguousarray(np.tile(np.concatenate([-sin, sin]), (H, 1)), dtype=np.float32))


def kernel(**inputs):
    import numpy as np
    import concourse.bacc as bacc
    from concourse.bass_utils import run_bass_kernel_spmd

    nc = bacc.Bacc("TRN2", target_bir_lowering=False, num_devices=1)
    arrays = {name: np.ascontiguousarray(inputs[name]) for name in _INS}
    arrays["cosT"], arrays["sinT"] = rotary_tables()
    args = [nc.dram_tensor(name, a.shape, mybir.dt.from_np(a.dtype), kind="ExternalInput").ap()
            for name, a in arrays.items()]
    args.append(nc.dram_tensor("out", (B, S, D), F32, kind="ExternalOutput").ap())
    build(nc, *args)
    return run_bass_kernel_spmd(nc, [arrays], core_ids=[0]).results[0]["out"]
```

```python
from contextlib import ExitStack

import concourse.bass as bass
from concourse import mybir

F32 = mybir.dt.float32
BF16 = mybir.dt.bfloat16
U32 = mybir.dt.uint32
ALU = mybir.AluOpType
ACT = mybir.ActivationFunctionType
AX = mybir.AxisListType

P = 128
B, S, D = 8, 512, 128
H, DH = 16, 8
TB = S // P
NT = B * TB
E, HID, CAP, K = 64, 512, 64, 3
HC = HID // P
PAIRS = E // 2
RING = 8
BLOCK = 2
EPS = 1e-5
SCALE = 1.0 / DH ** 0.5
NEG = -1e30
NPARTS = 3
Q_ROWS = (0, 0, 1, 1, 0, 2)
K_ROWS = (0, 1, 0, 1, 2, 0)
KR = len(Q_ROWS) * DH
KM = KR + 2
BANKS = 40
MAX_RING = 3
HG = 8
QG = 4
GROUPS = H // QG
OUT_OF_RANGE = 8192.0
WIDTH = D + 1 + K
FAR = 16384.0
ROWS = B * S * K

KEY_BANKS = ([[(h, 0, 0, 512)] for h in range(QG)] + [[(h, 1, 0, 384), (h, 3, 384, 128)] for h in range(QG)]
             + [[(h, 2, 0, 256), (h + 1, 2, 256, 256)] for h in (0, 2)])
QUERY_BANKS = [[(0, 3, 0, 512)], [(0, 0, 0, 128), (0, 2, 128, 384)], [(1, 3, 0, 512)],
               [(1, 0, 0, 128), (1, 2, 128, 384)], [(0, 1, 0, 256), (1, 1, 256, 256)]]
GROUP_BANKS = BANKS // GROUPS
PV_STEPS = ((3, (0,)), (7, (1, 3)), (9, (2,)))
PV_OF_BANK = (1, 1, 1, 1, 2, 2, 2, 2, 3, 3)


def key_place(h, i):
    for k, bank_ in enumerate(KEY_BANKS):
        for hh, ii, at, cols in bank_:
            if (hh, ii) == (h, i):
                return k, at


A_ORDER = (("den", 0, 3), ("mt1", 2, 2), ("xt", 4, 0), ("q", 6, 0), ("qr", 8, 0), ("out", 10, 3), ("k", 12, 0),
           ("wo", 13, 3), ("kr", 15, 0), ("v", 17, 0), ("xt2", 21, 3), ("mt0", 23, 1), ("lg", 26, 3), ("pos", 33, 3))
C_ORDER = (("ctx", 0, 3), ("n", 1, 1), ("wo", 2, 3), ("q", 3, 1), ("k", 4, 1), ("kt", 6, 1), ("vt", 7, 1),
           ("xt2", 8, 3), ("lg", 10, 3), ("pos", 14, 3), ("xt", 15, 0))
C_LEAD = 1
C_ROWS = (1, 8, 9)
C_ST = 10


class Chain:

    def __init__(self, eng, sem):
        self.eng, self.sem, self.base, self.k = eng, sem, 0, 0

    def __call__(self, ins):
        self.k += 1
        ins.then_inc(self.sem, 1)
        self.eng.wait_ge(self.sem, self.base + self.k)

    def mark(self, ins):
        self.k += 1
        ins.then_inc(self.sem, 1)

    def settle(self):
        self.eng.wait_ge(self.sem, self.base + self.k)

    def enter(self, i, per):
        self.start = self.base + self.k
        self.base, self.k, self.per = i * per + self.start, 0, per

    def leave(self, turns):
        assert self.k == self.per, (self.sem, self.k, self.per)
        self.base, self.k = self.start + turns * self.per, 0


def place_of(h):
    return 64 * (h // HG), h % HG


def wait(eng, sem, count):
    if not isinstance(count, int) or count > 0:
        eng.wait_ge(sem, count)


def over_batches(eng, stages, body, chain=None, per=0):
    first = stages + stages % 2
    turns = (B - first) // 2

    def plain(it):
        body(it, it % 2, [0 <= it - s < B for s in range(stages)])

    for it in range(first):
        plain(it)
    with eng.Fori(0, turns) as i:
        if chain:
            chain.enter(i, per)
        body(i * 2 + first, 0, [True] * stages)
        body(i * 2 + (first + 1), 1, [True] * stages)
        if chain:
            chain.leave(turns)
    for it in range(first + 2 * turns, B + stages - 1):
        plain(it)


def step_before(order, it, on, name):
    n = [o[0] for o in order].index(name)
    same_bank = [m for m in range(len(order)) if m % 2 == n % 2]
    for m in reversed([m for m in same_bank if m < n]):
        if on[order[m][2]]:
            return order[m], it
    for m in reversed(same_bank):
        if not isinstance(it, int) or 0 <= it - 1 - order[m][2] < B:
            return order[m], it - 1
    return None


def max_bank(k):
    return k % MAX_RING, MAX_RING if k >= MAX_RING else k + BANKS - max(m for m in range(BANKS) if m % MAX_RING == k)


def over_pairs(eng, turn, chain=None, per=0):
    def plain(p):
        turn(p, p % RING, p % 2, [0 <= p - s < PAIRS for s in range(4)])

    for p in range(RING):
        plain(p)
    turns = PAIRS // RING - 1
    with eng.Fori(0, turns) as i:
        if chain:
            chain.enter(i, per)
        for j in range(RING):
            turn(i * RING + (RING + j), j, j % 2, [True] * 4)
        if chain:
            chain.leave(turns)
    for p in range(PAIRS, PAIRS + 3):
        plain(p)


def flat(ap):
    return ap.rearrange("p a n -> p (a n)")


def build(nc, x, Wq, Wk, Wv, Wo, Wqk, bqk, bWv, bv, Wn, bn, bWo, bo, gate_w, gate_b, w1, b1, w2, b2,
          cosT, sinT, out):
    ctx = ExitStack()
    with ctx:
        def sb(name, shape, dt=F32):
            return ctx.enter_context(nc.sbuf_tensor(name, shape, dt))

        def sem(name):
            return ctx.enter_context(nc.semaphore(name))

        parts_d = [[nc.dram_tensor(f"parts_{n}{par}", (NPARTS, P, S), BF16, kind="Internal").ap() for n in "qk"]
                   for par in range(2)]
        bucket_d = [nc.dram_tensor(f"bucket_{n}", (E * CAP, WIDTH), F32, kind="Internal").ap() for n in range(2)]
        y_d = nc.dram_tensor("expert_out", (ROWS + S * K, D), F32, kind="Internal").ap()

        ident = sb("ident", [P, P])
        ident_b = sb("ident_b", [P, P], BF16)
        mask_q = sb("mask_q", [P, P], BF16)
        mask_k = sb("mask_k", [P, P], BF16)
        keep_k = sb("keep_k", [P, P])
        same_head = sb("same_head", [P, P])
        before = sb("before", [P, P], BF16)
        ones_b = sb("ones_b", [P, P], BF16)
        expert_no = sb("expert_no", [P, E])
        row_expert = sb("row_expert", [P, PAIRS])
        token_no = sb("token_no", [P, NT])
        zeros = sb("zeros", [P, WIDTH])
        minus_half = sb("minus_half", [P, NT])
        pool_scratch, dve_scratch = sb("pool_scratch", [P, 96], BF16), sb("dve_scratch", [P, 96], BF16)
        pool_columns, dve_columns = iter(range(96)), iter(range(96))
        cossin = sb("cossin", [P, 2, S])
        wT = sb("wT", [P, 6, P])
        wq2_s = sb("wq2_s", [P, P])
        wkv_s = sb("wkv_s", [P, 2 * P])
        wn_s = sb("wn_s", [P, P])
        wo2_s = sb("wo2_s", [P, P])
        wn_in = sb("wn_in", [P, H])
        bq_s = sb("bq_s", [P, 2])
        bn_s = sb("bn_s", [P, 2])
        bkv_s = sb("bkv_s", [P, 2 * P])
        bo_s = sb("bo_s", [P, P])
        gate_ws = sb("gate_ws", [P, E])
        gate_bs = sb("gate_bs", [P, E])
        b1_s = sb("b1_s", [P, E, HC])

        xres = sb("xres", [P, NT, D])
        stat1 = sb("stat1", [P, NT, 2])
        rstd1 = sb("rstd1", [P, NT])
        bn6 = sb("bn6", [P, NT, 6])
        var1 = sb("var1", [P, NT])
        nwt1 = sb("nwt1", [P, NT])
        mean1 = sb("mean1", [P, NT])
        count = sb("count", [P, E], BF16)
        gate_tab = [sb(f"gate_tab{n}", [P, NT, K]) for n in range(2)]

        vext = [sb(f"vext{n}", [P, TB, H, 32]) for n in range(2)]
        qstk = [sb(f"qstk{n}", [P, H // 2, S], BF16) for n in range(2)]
        kstk = [sb(f"kstk{n}", [P, H // 2, S], BF16) for n in range(2)]
        probs = sb("probs", [P, GROUP_BANKS, 512])
        xn = sb("xn", [P, TB, D])
        w_in = xn
        xnT = sb("xnT", [P, S])
        rope = [sb(f"rope_{n}", [P, 2, S]) for n in "qk"]
        parts = [sb(f"parts_{n}s", [P, NPARTS, S], BF16) for n in "qk"]
        v_s = sb("v_s", [P, TB, P])
        sel_o = sb("sel_o", [P, 32])
        sel_d = sb("sel_d", [P, 32])
        bmax = sb("bmax", [P, BANKS * 4])
        negm = sb("negm", [P, 2, TB, HG])
        mbuf = sb("mbuf", [P, S])
        mparts = mbuf[0:HG, :].bitcast(BF16).rearrange("p (a s) -> p a s", a=2)
        o_s = sb("o_s", [P, GROUPS, S])
        den_s = sb("den_s", [P, S])
        rden = sb("rden", [P, S])
        attnT = sb("attnT", [P, S])
        qs = [rope[0][:, 0, :], sb("qs1", [P, S])[:, :]]
        kn = cossin[:, 0, :].rearrange("p (t n) -> p t n", n=P)
        stm = [v_s[:, 0:TB - 1, :], mbuf[:, :].rearrange("p (t n) -> p t n", n=P)[:, 0:TB - 1, :]]
        nexp = rden

        xn2 = [sb(f"xn2_{n}", [P, TB, WIDTH]) for n in range(2)]
        xn2T = sb("xn2T", [P, S])
        st6 = [sb(f"st6_{n}", [P, TB, 6]) for n in range(2)]
        st2 = [sb(f"st2_{n}", [P, TB, 2]) for n in range(2)]
        svar = [sb(f"svar{n}", [P, TB]) for n in range(2)]
        spow = [sb(f"spow{n}", [P, TB]) for n in range(2)]
        snwt = [sb(f"snwt{n}", [P, TB]) for n in range(2)]
        smean = [sb(f"smean{n}", [P, TB]) for n in range(2)]
        logit = sb("logit", [P, TB, E])
        top8 = sb("top8", [P, TB, 8])
        idx8 = sb("idx8", [P, TB, 8], U32)
        topi = [t[:, :, D + 1:] for t in xn2]
        topd = sb("topd", [P, TB, K])
        tope = sb("tope", [P, TB, K])
        esum = sb("esum", [P, TB])
        onehot = sb("onehot", [P, K, TB, E], BF16)
        chosen = sb("chosen", [P, TB, E], BF16)
        csum = sb("csum", [P, E])
        ptmp = sb("ptmp", [P, K, TB, E])
        pos = sb("pos", [P, TB, K])
        room = sb("room", [P, TB, K])
        slot = sb("slot", [P, TB, K])
        slot_u = [sb(f"slot_u{n}", [P, TB * K], U32) for n in range(2)]
        yrows = [sb(f"yrows{n}", [P, TB * K, D]) for n in range(2)]

        w1_own = sb("w1_own", [P, RING // 2, 2, HID])
        w2_own = sb("w2_own", [P, RING // 2, 2, HC, D])
        lent = [t[:, :, :].rearrange("p a s -> p (a s)").bitcast(F32) for t in (*qstk, *kstk)]
        w1_s = [w1_own[:, r, :, :] for r in range(RING // 2)] + [
            t[:, 0:2 * HID].rearrange("p (a n) -> p a n", a=2) for t in lent]
        w2_s = [w2_own[:, r, :, :, :] for r in range(RING // 2)] + [
            t[:, 2 * HID:4 * HID].rearrange("p (a c n) -> p a c n", a=2, c=HC) for t in lent]
        xb_s = sb("xb_s", [P, RING, WIDTH])
        xbT = sb("xbT", [P, 2, P])
        hpre = probs[:, 0:2, :].rearrange("p q (a c n) -> p q a c n", a=2, c=HC)
        hact = probs[:, 2:4, :].rearrange("p q (a c n) -> p q a c n", a=2, c=HC)
        hrow = probs[:, 4:6, :]
        y_s = probs[:, 6, 0:2 * D].rearrange("p (q d) -> p q d", q=2)
        b2_s = probs[:, GROUP_BANKS - 2:GROUP_BANKS, :].rearrange("p b (q d) -> p (b q) d", d=D)
        same_expert = sb("same_expert", [P, BLOCK, 2])
        choice = sb("choice", [P, BLOCK])
        out_row = sb("out_row", [P, RING], U32)

        bank = ctx.enter_context(nc.psum_tensor("bank", [P, 8, 512], F32))
        SC = bank[:, 0:4, :]
        MX = bank[:, 2:5, :]
        ST = bank[:, 4, 0:P]
        O = bank[:, 5, :]
        X = [bank[:, 6, :], bank[:, 7, :]]
        a_bank = {o[0]: X[n % 2] for n, o in enumerate(A_ORDER)}
        c_bank = {o[0]: X[n % 2] for n, o in enumerate(C_ORDER)}

        def tiles(ap):
            return ap.rearrange("p (t n) -> p t n", t=TB)

        consts_dma, x_dma, w_dma, bias_dma = map(sem, ("consts_dma", "x_dma", "w_dma", "bias_dma"))
        bucket_zeroed, rows_zeroed = sem("bucket_zeroed"), sem("rows_zeroed")
        consts_ready, zeros_ready = sem("consts_ready"), sem("zeros_ready")
        wT_full, wT_copied, weights_ready = sem("wT_full"), sem("wT_copied"), sem("weights_ready")
        var1_ready, pow1_ready, ln1_ready = sem("var1_ready"), sem("pow1_ready"), sem("ln1_ready")
        dve_chain, pool_chain = sem("dve_chain"), sem("pool_chain")

        def sems(n, *names):
            return {s: sem(f"{s}_{n}") for s in names}

        both = ("xn_ready", "xt_full", "xnT_ready", "proj_full", "split_ready", "parts_written",
                "score_full", "probs_ready", "pv_done", "o_copied", "wo_full", "residual_ready")
        sa = sems("a", *both, "vpad_ready", "rope_ready", "v_ready", "max_full", "max_done", "negm_ready",
                  "mt_full", "high_ready",
                  "mparts_ready", "mrows_loaded", "den_full", "den_read", "recip_ready", "out_full", "attn_ready")
        sc_ = sems("c", *both, "nexp_ready", "q_ready", "k_ready", "high_ready", "kn_ready", "kvn_ready", "state_full",
                   "state_ready", "vext_cleared", "var_ready", "pow_ready", "factors_ready", "ctx_full",
                   "ctx_ready", "rows_added", "bias_added")
        for s_, n in ((sa, "a"), (sc_, "c")):
            s_["stack_loaded"] = [sem(f"stack_loaded_{n}_{t}") for t in range(2)]
        sc_["stack_loaded"][1] = sc_["stack_loaded"][0]
        def routing_sems(n):
            return {s: sem(f"{s}_route_{n}") for s in (
                "var_ready", "pow_ready", "factors_ready", "xn_ready", "xt2_full", "xn2T_ready", "logit_full",
                "topd_ready", "tope_ready", "chosen_ready", "pos_full", "pos_read", "slot_ready")} | {
                "scattered": [sem(f"scattered_{n}_{j}") for j in range(2)]}

        def expert_sems(n):
            return {s: sem(f"{s}_{n}") for s in (
                "xbt_full", "xbt_ready", "hrow_full", "hrow_ready", "h_full", "hpre_ready", "h_ready", "y_full",
                "y_ready")} | {
                "y_scattered": [sem(f"y_scattered_{n}_{j}") for j in range(2)],
                "landed": [sem(f"landed_{n}_{r}") for r in range(RING)],
                "block_landed": [sem(f"block_landed_{n}_{z}") for z in range(RING // BLOCK)]}

        ra, rc, eb, ed = routing_sems("a"), routing_sems("c"), expert_sems("b"), expert_sems("d")
        final_ready, out_stored = map(sem, ("final_ready", "out_stored"))
        rows_loaded, final_loaded = ([sem(f"{s}_{j}") for j in range(2)] for s in ("rows_loaded", "final_loaded"))

        x_v = x.rearrange("b (t p) d -> p (b t) d", p=P)
        out_v = out.rearrange("b (t p) d -> p (b t) d", p=P)
        w1_v = w1.rearrange("e d h -> d e h")
        w2_v = w2.rearrange("e (p c) d -> p e c d", c=HC)
        b2_v = b2.rearrange("(q t) d -> t q d", t=2)
        bucket_v = [t.rearrange("(q p) d -> p q d", p=P) for t in bucket_d]
        y_v = y_d.rearrange("(n p k) d -> p n (k d)", p=P, k=K)

        A_READERS = {"den": (sa["den_read"], 1, 1), "mt1": (sa["mparts_ready"], 2, 2), "xt": (sa["xnT_ready"], 1, 1),
                     "q": (sa["rope_ready"], 4, 1), "qr": (sa["rope_ready"], 4, 2), "out": (sa["attn_ready"], 1, 1),
                     "wo": (sa["residual_ready"], 1, 1), "k": (sa["rope_ready"], 4, 3), "kr": (sa["rope_ready"], 4, 4),
                     "v": (sa["v_ready"], 1, 1), "xt2": (ra["xn2T_ready"], 1, 1), "mt0": (sa["mparts_ready"], 2, 1),
                     "lg": (ra["chosen_ready"], 1, 1), "pos": (ra["pos_read"], 1, 1)}
        C_READERS = {"ctx": (sc_["ctx_ready"], 1, 1), "xt": (sc_["xnT_ready"], 1, 1), "wo": (sc_["residual_ready"], 1, 1),
                     "n": (sc_["nexp_ready"], 1, 1), "kt": (sc_["kn_ready"], 1, 1),
                     "vt": (sc_["kvn_ready"], 1, 1), "q": (sc_["q_ready"], 1, 1), "k": (sc_["k_ready"], 1, 1),
                     "xt2": (rc["xn2T_ready"], 1, 1), "lg": (rc["chosen_ready"], 1, 1), "pos": (rc["pos_read"], 1, 1)}
        PAIR_DMAS = 2
        BLOCK_DMAS = 3
        MROW_DMAS = 2 * HG
        STACK_DMAS = 2 * len(Q_ROWS)
        BIAS_DMAS = 2 + DH + 4 + 1
        BUCKET_ZERO_DMAS = 2

        def masked(u):
            return probs[:, u % (2 * QG), :]

        block = ctx.enter_context(nc.Block())

        @block.sync
        def _(sp):
            for dst, src in ((w_in[:, 0, :], Wq), (w_in[:, 1, :], Wk), (w_in[:, 2, :], Wv), (w_in[:, 3, :], Wo)):
                sp.dma_start(dst, src).then_inc(w_dma, 16)
            sp.dma_start(xres[:, :, :], x_v).then_inc(x_dma, 16)
            for dst, src in ((cossin[:, 0, :], cosT), (cossin[:, 1, :], sinT), (wq2_s[:, :], Wqk[:, 0:P]),
                             (wkv_s[:, 0:P], Wqk[:, P:2 * P]), (wkv_s[:, P:2 * P], bWv), (wo2_s[:, :], bWo),
                             (wn_in[:, :], Wn), (gate_ws[:, :], gate_w)):
                sp.dma_start(dst, src).then_inc(consts_dma, 16)
            for t in range(2):
                sp.dma_start(bq_s[:, t:t + 1], bqk[t * P:(t + 1) * P].rearrange("(p o) -> p o", o=1)) \
                    .then_inc(bias_dma, 16)
            for j in range(DH):
                sp.dma_start(bn_s[j:P:DH, 0:1], bn.rearrange("(h o) -> h o", o=1)).then_inc(bias_dma, 16)
            for dst, src in ((bkv_s[:, 0:P], bqk[P:2 * P]), (bkv_s[:, P:2 * P], bv), (bo_s[:, :], bo),
                             (gate_bs[:, :], gate_b)):
                sp.dma_start(dst, src.unsqueeze(0).to_broadcast([P, src.shape[0]])).then_inc(bias_dma, 16)
            sp.dma_start(b1_s[:, :, :], b1.rearrange("e (p c) -> p e c", c=HC)).then_inc(bias_dma, 16)
            sp.wait_ge(zeros_ready, 1)
            for t in bucket_d:
                sp.dma_start(t.rearrange("(p r) d -> p r d", p=P), zeros[:, :].unsqueeze(1)
                             .to_broadcast([P, E * CAP // P, WIDTH])).then_inc(bucket_zeroed, 16)

            def zero_rows(b):
                sp.dma_start(y_d.rearrange("(b p r) d -> p b r d", p=P, r=TB * K)[:, bass.ds(b, 1), :, :]
                             .rearrange("p b r d -> p (b r) d"),
                             zeros[:, 0:D].unsqueeze(1).to_broadcast([P, TB * K, D])).then_inc(rows_zeroed, 16)

            def load_rows(b, par, loaded):
                sp.dma_start(yrows[par][:, :, :].rearrange("p (n k) d -> p n (k d)", k=K),
                             y_v[:, bass.ds(b * TB, TB), :]).then_inc(loaded[par], 16)

            def load_weights(e, q, r):
                sp.dma_start(w1_s[r], w1_v[:, bass.ds(q * 2, 2), :]).then_inc(e["landed"][r], 16)
                sp.dma_start(w2_s[r], w2_v[:, bass.ds(q * 2, 2), :, :]).then_inc(e["landed"][r], 16)

            def load_block(e, bucket, q, z):
                at = slice(z * BLOCK, (z + 1) * BLOCK)
                sp.dma_start(xb_s[:, at, :], bucket[:, bass.ds(q, BLOCK), :]).then_inc(e["block_landed"][z], 16)
                for t in range(2):
                    sp.dma_start(b2_s[CAP * t:CAP * (t + 1), at, :], b2_v[t][bass.ds(q, BLOCK), :].unsqueeze(0)
                                 .to_broadcast([CAP, BLOCK, D])).then_inc(e["block_landed"][z], 16)

            def write_parts(s, b, par, n):
                sp.wait_ge(s["split_ready"], b * 2 + n + 1)
                sp.dma_start(parts_d[par][n].rearrange("g p s -> p g s"), parts[n][:, :, :]) \
                    .then_inc(s["parts_written"], 16)

            def load_stacks(s, par, t):
                for n, rows_ in enumerate((Q_ROWS, K_ROWS)):
                    src = parts_d[par][n].rearrange("g (t a d) s -> g t d a s", t=2, d=DH)
                    for g, part in enumerate(rows_):
                        at = 64 * t + DH * g
                        sp.dma_start((qstk, kstk)[n][par][at:at + DH, :, :], src[part, t]) \
                            .then_inc(s["stack_loaded"][t], 16)

            def maxima_rows(b, par, half, parts_of=None):
                sp.wait_ge(sa["mparts_ready"], b * 2 + half + 1)
                for j in range(HG):
                    for part in range(2):
                        if (j, part) == (HG - 1, 1) and parts_of is not None:
                            sp.wait_ge(sa["parts_written"], (parts_of + 1) * 32)
                        p0, col = place_of(HG * half + j)
                        sp.dma_start(qstk[par][p0 + KR + part:p0 + KR + part + 1, col, :],
                                     mparts[j:j + 1, part, :]).then_inc(sa["mrows_loaded"], 16)

            def a_body(it, par, on):
                a, b, c = it, it - 1, it - 2
                if on[1]:
                    wait(sp, sa["score_full"], (b - 1) * BANKS)
                    load_stacks(sa, 1 - par, 1)
                if on[2]:
                    maxima_rows(c, par, 1)
                if on[0]:
                    zero_rows(a)
                    write_parts(sa, a, par, 0)
                    write_parts(sa, a, par, 1)
                if on[1]:
                    maxima_rows(b, 1 - par, 0, a if on[0] else None)
                elif on[0]:
                    sp.wait_ge(sa["parts_written"], (a + 1) * 32)
                if on[0]:
                    wait(sp, sa["score_full"], (a - 2) * BANKS + BANKS // 2)
                    load_stacks(sa, par, 0)

            def c_body(it, par, on):
                b = it - 1
                if on[0]:
                    wait(sp, sc_["var_ready"], it)
                    load_rows(it + 1, 1 - par, rows_loaded)
                if on[1]:
                    write_parts(sc_, b, 1 - par, 0)
                    write_parts(sc_, b, 1 - par, 1)
                    sp.wait_ge(sc_["parts_written"], (b + 1) * 32)
                    for t in range(2):
                        load_stacks(sc_, 1 - par, t)

            def expert_phase(e, attention, stacks_free, scattered, bucket):
                for q in range(RING // 2):
                    load_weights(e, q, q)
                attention()
                sp.wait_ge(*stacks_free)
                for q in range(RING // 2, RING):
                    load_weights(e, q, q)
                for t in scattered:
                    sp.wait_ge(t, B // 2 * TB * K * 16)
                for z in range(RING // BLOCK):
                    load_block(e, bucket, z * BLOCK, z)
                with sp.Fori(0, PAIRS // RING - 1) as i:
                    for r in range(RING):
                        q = i * RING + r
                        sp.wait_ge(e["y_ready"], q + 1)
                        load_weights(e, q + RING, r)
                        if r % BLOCK == BLOCK - 1:
                            load_block(e, bucket, q + (RING - BLOCK + 1), r // BLOCK)
                for j in range(2):
                    sp.wait_ge(e["y_scattered"][j], PAIRS // 2 * 16)

            zero_rows(B)
            expert_phase(eb, lambda: over_batches(sp, 4, a_body), (sa["score_full"], B * BANKS),
                         ra["scattered"], bucket_v[0])
            load_rows(0, 0, rows_loaded)
            expert_phase(ed, lambda: over_batches(sp, 4, c_body), (sc_["score_full"], B * H),
                         rc["scattered"], bucket_v[1])

            def store_out(b):
                sp.wait_ge(final_ready, b + 1)
                sp.dma_start(out_v[:, bass.ds(b * TB, TB), :], xres[:, bass.ds(b * TB, TB), :]).then_inc(out_stored, 16)

            for b in range(2):
                load_rows(b, b, final_loaded)
            with sp.Fori(0, B // 2 - 1) as i:
                for par in range(2):
                    store_out(i * 2 + par)
                    load_rows(i * 2 + (par + 2), par, final_loaded)
            for b in range(B - 2, B):
                store_out(b)
            sp.wait_ge(out_stored, B * 16)

        @block.gpsimd
        def _(pool):
            link = Chain(pool, pool_chain)

            def select(t, pattern, op, fill, base=0, cm=1):
                link(nc.gpsimd.affine_select(out=t, in_=t, pattern=pattern, compare_op=op, fill=fill, base=base,
                                             channel_multiplier=cm))

            nc.gpsimd.memset(zeros[:, :], 0.0).then_inc(zeros_ready, 1)
            for t in vext:
                nc.gpsimd.memset(t[:, :, :, :], 1.0)
            nc.gpsimd.memset(sel_o[:, :], 0.0)
            nc.gpsimd.memset(sel_d[:, :], 0.0)
            nc.gpsimd.memset(minus_half[:, :], -0.5)
            nc.gpsimd.iota(token_no[:, :], pattern=[[K * P, NT]], base=-int(FAR), channel_multiplier=K,
                           allow_small_or_imprecise_dtypes=True)
            nc.gpsimd.iota(row_expert[:, :], pattern=[[2, PAIRS]], base=0, channel_multiplier=0,
                           allow_small_or_imprecise_dtypes=True)
            nc.gpsimd.memset(ident[:, :], 0.0)
            nc.gpsimd.memset(ident_b[:, :], 0.0)
            nc.gpsimd.memset(mask_q[:, :], 0.0)
            nc.gpsimd.memset(mask_k[:, :], 0.0)
            nc.gpsimd.memset(keep_k[:, :], 1.0)
            nc.gpsimd.memset(same_head[:, :], 1.0)
            nc.gpsimd.memset(before[:, :], 1.0)
            nc.gpsimd.memset(count[:, :], 0.0)
            nc.gpsimd.memset(kstk[0][:, :, :], 1.0)
            nc.gpsimd.memset(kstk[1][:, :, :], 1.0)
            nc.gpsimd.iota(expert_no[:, :], pattern=[[1, E]], base=0, channel_multiplier=0,
                           allow_small_or_imprecise_dtypes=True)
            link(nc.gpsimd.memset(ones_b[:, :], 1.0))
            select(ident[:, :], [[-1, P]], ALU.not_equal, 1.0)
            select(ident_b[:, :], [[-1, P]], ALU.not_equal, 1.0)
            select(mask_q[:, :], [[-1, P]], ALU.is_ge, NEG)
            select(mask_k[:, :], [[1, P]], ALU.is_ge, NEG, cm=-1)
            select(keep_k[:, :], [[1, P]], ALU.is_ge, 0.0, cm=-1)
            select(same_head[:, :].rearrange("p (h d) -> p h d", d=DH), [[-DH, H], [0, DH]], ALU.is_ge, 0.0)
            select(same_head[:, :].rearrange("p (h d) -> p h d", d=DH), [[DH, H], [0, DH]], ALU.is_ge, 0.0,
                   base=DH - 1, cm=-1)
            select(before[:, :], [[1, P]], ALU.is_gt, 0.0, cm=-1)
            for t, base in ((sel_o, 0), (sel_d, -DH)):
                select(t[:, :].rearrange("p (j d) -> p j d", d=DH), [[-32, QG], [-1, DH]], ALU.not_equal, 1.0, base=base)
            nc.gpsimd.memset(snwt[0][:, :], 0.0).then_inc(consts_ready, 1)
            pool.wait_ge(var1_ready, 1)
            nc.gpsimd.tensor_tensor(rstd1[:, :], var1[:, :], minus_half[:, :], ALU.pow).then_inc(pow1_ready, 1)

            def split(n, s, b):
                high, src = parts[n][:, 0, :], rope[n][:, 0, :]
                wait(pool, s["parts_written"], b * 32)
                pool.wait_ge(s["rope_ready"], b * 4 + 2 * n + 2)
                nc.gpsimd.tensor_tensor(high, rope[n][:, 0, :], rope[n][:, 1, :], ALU.add)
                link(nc.gpsimd.tensor_tensor(src, rope[n][:, 0, :], rope[n][:, 1, :], ALU.add))
                split_rest(n, s, src)

            def split_rest(n, s, src):
                high, mid, low = (parts[n][:, j, :] for j in range(NPARTS))
                rest = rope[n][:, 1, :]
                nc.gpsimd.tensor_tensor(mid, src, high, ALU.subtract)
                link(nc.gpsimd.tensor_tensor(rest, src, high, ALU.subtract))
                nc.gpsimd.tensor_tensor(low, rest, mid, ALU.subtract).then_inc(s["split_ready"], 1)

            def fence():
                n = next(pool_columns)
                return nc.gpsimd.tensor_tensor(pool_scratch[:, n:n + 1], minus_half[:, 0:1], minus_half[:, 0:1], ALU.mult)

            def power(n, ready, done, b):
                pool.wait_ge(ready, b + 1)
                nc.gpsimd.tensor_tensor(spow[n][:, :], svar[n][:, :], minus_half[:, 0:TB], ALU.pow).then_inc(done, 1)

            def scatter_before(r, it, par, bucket):
                if not isinstance(it, int) or 0 <= it - 4 < B:
                    scatter(r, it - 4, par, bucket)

            def scatter(r, d, dp, bucket):
                pool.wait_ge(r["slot_ready"], d + 1)
                fence()
                for t in range(TB):
                    for k in range(K):
                        j = t * K + k
                        nc.gpsimd.indirect_dma_start(
                            bucket[:, :], bass.IndirectOffsetOnAxis(ap=slot_u[dp][:, j:j + 1], axis=0),
                            xn2[dp][:, t, :], None, bounds_check=E * CAP - 1, oob_is_err=False) \
                            .then_inc(r["scattered"][dp], 16)

            def expert_phase(e):
                def turn(p, r, par, on):
                    if on[3]:
                        q, at = p - 3, (r - 3) % RING
                        link.settle()
                        pool.wait_ge(e["y_ready"], q + 1)
                        link.mark(fence())
                        nc.gpsimd.indirect_dma_start(
                            y_d[:, :], bass.IndirectOffsetOnAxis(ap=out_row[:, at:at + 1], axis=0),
                            y_s[:, 1 - par, :], None, bounds_check=ROWS - 1, oob_is_err=False).then_inc(e["y_scattered"][1 - par], 16)
                over_pairs(pool, turn, link, RING)

            def a_body(it, par, on):
                a, b, d = it, it - 1, it - 3
                if on[1]:
                    pool.wait_ge(sa["v_ready"], b + 1)
                    wait(pool, sa["pv_done"], (b - 1) * len(PV_STEPS) * GROUPS)
                    fence()
                    nc.gpsimd.tensor_copy(vext[1 - par][:, :, :, 0:DH],
                                          v_s[:, :, :].rearrange("p t (h d) -> p t h d", d=DH)) \
                        .then_inc(sa["vpad_ready"], 1)
                if on[0]:
                    split(0, sa, a)
                if on[3]:
                    power(0, ra["var_ready"], ra["pow_ready"], d)
                if on[0]:
                    split(1, sa, a)
                scatter_before(ra, it, par, bucket_d[0])

            pool.wait_ge(bucket_zeroed, BUCKET_ZERO_DMAS * 16)
            over_batches(pool, 4, a_body, link, 8)
            scatter(ra, B - 1, (B - 1) % 2, bucket_d[0])

            pool.wait_ge(sa["pv_done"], B * len(PV_STEPS) * GROUPS)
            nc.gpsimd.memset(count[:, :], 0.0)
            nc.gpsimd.memset(vext[0][:, :, :, :], 0.0)
            nc.gpsimd.memset(vext[1][:, :, :, :], 0.0).then_inc(sc_["vext_cleared"], 1)
            pool.wait_ge(rows_zeroed, (B + 1) * 16)
            expert_phase(eb)

            def c_body(it, par, on):
                a, b, c, d = it, it - 1, it - 2, it - 3
                if on[3]:
                    power(0, rc["var_ready"], rc["pow_ready"], d)
                if on[1]:
                    for n, src in ((0, qs[1 - par]), (1, rope[1][:, 0, :])):
                        pool.wait_ge(sc_["high_ready"], b * 2 + n + 1)
                        split_rest(n, sc_, src)
                if on[0]:
                    power(1, sc_["var_ready"], sc_["pow_ready"], a)
                if on[2]:
                    pool.wait_ge(sc_["xn_ready"], c + 1)
                    xt = xres[:, bass.ds(c * TB, TB), :]
                    nc.gpsimd.tensor_tensor(xt, xt, bo_s[:, :].unsqueeze(1).to_broadcast([P, TB, D]), ALU.add) \
                        .then_inc(sc_["bias_added"], 1)
                scatter_before(rc, it, par, bucket_d[1])

            over_batches(pool, 4, c_body, link, 4)
            scatter(rc, B - 1, (B - 1) % 2, bucket_d[1])
            pool.wait_ge(rows_loaded[0], (B // 2 + 1) * 16)
            expert_phase(ed)

        @block.scalar
        def _(act):
            act.wait_ge(wT_full, 1)
            turned = tiles(X[0])
            nc.scalar.activation(wT[:, 0, :], turned[:, 0, :], ACT.Copy)
            nc.scalar.activation(wT[:, 2, :], turned[:, 1, :], ACT.Copy)
            nc.scalar.activation(wT[:, 4:6, :], turned[:, 2:4, :], ACT.Copy).then_inc(wT_copied, 1)

            def evacuate(dst, src, full, count_, done):
                act.wait_ge(full, count_)
                nc.scalar.activation(dst, src, ACT.Copy).then_inc(done, 1)

            def take_out(s, n, steps, g, reads):
                act.wait_ge(s["pv_done"], steps)
                wait(act, *reads)
                nc.scalar.activation(o_s[:, g, :], O, ACT.Copy).then_inc(s["o_copied"], 1)

            def transposed_again(r, banks, d):
                evacuate(xn2T[:, :], banks["xt2"], r["xt2_full"], d + 1, r["xn2T_ready"])

            def normalise(dst, tile0, factor, offset):
                for t in range(TB):
                    last = nc.scalar.activation(dst[:, t, 0:D], flat(xres[:, bass.ds(tile0 + t, 1), :]), ACT.Identity,
                                                scale=factor(t), bias=offset(t))
                return last

            def normalise_again(r, d, dp):
                act.wait_ge(r["factors_ready"], d + 1)
                wait(act, r["scattered"][dp], (d - dp) * (TB * K * 16 // 2))
                normalise(xn2[dp], d * TB, lambda t: spow[0][:, t:t + 1], lambda t: smean[0][:, t:t + 1]) \
                    .then_inc(r["xn_ready"], 1)

            def gate_exp(r, d):
                act.wait_ge(r["topd_ready"], d + 1)
                nc.scalar.activation(tope[:, :, :], topd[:, :, :], ACT.Exp).then_inc(r["tope_ready"], 1)

            def a_body(it, par, on):
                a, b, c, d = it, it - 1, it - 2, it - 3
                steps = {u: (name, stage) for name, u, stage in A_ORDER}
                for u in range(BANKS):
                    g, j = divmod(u, GROUP_BANKS)
                    if on[2]:
                        act.wait_ge(sa["score_full"], c * BANKS + u + 1)
                        wait(act, sa["pv_done"], (c * GROUPS + g - 1) * len(PV_STEPS) + PV_OF_BANK[j])
                        nc.scalar.activation(probs[:, j, :], SC[:, u % 2, :], ACT.Exp, scale=SCALE) \
                            .then_inc(sa["probs_ready"], 1)
                        if g and j == 3:
                            take_out(sa, c * GROUPS + g - 1, (c * GROUPS + g) * len(PV_STEPS), g - 1,
                                     (sa["out_full"], c))
                    if u == 0 and on[0]:
                        wait(act, sa["xt_full"], a)
                        t0 = a * TB
                        normalise(xn, t0, lambda t: rstd1[:, bass.ds(t0 + t, 1)],
                                  lambda t: mean1[:, bass.ds(t0 + t, 1)]) \
                            .then_inc(sa["xn_ready"], 1)
                    if u == 19 and on[3]:
                        normalise_again(ra, d, 1 - par)
                    if u == 31 and on[3]:
                        gate_exp(ra, d)
                    name, stage = steps.get(u, (None, 0))
                    if not on[stage]:
                        continue
                    if name == "den":
                        wait(act, sa["recip_ready"], d * 4)
                        evacuate(den_s[:, :], a_bank["den"], sa["den_full"], d + 1, sa["den_read"])
                    if name in ("mt1", "mt0"):
                        n = c * 2 + 1 if name == "mt1" else b * 2
                        act.wait_ge(sa["mt_full"], n + 1)
                        wait(act, sa["mrows_loaded"], n * MROW_DMAS * 16)
                        nc.scalar.activation(mparts[:, 0, :], a_bank[name][0:HG, :], ACT.Copy) \
                            .then_inc(sa["high_ready"], 1)
                    if name == "xt":
                        evacuate(xnT[:, :], a_bank["xt"], sa["xt_full"], a + 1, sa["xnT_ready"])
                    if name == "v":
                        wait(act, sa["vpad_ready"], a)
                        evacuate(v_s[:, :, :], tiles(a_bank["v"]), sa["proj_full"], a * 5 + 5, sa["v_ready"])
                    if name == "xt2":
                        transposed_again(ra, a_bank, d)
                if on[2]:
                    take_out(sa, c * GROUPS + GROUPS - 1, (c + 1) * GROUPS * len(PV_STEPS), GROUPS - 1,
                             (sa["out_full"], c))

            act.wait_ge(ln1_ready, 1)
            over_batches(act, 4, a_body)

            def expert_phase(e):
                def turn(p, r, par, on):
                    if on[0]:
                        act.wait_ge(e["xbt_full"], p + 1)
                        nc.scalar.activation(xbT[:, par, :], bank[:, par, 0:P], ACT.Copy).then_inc(e["xbt_ready"], 1)
                    if on[1]:
                        act.wait_ge(e["hrow_full"], p)
                        nc.scalar.activation(hrow[:, 1 - par, :], bank[:, 2 + (1 - par), :], ACT.Copy) \
                            .then_inc(e["hrow_ready"], 1)
                    if on[2]:
                        act.wait_ge(e["hpre_ready"], p - 1)
                        wait(act, e["y_full"], p - 3)
                        nc.scalar.activation(hact[:, par, :, :, :], hpre[:, par, :, :, :], ACT.Gelu) \
                            .then_inc(e["h_ready"], 1)
                over_pairs(act, turn)

            expert_phase(eb)

            def c_body(it, par, on):
                a, b, c, d = it, it - 1, it - 2, it - 3
                steps = {u: (name, stage) for name, u, stage in C_ORDER}
                for u in range(H):
                    g, j = divmod(u, QG)
                    if on[2] and g and j == 3:
                        take_out(sc_, c * GROUPS + g - 1, c * GROUPS + g, g - 1, (sc_["ctx_full"], c))
                    if on[3] and u == 13:
                        gate_exp(rc, d)
                    if on[3] and u == 7:
                        normalise_again(rc, d, 1 - par)
                    if on[0] and u == 13:
                        act.wait_ge(sc_["factors_ready"], a + 1)
                        wait(act, sc_["xt_full"], a)
                        normalise(xn, a * TB, lambda t: spow[1][:, t:t + 1], lambda t: smean[1][:, t:t + 1]) \
                            .then_inc(sc_["xn_ready"], 1)
                    if on[1] and u == 4:
                        wait(act, sc_["parts_written"], b * 32)
                        act.wait_ge(sc_["q_ready"], b + 1)
                        nc.scalar.activation(parts[0][:, 0, :], qs[1 - par], ACT.Copy).then_inc(sc_["high_ready"], 1)
                    name, stage = steps.get(u, (None, 0))
                    if not on[stage]:
                        continue
                    if name == "ctx":
                        wait(act, sc_["wo_full"], d)
                        evacuate(attnT[:, :], c_bank["ctx"], sc_["ctx_full"], d + 1, sc_["ctx_ready"])
                    if name == "xt":
                        evacuate(xnT[:, :], c_bank["xt"], sc_["xt_full"], a + 1, sc_["xnT_ready"])
                    if name == "n":
                        act.wait_ge(sc_["proj_full"], b * 5 + 1)
                        wait(act, sc_["q_ready"], b)
                        nc.scalar.activation(nexp[:, :], c_bank["n"], ACT.Exp, scale=-1.0, bias=bn_s[:, 1:2]) \
                            .then_inc(sc_["nexp_ready"], 1)
                    if name == "k":
                        act.wait_ge(sc_["proj_full"], b * 5 + 3)
                        nc.scalar.activation(rope[1][:, 0, :], c_bank["k"], ACT.Identity, bias=bq_s[:, 1:2]) \
                            .then_inc(sc_["k_ready"], 1)
                        act.wait_ge(sc_["k_ready"], b + 1)
                        nc.scalar.activation(parts[1][:, 0, :], rope[1][:, 0, :], ACT.Copy).then_inc(sc_["high_ready"], 1)
                    if name == "xt2":
                        transposed_again(rc, c_bank, d)
                if on[2]:
                    take_out(sc_, c * GROUPS + GROUPS - 1, (c + 1) * GROUPS, GROUPS - 1, (sc_["ctx_full"], c))

            over_batches(act, 4, c_body)
            expert_phase(ed)

        @block.vector
        def _(dve):
            link = Chain(dve, dve_chain)
            tt, ts, stt = nc.vector.tensor_tensor, nc.vector.tensor_scalar, nc.vector.scalar_tensor_tensor

            def refine(y, v, t):
                link(tt(t, y, y, ALU.mult))
                link(tt(t, t, v, ALU.mult))
                link(ts(t, t, -0.5, 1.5, ALU.mult, ALU.add))
                return tt(y, y, t, ALU.mult)

            nc.vector.memset(svar[0][:, :], 0.0)
            nc.vector.memset(svar[1][:, :], 0.0)
            dve.wait_ge(x_dma, 16)
            for t in range(NT):
                last = nc.vector.bn_stats(bn6[:, t, :], xres[:, t, :])
            link(last)
            for t in range(NT):
                last = nc.vector.bn_aggr(stat1[:, t, :], bn6[:, t, :])
            link(last)
            ts(var1[:, :], stat1[:, :, 1], EPS, None, ALU.add).then_inc(var1_ready, 1)
            dve.wait_ge(wT_copied, 1)
            for n in (0, 2):
                for t in range(2):
                    last = nc.vector.tensor_copy(
                        wT[:, n + 1, :].rearrange("p (h t d) -> p h t d", t=2, d=DH // 2)[:, :, t, :],
                        wT[:, n, :].rearrange("p (h t d) -> p h t d", t=2, d=DH // 2)[:, :, 1 - t, :])
            dve.wait_ge(consts_dma, 8 * 16)
            dve.wait_ge(bias_dma, BIAS_DMAS * 16)
            ts(bn_s[:, 1:2], bn_s[:, 0:1], -1.0, None, ALU.mult)
            nc.vector.tensor_copy(wn_s[:, :].rearrange("p (h d) -> p h d", d=DH),
                                  wn_in[:, :].unsqueeze(2).to_broadcast([P, H, DH])).then_inc(weights_ready, 1)
            dve.wait_ge(pow1_ready, 1)
            dve.wait_ge(consts_ready, 1)
            ts(row_expert[CAP:P, :], row_expert[CAP:P, :], 1.0, None, ALU.add)
            link(refine(rstd1[:, :], var1[:, :], nwt1[:, :]))
            stt(mean1[:, :], stat1[:, :, 0], -1.0, rstd1[:, :], ALU.mult, ALU.mult).then_inc(ln1_ready, 1)

            def fence():
                n = next(dve_columns)
                nc.vector.tensor_copy(dve_scratch[:, n:n + 1], ident[:, 0:1])

            def statistics(n, tile0):
                fence()
                for t in range(TB):
                    last = nc.vector.bn_stats(st6[n][:, t, :], flat(xres[:, bass.ds(tile0 + t, 1), :]))
                link(last)
                fence()
                for t in range(TB):
                    last = nc.vector.bn_aggr(st2[n][:, t, :], st6[n][:, t, :])
                link(last)
                return ts(svar[n][:, :], st2[n][:, :, 1], EPS, None, ALU.add)

            def norm_factors(n, s, b):
                dve.wait_ge(s["pow_ready"], b + 1)
                wait(dve, s["xn_ready"], b)
                link(refine(spow[n][:, :], svar[n][:, :], snwt[n][:, :]))
                stt(smean[n][:, :], st2[n][:, :, 0], -1.0, spow[n][:, :], ALU.mult, ALU.mult) \
                    .then_inc(s["factors_ready"], 1)

            def choose(r, banks, d):
                dve.wait_ge(r["logit_full"], d + 1)
                link(tt(logit[:, :, :], banks["lg"][:, 0:TB * E].rearrange("p (t e) -> p t e", e=E),
                        gate_bs[:, :].unsqueeze(1).to_broadcast([P, TB, E]), ALU.add))
                fence()
                for t in range(TB):
                    last = nc.vector.max(top8[:, t, :], logit[:, t, :])
                link(last)
                tt(topd[:, :, :], top8[:, :, 0:K], top8[:, :, 0:1].to_broadcast([P, TB, K]), ALU.subtract) \
                    .then_inc(r["topd_ready"], 1)
                for t in range(TB):
                    last = nc.vector.max_index(idx8[:, t, :], top8[:, t, :], logit[:, t, :])
                link(last)

            def mark_chosen(r, d, dp):
                link(nc.vector.tensor_copy(topi[dp], idx8[:, :, 0:K]))
                for k in range(K):
                    last = tt(onehot[:, k, :, :], expert_no[:, :].unsqueeze(1).to_broadcast([P, TB, E]),
                              topi[dp][:, :, k:k + 1].to_broadcast([P, TB, E]), ALU.is_equal)
                link(last)
                link(tt(ptmp[:, 0, :, :], onehot[:, 0, :, :], onehot[:, 1, :, :], ALU.add))
                tt(chosen[:, :, :], ptmp[:, 0, :, :], onehot[:, 2, :, :], ALU.add).then_inc(r["chosen_ready"], 1)

            def find_positions(r, banks, d, dp):
                nc.vector.tensor_copy(xn2[dp][:, :, D], token_no[:, bass.ds(d * TB, TB)])
                dve.wait_ge(r["pos_full"], d + 1)
                pos_ps = banks["pos"][:, 0:TB * E].rearrange("p (t e) -> p t e", e=E)
                for k in range(K):
                    last = tt(ptmp[:, k, :, :], onehot[:, k, :, :], pos_ps, ALU.mult)
                last.then_inc(r["pos_read"], 1)
                dve.wait_ge(r["pos_read"], d + 1)
                for k in range(K):
                    last = nc.vector.reduce_sum(pos[:, :, k], ptmp[:, k, :, :], AX.X)
                link(last)

            def find_slots(r, n, d, dp):
                dve.wait_ge(r["tope_ready"], d + 1)
                link(nc.vector.reduce_sum(esum[:, :], tope[:, :, :], AX.X))
                link(nc.vector.reciprocal(esum[:, :], esum[:, :]))
                link(tt(tope[:, :, :], tope[:, :, :], esum[:, :].unsqueeze(2).to_broadcast([P, TB, K]), ALU.mult))
                link(nc.vector.reduce_sum(csum[:, :], chosen[:, :, :].rearrange("p t e -> p e t"), AX.X))
                link(tt(count[:, :], count[:, :], csum[:, :], ALU.add))
                ts(room[:, :, :], pos[:, :, :], float(CAP), None, ALU.is_lt)
                link(stt(slot[:, :, :], topi[dp], float(CAP), pos[:, :, :], ALU.mult, ALU.add))
                link(tt(gate_tab[n][:, bass.ds(d * TB, TB), :], tope[:, :, :], room[:, :, :], ALU.mult))
                link(ts(room[:, :, :], room[:, :, :], -OUT_OF_RANGE, OUT_OF_RANGE, ALU.mult, ALU.add))
                tt(slot_u[dp][:, :].rearrange("p (t k) -> p t k", k=K), slot[:, :, :], room[:, :, :], ALU.add) \
                    .then_inc(r["slot_ready"], 1)

            def reciprocals(d, n):
                if n == 0:
                    dve.wait_ge(sa["den_read"], d + 1)
                at = slice(n * P, (n + 1) * P)
                nc.vector.reciprocal(rden[:, at], den_s[:, at]).then_inc(sa["recip_ready"], 1)

            def maxima(b, k):
                dve.wait_ge(sa["max_full"], b * BANKS + k + 1)
                nc.vector.tensor_reduce(bmax[:, 4 * k:4 * k + 4], tiles(MX[:, max_bank(k)[0], :]), AX.X, ALU.max) \
                    .then_inc(sa["max_done"], 1)

            def join_maxima(it, half):
                dve.wait_ge(sa["max_done"], it * BANKS + 20 * (half + 1))
                wait(dve, sa["mt_full"], it * 2 + half)
                v = bmax[:, 80 * half:80 * half + 80].rearrange("p (r c) -> p r c", c=20)
                wide = v[:, :, 0:16].rearrange("p r (h c) -> p r h c", c=8)
                tail = v[:, :, 16:20].rearrange("p r (h c) -> p r h c", c=2)
                dst = negm[:, half, :, :].rearrange("p q (r h) -> p q r h", h=2)
                for q, src in ((3, wide[:, :, :, 0:4]), (0, wide[:, :, :, 4:5]), (2, wide[:, :, :, 5:8]), (1, tail)):
                    last = nc.vector.tensor_reduce(dst[:, q, :, :], src, AX.X, ALU.max, negate=True)
                last.then_inc(sa["negm_ready"], 1)

            def split_maxima(it, half):
                dve.wait_ge(sa["mt_full"], it * 2 + half + 1)
                dve.wait_ge(sa["high_ready"], it * 2 + half + 1)
                tt(mparts[:, 1, :], a_bank[("mt0", "mt1")[half]][0:HG, :], mparts[:, 0, :], ALU.subtract) \
                    .then_inc(sa["mparts_ready"], 1)

            def a_body(it, par, on):
                a, b, c, d = it, it - 1, it - 2, it - 3
                rope_slots = [u for name, u, _ in A_ORDER if name in ("q", "qr", "k", "kr")]
                for u in range(BANKS):
                    if u == 0 and on[2]:
                        join_maxima(c, 1)
                    if u == BANKS // 2 and on[1]:
                        join_maxima(b, 0)
                    if u in (1, 3, 5, 7) and on[3]:
                        reciprocals(d, u // 2)
                    if u == 4 and on[2]:
                        split_maxima(c, 1)
                    if u in rope_slots and on[0]:
                        j = rope_slots.index(u)
                        dve.wait_ge(sa["proj_full"], a * 5 + j + 1)
                        if j % 2 == 0:
                            wait(dve, sa["split_ready"], a * 2 + j // 2 - 1)
                        tt(rope[j // 2][:, j % 2, :], a_bank[("q", "qr", "k", "kr")[j]], cossin[:, j % 2, :], ALU.mult) \
                            .then_inc(sa["rope_ready"], 1)
                    if u == 10 and on[3]:
                        dve.wait_ge(sa["out_full"], d + 1)
                        dve.wait_ge(sa["recip_ready"], (d + 1) * 4)
                        wait(dve, sa["wo_full"], d)
                        tt(attnT[:, :], a_bank["out"], rden[:, :], ALU.mult).then_inc(sa["attn_ready"], 1)
                    if u == 13 and on[3]:
                        dve.wait_ge(sa["wo_full"], d + 1)
                        xt = xres[:, bass.ds(d * TB, TB), :]
                        tt(xt, tiles(a_bank["wo"]), xt, ALU.add).then_inc(sa["residual_ready"], 1)
                        dve.wait_ge(sa["residual_ready"], d + 1)
                        statistics(0, d * TB).then_inc(ra["var_ready"], 1)
                    if u == 17 and on[3]:
                        norm_factors(0, ra, d)
                    if u == 25 and on[1]:
                        split_maxima(b, 0)
                    if u == 28 and on[3]:
                        choose(ra, a_bank, d)
                    if u == 30 and on[3]:
                        mark_chosen(ra, d, 1 - par)
                    if u == 34 and on[3]:
                        find_positions(ra, a_bank, d, 1 - par)
                    if u == 36 and on[3]:
                        find_slots(ra, 0, d, 1 - par)
                    if on[1]:
                        maxima(b, u)

            over_batches(dve, 4, a_body, link, 2 * 21)

            def expert_phase(e):
                def turn(p, r, par, on):
                    if on[2]:
                        q = p - 2
                        dve.wait_ge(e["h_full"], q + 1)
                        wait(dve, e["h_ready"], q - 1)
                        tt(hpre[:, par, :, :, :].rearrange("p a c n -> p (a c) n"),
                           bank[:, 6 + par, :].rearrange("p (a n) -> p a n", n=CAP),
                           b1_s[:, bass.ds(q * 2, 2), :].rearrange("p a c -> p (a c)").unsqueeze(2)
                           .to_broadcast([P, 2 * HC, CAP]), ALU.add).then_inc(e["hpre_ready"], 1)
                    if on[3]:
                        q = p - 3
                        dve.wait_ge(e["y_full"], q + 1)
                        wait(dve, e["y_scattered"][1 - par], (q - (1 - par)) * 8)
                        tt(y_s[:, 1 - par, :], bank[:, 4 + (1 - par), 0:D],
                           b2_s[:, (r - 3) % RING, :], ALU.add).then_inc(e["y_ready"], 1)
                    if on[0] and r % BLOCK == 0:
                        z = r // BLOCK
                        at = slice(z * BLOCK, (z + 1) * BLOCK)
                        dve.wait_ge(e["block_landed"][z], (p - r) * (BLOCK_DMAS * 16 // RING) + BLOCK_DMAS * 16)
                        link(tt(same_expert[:, :, :], xb_s[:, at, D + 2:D + 4],
                                row_expert[:, bass.ds(p, BLOCK)].unsqueeze(2).to_broadcast([P, BLOCK, 2]), ALU.is_equal))
                        link(stt(choice[:, :], same_expert[:, :, 1], 2.0, same_expert[:, :, 0], ALU.mult, ALU.add))
                        link(stt(out_row[:, at], xb_s[:, at, D], FAR, choice[:, :], ALU.add, ALU.add))
                over_pairs(dve, turn, link, 3 * RING // BLOCK)

            expert_phase(eb)

            def add_rows(n, b, par, k):
                for t in range(TB):
                    xt = flat(xres[:, bass.ds(b * TB + t, 1), :])
                    last = stt(xt, yrows[par][:, t * K + k, :], flat(gate_tab[n][:, bass.ds(b * TB + t, 1), k:k + 1]),
                               xt, ALU.mult, ALU.add)
                return last

            dve.wait_ge(sc_["vext_cleared"], 1)

            def mask_scores(c, u):
                dve.wait_ge(sc_["score_full"], c * H + u + 1)
                wait(dve, sc_["pv_done"], c * GROUPS + u // QG - 1)
                tt(masked(u).rearrange("p (t n) -> p t n", n=P), SC[:, u % 4, :].rearrange("p (t n) -> p t n", n=P),
                   keep_k[:, :].unsqueeze(1).to_broadcast([P, TB, P]), ALU.mult).then_inc(sc_["probs_ready"], 1)

            def c_body(it, par, on):
                a, b, c, d = it, it - 1, it - 2, it - 3
                reads = {u + 1: name for name, u, _ in C_ORDER}
                for u in range(H):
                    if on[2]:
                        mask_scores(c, u)
                    if on[1] and reads.get(u) == "q":
                        dve.wait_ge(sc_["proj_full"], b * 5 + 2)
                        dve.wait_ge(sc_["nexp_ready"], b + 1)
                        wait(dve, sc_["ctx_full"], b - 1)
                        stt(qs[1 - par], c_bank["q"], bq_s[:, 0:1], nexp[:, :], ALU.add, ALU.mult) \
                            .then_inc(sc_["q_ready"], 1)
                    if on[3] and reads.get(u) == "wo":
                        dve.wait_ge(sc_["wo_full"], d + 1)
                        dve.wait_ge(sc_["bias_added"], d + 1)
                        xt = xres[:, bass.ds(d * TB, TB), :]
                        tt(xt, tiles(c_bank["wo"]), xt, ALU.add).then_inc(sc_["residual_ready"], 1)
                        dve.wait_ge(sc_["residual_ready"], d + 1)
                        statistics(0, d * TB).then_inc(rc["var_ready"], 1)
                    if on[1] and reads.get(u) == "kt":
                        dve.wait_ge(sc_["proj_full"], b * 5 + 4)
                        wait(dve, sc_["state_full"], b * 3)
                        tt(kn[:, :, :], tiles(c_bank["kt"]), bkv_s[:, 0:P].unsqueeze(1).to_broadcast([P, TB, P]),
                           ALU.add).then_inc(sc_["kn_ready"], 1)
                    if on[1] and reads.get(u) == "vt":
                        dve.wait_ge(sc_["proj_full"], b * 5 + 5)
                        wait(dve, sc_["pv_done"], (b - 1) * GROUPS)
                        tt(vext[1 - par][:, :, :, 0:DH], c_bank["vt"].rearrange("p (t h d) -> p t h d", t=TB, d=DH),
                           bkv_s[:, P:2 * P].rearrange("p (h d) -> p h d", d=DH).unsqueeze(1)
                           .to_broadcast([P, TB, H, DH]),
                           ALU.add).then_inc(sc_["kvn_ready"], 1)
                    if on[1] and C_ST < u < C_ST + TB:
                        j = u - C_ST - 1
                        dve.wait_ge(sc_["state_full"], b * 3 + j + 1)
                        tt(stm[1 - par][:, j, :], ST, same_head[:, :], ALU.mult).then_inc(sc_["state_ready"], 1)
                    if on[3] and u == 5:
                        norm_factors(0, rc, d)
                    if on[0] and u in C_ROWS:
                        k = C_ROWS.index(u)
                        if k == 0:
                            dve.wait_ge(rows_loaded[par], (a - par + 2) * 8)
                        if k > 0:
                            dve.wait_ge(sc_["rows_added"], a * (K - 1) + k)
                        last = add_rows(0, a, par, k)
                        if k < K - 1:
                            last.then_inc(sc_["rows_added"], 1)
                        else:
                            link(last)
                            statistics(1, a * TB).then_inc(sc_["var_ready"], 1)
                    if on[3] and reads.get(u) == "lg":
                        choose(rc, c_bank, d)
                    if on[0] and u == 12:
                        norm_factors(1, sc_, a)
                    if on[3] and u == 12:
                        mark_chosen(rc, d, 1 - par)
                    if on[3] and reads.get(u) == "pos":
                        find_positions(rc, c_bank, d, 1 - par)
                        find_slots(rc, 1, d, 1 - par)

            over_batches(dve, 4, c_body, link, 2 * 28)
            expert_phase(ed)

            def final(b, par):
                dve.wait_ge(final_loaded[par], (b - par + 2) * 8)
                for k in range(K - 1):
                    link(add_rows(1, b, par, k))
                add_rows(1, b, par, K - 1).then_inc(final_ready, 1)

            with dve.Fori(0, B // 2) as i:
                link.enter(i, 2 * (K - 1))
                for par in range(2):
                    final(i * 2 + par, par)
                link.leave(B // 2)

        @block.tensor
        def _(pe):
            mm = nc.tensor.matmul

            pe.wait_ge(consts_ready, 1)
            pe.wait_ge(w_dma, 4 * 16)
            for n in range(4):
                last = nc.tensor.transpose(tiles(X[0])[:, n, :], w_in[:, n, :], ident[:, :])
            last.then_inc(wT_full, 1)
            pe.wait_ge(wT_copied, 1)
            pe.wait_ge(weights_ready, 1)

            def turn_tiles(dst, src, ready, full, b):
                pe.wait_ge(ready, b + 1)
                for t in range(TB):
                    last = nc.tensor.transpose(tiles(dst)[:, t, :], src[:, t, 0:D], ident[:, :])
                last.then_inc(full, 1)

            def project(dst, s, w):
                mm(dst, w, xnT[:, :], start=True, stop=True).then_inc(s["proj_full"], 1)

            def tile_products(dst, w, srcT, width):
                for t in range(TB):
                    last = mm(dst[:, t * width:(t + 1) * width], srcT[:, t * P:(t + 1) * P], w, start=True, stop=True)
                return last

            def positions(dst, r, d):
                pe.wait_ge(r["chosen_ready"], d + 1)
                for t in range(TB):
                    o = dst[:, t * E:(t + 1) * E]
                    mm(o, ones_b[:, :], count[:, :], start=True, stop=False)
                    for j in range(t):
                        mm(o, ones_b[:, :], chosen[:, j, :], start=False, stop=False)
                    last = mm(o, before[:, :], chosen[:, t, :], start=False, stop=True)
                last.then_inc(r["pos_full"], 1)

            def scores(dst, left, right, head0, segments, rows_, mask, query_major):
                for n, (h, i, at, cols) in enumerate(segments):
                    p0, col = place_of(head0 + h)
                    lhs = left[p0:p0 + rows_, col, P * i:P * (i + 1)]
                    rhs = right[p0:p0 + rows_, col, 0:cols] if query_major else right[p0:p0 + rows_, col, P * i:S]
                    mm(dst[:, at:at + cols], lhs, rhs, start=(n == 0), stop=False, skip_group_check=True)
                diag = [at + cols - P if query_major else at for _, _, at, cols in segments]
                for a in diag:
                    last = mm(dst[:, a:a + P], ident_b[:, :], mask[:, :], start=False, stop=(a == diag[-1]),
                              skip_group_check=True)
                return last

            def claim(order, readers, it, on, name):
                found = step_before(order, it, on, name)
                if found:
                    (before_, _, stage), at = found
                    s, per, which = readers[before_]
                    pe.wait_ge(s, (at - stage) * per + which)

            def select_heads(dst, sel, full):
                for g in range(GROUPS):
                    last = mm(dst[32 * g:32 * g + 32, :], sel[:, :], o_s[:, g, :], start=True, stop=True)
                if full:
                    last.then_inc(full, 1)

            def turn_maxima(dst, b, half):
                pe.wait_ge(sa["negm_ready"], b * 2 + half + 1)
                for q in range(TB):
                    last = nc.tensor.transpose(dst[0:HG, q * P:(q + 1) * P], negm[:, half, q, :], ident[:, :])
                last.then_inc(sa["mt_full"], 1)

            def a_body(it, par, on):
                a, b, c, d = it, it - 1, it - 2, it - 3
                steps = {u: (name, stage) for name, u, stage in A_ORDER}

                def products(g, n):
                    last_bank, blocks = PV_STEPS[n]
                    pe.wait_ge(sa["probs_ready"], c * BANKS + g * GROUP_BANKS + last_bank + 1)
                    if n == 0:
                        if g == 0:
                            pe.wait_ge(sa["vpad_ready"], c + 1)
                        wait(pe, sa["o_copied"], c * GROUPS + g)
                    for i in blocks:
                        for j in range(QG):
                            k, at = key_place(j, i)
                            last = mm(O[32 * j:32 * j + 32, P * i:S], vext[par][:, i, QG * g + j, :],
                                      probs[:, k, at:at + S - P * i], start=(i == 0), stop=(i == 2),
                                      skip_group_check=True)
                    last.then_inc(sa["pv_done"], 1)

                for u in range(BANKS):
                    g, j = divmod(u, GROUP_BANKS)
                    if on[2]:
                        wait(pe, sa["probs_ready"], c * BANKS + u - 1)
                        if u in (0, BANKS // 2):
                            pe.wait_ge(sa["mrows_loaded"], (c * 2 + (u > 0) + 1) * MROW_DMAS * 16)
                        scores(SC[:, u % 2, :], kstk[par], qstk[par], QG * g, KEY_BANKS[j], KM, mask_k, False) \
                            .then_inc(sa["score_full"], 1)
                    name, stage = steps.get(u, (None, 0))
                    if name and on[stage]:
                        dst = a_bank[name]
                        if name == "den":
                            pe.wait_ge(sa["o_copied"], (d + 1) * GROUPS)
                        claim(A_ORDER, A_READERS, it, on, name)
                        if name == "den":
                            select_heads(dst, sel_d, sa["den_full"])
                        if name == "out":
                            select_heads(dst, sel_o, sa["out_full"])
                        if name == "mt1":
                            turn_maxima(dst, c, 1)
                        if name == "mt0":
                            turn_maxima(dst, b, 0)
                        if name == "xt":
                            turn_tiles(dst, xn, sa["xn_ready"], sa["xt_full"], a)
                        if name in ("q", "qr", "k", "kr"):
                            if name == "q":
                                pe.wait_ge(sa["xnT_ready"], a + 1)
                            project(dst, sa, wT[:, ("q", "qr", "k", "kr").index(name), :])
                        if name == "v":
                            tile_products(dst, wT[:, 4, :], xnT, P).then_inc(sa["proj_full"], 1)
                        if name == "wo":
                            pe.wait_ge(sa["attn_ready"], d + 1)
                            tile_products(dst, wT[:, 5, :], attnT, D).then_inc(sa["wo_full"], 1)
                        if name == "xt2":
                            turn_tiles(dst, xn2[1 - par], ra["xn_ready"], ra["xt2_full"], d)
                        if name == "lg":
                            pe.wait_ge(ra["xn2T_ready"], d + 1)
                            tile_products(dst, gate_ws[:, :], xn2T, E).then_inc(ra["logit_full"], 1)
                        if name == "pos":
                            positions(dst, ra, d)
                    if on[1]:
                        if u in (0, BANKS // 2):
                            pe.wait_ge(sa["stack_loaded"][u > 0], (b + 1) * STACK_DMAS * 16)
                        at, back = max_bank(u)
                        wait(pe, sa["max_done"], b * BANKS + u - back + 1)
                        scores(MX[:, at, :], qstk[1 - par], kstk[1 - par], 2 * (u // 5), QUERY_BANKS[u % 5], KR,
                               mask_q, True).then_inc(sa["max_full"], 1)
                    if on[2]:
                        if j == 1 and g:
                            products(g - 1, 2)
                        if j == 5:
                            products(g, 0)
                        if j == 9:
                            products(g, 1)
                if on[2]:
                    products(GROUPS - 1, 2)

            over_batches(pe, 4, a_body)

            def expert_phase(e):
                def turn(p, r, par, on):
                    if on[0]:
                        if r % BLOCK == 0:
                            pe.wait_ge(e["block_landed"][r // BLOCK],
                                       (p - r) * (BLOCK_DMAS * 16 // RING) + BLOCK_DMAS * 16)
                        wait(pe, e["xbt_ready"], p - 1)
                        nc.tensor.transpose(bank[:, par, 0:P], xb_s[:, r, 0:D], ident[:, :]).then_inc(e["xbt_full"], 1)
                    if on[1]:
                        q, rq, bq_ = p - 1, (r - 1) % RING, 1 - par
                        pe.wait_ge(e["landed"][rq], (q - rq) * (PAIR_DMAS * 16 // RING) + PAIR_DMAS * 16)
                        pe.wait_ge(e["xbt_ready"], q + 1)
                        wait(pe, e["hrow_ready"], q - 1)
                        for t in range(2):
                            last = mm(bank[CAP * t:CAP * (t + 1), 2 + bq_, :], xbT[:, bq_, CAP * t:CAP * (t + 1)],
                                      w1_s[rq][:, t, :], start=True, stop=True)
                        last.then_inc(e["hrow_full"], 1)
                    if on[2]:
                        q = p - 2
                        pe.wait_ge(e["hrow_ready"], q + 1)
                        wait(pe, e["hpre_ready"], q - 1)
                        for c in range(HC):
                            last = nc.tensor.transpose(
                                bank[:, 6 + par, :].rearrange("p (t c n) -> p t c n", t=2, c=HC)[:, :, c, :],
                                hrow[:, par, c:HID:HC], ident[:, :])
                        last.then_inc(e["h_full"], 1)
                    if on[3]:
                        q, rq, bq_ = p - 3, (r - 3) % RING, 1 - par
                        pe.wait_ge(e["h_ready"], q + 1)
                        wait(pe, e["y_ready"], q - 1)
                        for c in range(HC):
                            for t in range(2):
                                last = mm(bank[CAP * t:CAP * (t + 1), 4 + bq_, 0:D], hact[:, bq_, t, c, :],
                                          w2_s[rq][:, t, c, :], start=(c == 0), stop=(c == HC - 1))
                        last.then_inc(e["y_full"], 1)
                over_pairs(pe, turn)

            expert_phase(eb)

            def c_body(it, par, on):
                a, b, c, d = it, it - 1, it - 2, it - 3
                steps = {u: (name, stage) for name, u, stage in C_ORDER}

                def products(g):
                    pe.wait_ge(sc_["probs_ready"], c * H + QG * g + QG)
                    wait(pe, sc_["o_copied"], c * GROUPS + g)
                    for t in range(TB):
                        for j in range(QG):
                            last = mm(O[32 * j:32 * j + 32, t * P:(t + 1) * P], vext[par][:, t, QG * g + j, :],
                                      masked(QG * g + j)[:, t * P:(t + 1) * P], start=(t == 0), stop=(t == TB - 1),
                                      skip_group_check=True)
                    last.then_inc(sc_["pv_done"], 1)

                def head_scores(h):
                    if h == 0:
                        pe.wait_ge(sc_["stack_loaded"][0], (c + 1) * 2 * STACK_DMAS * 16)
                    wait(pe, sc_["probs_ready"], c * H + h - 3)
                    p0, col = place_of(h)
                    for t in range(TB):
                        last = mm(SC[:, h % 4, t * P:(t + 1) * P],
                                  kstk[par][p0:p0 + KR, col, t * P:(t + 1) * P],
                                  qstk[par][p0:p0 + KR, col, t * P:(t + 1) * P], start=True, stop=True)
                    last.then_inc(sc_["score_full"], 1)

                for u in range(H):
                    if on[2]:
                        for h in range(0 if u == 0 else u + C_LEAD, min(u + C_LEAD + 1, H)):
                            head_scores(h)
                    name, stage = steps.get(u, (None, 0))
                    if name and on[stage]:
                        dst = c_bank[name]
                        if name == "ctx":
                            pe.wait_ge(sc_["o_copied"], (d + 1) * GROUPS)
                        claim(C_ORDER, C_READERS, it, on, name)
                        if name == "ctx":
                            select_heads(dst, sel_o, None)
                            pe.wait_ge(sc_["state_ready"], (d + 1) * (TB - 1))
                            for t in range(1, TB):
                                last = mm(dst[:, t * P:(t + 1) * P], stm[1 - par][:, t - 1, :],
                                          qs[1 - par][:, t * P:(t + 1) * P],
                                          start=False, stop=(t == TB - 1), skip_group_check=True)
                            last.then_inc(sc_["ctx_full"], 1)
                        if name == "xt":
                            turn_tiles(dst, xn, sc_["xn_ready"], sc_["xt_full"], a)
                        if name == "n":
                            pe.wait_ge(sc_["xnT_ready"], b + 1)
                            project(dst, sc_, wn_s[:, :])
                        if name == "q":
                            project(dst, sc_, wq2_s[:, :])
                        if name == "k":
                            project(dst, sc_, wkv_s[:, 0:P])
                        if name in ("kt", "vt"):
                            at = P * ("kt", "vt").index(name)
                            tile_products(dst, wkv_s[:, at:at + P], xnT, P).then_inc(sc_["proj_full"], 1)
                        if name == "wo":
                            pe.wait_ge(sc_["ctx_ready"], d + 1)
                            tile_products(dst, wo2_s[:, :], attnT, D).then_inc(sc_["wo_full"], 1)
                        if name == "xt2":
                            turn_tiles(dst, xn2[1 - par], rc["xn_ready"], rc["xt2_full"], d)
                        if name == "lg":
                            pe.wait_ge(rc["xn2T_ready"], d + 1)
                            tile_products(dst, gate_ws[:, :], xn2T, E).then_inc(rc["logit_full"], 1)
                        if name == "pos":
                            positions(dst, rc, d)
                    if on[1] and C_ST <= u < C_ST + TB - 1:
                        j = u - C_ST
                        pe.wait_ge(sc_["kvn_ready"], b + 1)
                        wait(pe, sc_["state_ready"], b * 3 + j)
                        mm(ST.rearrange("p (h d) -> p h d", d=DH), kn[:, j, :], vext[1 - par][:, j, :, 0:DH],
                           start=(j == 0), stop=True, skip_group_check=True).then_inc(sc_["state_full"], 1)
                    if on[2] and u % QG == 2 and u > QG:
                        products(u // QG - 1)
                if on[2]:
                    products(GROUPS - 1)

            over_batches(pe, 4, c_body)
            expert_phase(ed)


_INS = ["L0_attn_a_x", "L0_attn_a_Wq", "L0_attn_a_Wk", "L0_attn_a_Wv", "L0_attn_a_Wo", "L0_attn_b_Wqk",
        "L0_attn_b_bqk", "L0_attn_b_Wv", "L0_attn_b_bv", "L0_attn_b_Wn", "L0_attn_b_bn", "L0_attn_b_Wo",
        "L0_attn_b_bo", "L0_ffn_gate_w", "L0_ffn_gate_b", "L0_ffn_w1", "L0_ffn_b1", "L0_ffn_w2", "L0_ffn_b2"]


def rotary_tables():
    import numpy as np
    inv = (1.0 / np.float32(10000.0) ** (np.arange(0, DH, 2, dtype=np.float32) / np.float32(DH))).astype(np.float32)
    f = np.outer(np.arange(S, dtype=np.float32), inv).astype(np.float32)
    cos, sin = np.cos(f).T, np.sin(f).T
    return (np.ascontiguousarray(np.tile(np.concatenate([cos, cos]), (H, 1)), dtype=np.float32),
            np.ascontiguousarray(np.tile(np.concatenate([-sin, sin]), (H, 1)), dtype=np.float32))


def kernel(**inputs):
    import numpy as np
    import concourse.bacc as bacc
    from concourse.bass_utils import run_bass_kernel_spmd

    nc = bacc.Bacc("TRN2", target_bir_lowering=False, num_devices=1)
    arrays = {name: np.ascontiguousarray(inputs[name]) for name in _INS}
    arrays["cosT"], arrays["sinT"] = rotary_tables()
    args = [nc.dram_tensor(name, a.shape, mybir.dt.from_np(a.dtype), kind="ExternalInput").ap()
            for name, a in arrays.items()]
    args.append(nc.dram_tensor("out", (B, S, D), F32, kind="ExternalOutput").ap())
    build(nc, *args)
    return run_bass_kernel_spmd(nc, [arrays], core_ids=[0]).results[0]["out"]
```
